# Optimizing a Trainium2 kernel written in Bass

```python
import numpy as np
import jax
import jax.numpy as jnp

def _softmax(x, axis=-1):
    return jax.nn.softmax(x, axis=axis)

def _gelu(x):
    return jax.nn.gelu(x, approximate=True)

def _silu(x):
    return jax.nn.silu(x)

def _sigmoid(x):
    return jax.nn.sigmoid(x)

def _layernorm(x, axis=-1, eps=1e-05):
    m = jnp.mean(x, axis=axis, keepdims=True)
    v = jnp.var(x, axis=axis, keepdims=True)
    return (x - m) / jnp.sqrt(v + eps)

def _scatter_add(tgt, idx, src, axis=0):
    return tgt.at[idx].add(src)

def _segment_sum(src, seg, n):
    return jax.ops.segment_sum(src, seg, n)
kernel_name = 'mk_gnn_ffn_d1_gnn_r8_728a32'

def setup_inputs(seed: int=0):
    np.random.seed(seed)
    _w = jnp.asarray

    def _rec_inputs():
        import jax
        import jax.numpy as jnp
        _gk = jax.random.key(seed)
        x = -8.776e-05 + 1 * jax.random.normal(jax.random.fold_in(_gk, 1), (6250, 256), jnp.float32)
        _s = jax.random.randint(jax.random.fold_in(_gk, 2), (50000,), 0, 6250, jnp.int32)
        _d = jax.random.randint(jax.random.fold_in(_gk, 3), (50000,), 0, 6250, jnp.int32)
        _loop = jnp.arange(6250, dtype=jnp.int32)
        src = jnp.concatenate([_s, _d, _loop])
        dst = jnp.concatenate([_d, _s, _loop])
        _o = jnp.argsort(dst, stable=True)
        src = src[_o]
        dst = dst[_o]
        edge_attr_64 = 1.36993e-05 + 0.999972 * jax.random.normal(jax.random.fold_in(_gk, 11), (106250, 64), jnp.float32)
        edge_weight = jax.random.uniform(jax.random.fold_in(_gk, 13), (106250,), jnp.float32, 0.0, 0.999998)
        return (x, src, dst, edge_attr_64, edge_weight)
    x, src, dst, edge_attr_64, edge_weight = _rec_inputs()

    def _L0_gnn_setup():
        import jax, jax.numpy as jnp
        import numpy as np
        N = 2500
        E = 40000
        D = 256
        H = 8
        DH = D // H
        ED = 64
        FF = 4 * D
        EPS = 1e-05

        def _layernorm(x, g, b):
            m = jnp.mean(x, axis=-1, keepdims=True)
            v = jnp.var(x, axis=-1, keepdims=True)
            return (x - m) * jax.lax.rsqrt(v + EPS) * g + b

        def _edge_attention(xn, edge_index, ef, ew, Wq, bq, Wk, bk, Wv, bv, We, be, Wo, bo):
            n = xn.shape[0]
            scale = DH ** (-0.5)
            q = (xn @ Wq + bq).reshape(n, H, DH)
            k = (xn @ Wk + bk).reshape(n, H, DH)
            v = (xn @ Wv + bv).reshape(n, H, DH)
            src, dst = (edge_index[0], edge_index[1])
            ep = ef @ We + be
            scores = jnp.einsum('ehd,ehd->eh', q[dst], k[src] + ep[:, None, :]) * scale
            scores = scores * ew[:, None]
            m = jax.ops.segment_max(scores, dst, num_segments=n)
            m = jnp.where(jnp.isfinite(m), m, 0.0)
            ex = jnp.exp(scores - m[dst])
            s = jax.ops.segment_sum(ex, dst, num_segments=n)
            attn = ex / s[dst]
            out = jax.ops.segment_sum(attn[:, :, None] * v[src], dst, num_segments=n)
            out = out.reshape(n, D) @ Wo + bo
            return out
        key = jax.random.key(seed)
        ks = jax.random.split(key, 32)

        def lin_w(k, i, o):
            return (jax.random.normal(k, (i, o), jnp.float32) / np.sqrt(i)).astype(jnp.float32)
        return {'x': jax.random.normal(ks[0], (N, D), jnp.float32), 'edge_features': jax.random.normal(ks[1], (E, ED), jnp.float32), 'edge_weights': jax.random.uniform(ks[2], (E,), jnp.float32), 'edge_index': jax.random.randint(ks[3], (2, E), 0, N, dtype=jnp.int32), 'Wq': lin_w(ks[4], D, D), 'bq': jnp.zeros((D,), jnp.float32), 'Wk': lin_w(ks[5], D, D), 'bk': jnp.zeros((D,), jnp.float32), 'Wv': lin_w(ks[6], D, D), 'bv': jnp.zeros((D,), jnp.float32), 'We': lin_w(ks[7], ED, DH), 'be': jnp.zeros((DH,), jnp.float32), 'Wo': lin_w(ks[8], D, D), 'bo': jnp.zeros((D,), jnp.float32), 'ln1_g': jnp.ones((D,), jnp.float32), 'ln1_b': jnp.zeros((D,), jnp.float32), 'ln2_g': jnp.ones((D,), jnp.float32), 'ln2_b': jnp.zeros((D,), jnp.float32), 'W1': lin_w(ks[9], D, FF), 'b1': jnp.zeros((FF,), jnp.float32), 'W2': lin_w(ks[10], FF, D), 'b2': jnp.zeros((D,), jnp.float32), 'alpha': jnp.ones((1,), jnp.float32), 'beta': jnp.ones((1,), jnp.float32)}
    _L0_gnn_all = _L0_gnn_setup()
    _L0_gnn_in = {k: v for k, v in _L0_gnn_all.items() if k in ('Wq', 'bq', 'Wk', 'bk', 'Wv', 'bv', 'We', 'be', 'Wo', 'bo', 'ln1_g', 'ln1_b', 'ln2_g', 'ln2_b', 'W1', 'b1', 'W2', 'b2', 'alpha', 'beta')}
    del _L0_gnn_all

    def _L0_ffn_setup():
        import jax, jax.numpy as jnp
        import numpy as np
        IN_CH = 256
        OUT_CH = 256
        key = jax.random.key(seed)
        kx, kw, kb = jax.random.split(key, 3)
        x = jax.random.normal(kx, (8, 512, IN_CH), dtype=jnp.float32)
        bound = 1.0 / np.sqrt(IN_CH)
        weight = jax.random.uniform(kw, (OUT_CH, IN_CH), dtype=jnp.float32, minval=-bound, maxval=bound)
        bias = jax.random.uniform(kb, (OUT_CH,), dtype=jnp.float32, minval=-bound, maxval=bound)
        return {'x': x, 'weight': weight, 'bias': bias}
    _L0_ffn_all = _L0_ffn_setup()
    _L0_ffn_in = {k: v for k, v in _L0_ffn_all.items() if k in ('weight', 'bias')}
    del _L0_ffn_all
    return {'x': x, 'src': src, 'dst': dst, 'edge_attr_64': edge_attr_64, 'edge_weight': edge_weight, 'L0_gnn_Wq': _L0_gnn_in['Wq'], 'L0_gnn_bq': _L0_gnn_in['bq'], 'L0_gnn_Wk': _L0_gnn_in['Wk'], 'L0_gnn_bk': _L0_gnn_in['bk'], 'L0_gnn_Wv': _L0_gnn_in['Wv'], 'L0_gnn_bv': _L0_gnn_in['bv'], 'L0_gnn_We': _L0_gnn_in['We'], 'L0_gnn_be': _L0_gnn_in['be'], 'L0_gnn_Wo': _L0_gnn_in['Wo'], 'L0_gnn_bo': _L0_gnn_in['bo'], 'L0_gnn_ln1_g': _L0_gnn_in['ln1_g'], 'L0_gnn_ln1_b': _L0_gnn_in['ln1_b'], 'L0_gnn_ln2_g': _L0_gnn_in['ln2_g'], 'L0_gnn_ln2_b': _L0_gnn_in['ln2_b'], 'L0_gnn_W1': _L0_gnn_in['W1'], 'L0_gnn_b1': _L0_gnn_in['b1'], 'L0_gnn_W2': _L0_gnn_in['W2'], 'L0_gnn_b2': _L0_gnn_in['b2'], 'L0_gnn_alpha': _L0_gnn_in['alpha'], 'L0_gnn_beta': _L0_gnn_in['beta'], 'L0_ffn_weight': _L0_ffn_in['weight'], 'L0_ffn_bias': _L0_ffn_in['bias']}

def reference(x, src, dst, edge_attr_64, edge_weight, L0_gnn_Wq, L0_gnn_bq, L0_gnn_Wk, L0_gnn_bk, L0_gnn_Wv, L0_gnn_bv, L0_gnn_We, L0_gnn_be, L0_gnn_Wo, L0_gnn_bo, L0_gnn_ln1_g, L0_gnn_ln1_b, L0_gnn_ln2_g, L0_gnn_ln2_b, L0_gnn_W1, L0_gnn_b1, L0_gnn_W2, L0_gnn_b2, L0_gnn_alpha, L0_gnn_beta, L0_ffn_weight, L0_ffn_bias):
    import jax
    import jax.numpy as jnp

    def _L0_gnn_ref(x, edge_features, edge_weights, edge_index, Wq, bq, Wk, bk, Wv, bv, We, be, Wo, bo, ln1_g, ln1_b, ln2_g, ln2_b, W1, b1, W2, b2, alpha, beta):
        import jax, jax.numpy as jnp
        import numpy as np
        N = 2500
        E = 40000
        D = 256
        H = 8
        DH = D // H
        ED = 64
        FF = 4 * D
        EPS = 1e-05

        def _layernorm(x, g, b):
            m = jnp.mean(x, axis=-1, keepdims=True)
            v = jnp.var(x, axis=-1, keepdims=True)
            return (x - m) * jax.lax.rsqrt(v + EPS) * g + b

        def _edge_attention(xn, edge_index, ef, ew, Wq, bq, Wk, bk, Wv, bv, We, be, Wo, bo):
            n = xn.shape[0]
            scale = DH ** (-0.5)
            q = (xn @ Wq + bq).reshape(n, H, DH)
            k = (xn @ Wk + bk).reshape(n, H, DH)
            v = (xn @ Wv + bv).reshape(n, H, DH)
            src, dst = (edge_index[0], edge_index[1])
            ep = ef @ We + be
            scores = jnp.einsum('ehd,ehd->eh', q[dst], k[src] + ep[:, None, :]) * scale
            scores = scores * ew[:, None]
            m = jax.ops.segment_max(scores, dst, num_segments=n)
            m = jnp.where(jnp.isfinite(m), m, 0.0)
            ex = jnp.exp(scores - m[dst])
            s = jax.ops.segment_sum(ex, dst, num_segments=n)
            attn = ex / s[dst]
            out = jax.ops.segment_sum(attn[:, :, None] * v[src], dst, num_segments=n)
            out = out.reshape(n, D) @ Wo + bo
            return out
        xn = _layernorm(x, ln1_g, ln1_b)
        attn_out = _edge_attention(xn, edge_index, edge_features, edge_weights, Wq, bq, Wk, bk, Wv, bv, We, be, Wo, bo)
        x = x + alpha * attn_out
        xn = _layernorm(x, ln2_g, ln2_b)
        ff = jax.nn.gelu(xn @ W1 + b1, approximate=False) @ W2 + b2
        x = x + beta * ff
        return x

    def _L0_ffn_ref(x, weight, bias):
        import jax, jax.numpy as jnp
        import numpy as np
        IN_CH = 256
        OUT_CH = 256
        return jnp.einsum('bsi,oi->bso', x, weight) + bias
    edge_index = jnp.stack([src, dst])
    x = x + _L0_gnn_ref(_layernorm(x, axis=-1), edge_attr_64, edge_weight, edge_index, L0_gnn_Wq, L0_gnn_bq, L0_gnn_Wk, L0_gnn_bk, L0_gnn_Wv, L0_gnn_bv, L0_gnn_We, L0_gnn_be, L0_gnn_Wo, L0_gnn_bo, L0_gnn_ln1_g, L0_gnn_ln1_b, L0_gnn_ln2_g, L0_gnn_ln2_b, L0_gnn_W1, L0_gnn_b1, L0_gnn_W2, L0_gnn_b2, L0_gnn_alpha, L0_gnn_beta)
    x = x + _L0_ffn_ref(_layernorm(x, axis=-1)[None], L0_ffn_weight, L0_ffn_bias)[0]
    return x

_drawn_inputs = setup_inputs


def setup_inputs(seed=0):
    import zlib

    import numpy as np

    out = dict(_drawn_inputs(seed))
    spreads = {'L0_gnn_bq': (0.0, 0.478),
     'L0_gnn_bk': (0.0, 0.8),
     'L0_gnn_bv': (0.0, 0.1),
     'L0_gnn_be': (0.0, 0.8),
     'L0_gnn_bo': (0.0, 0.1),
     'L0_gnn_ln1_g': (1.0, 0.2),
     'L0_gnn_ln1_b': (0.0, 0.1),
     'L0_gnn_ln2_g': (1.0, 0.2),
     'L0_gnn_ln2_b': (0.0, 0.1),
     'L0_gnn_b1': (0.0, 0.1),
     'L0_gnn_b2': (0.0, 0.1)}
    factors = {'L0_ffn_bias': 3.346}
    for name, (base, spread) in spreads.items():
        noise = np.random.default_rng([zlib.crc32(name.encode()), seed]).standard_normal(out[name].shape)
        drawn = base * np.exp(spread * noise) if base else spread * noise
        out[name] = jnp.asarray(drawn.astype(out[name].dtype))
    for name, factor in factors.items():
        out[name] = (out[name] * factor).astype(out[name].dtype)
    return out
```

```python
from contextlib import ExitStack

import concourse.bass as bass
from concourse import mybir

ALU = mybir.AluOpType
ACT = mybir.ActivationFunctionType
AX = mybir.AxisListType
F32 = mybir.dt.float32
BF16 = mybir.dt.bfloat16
I32 = mybir.dt.int32
U32 = mybir.dt.uint32

P = 128
N, E, D, H, ED, FF = 6250, 106250, 256, 8, 64, 1024
DH = D // H
NW = -(-N // P)
NPAD = NW * P
GW = 7
NG = NW // GW
T = 18
PAIRS = T // 2
CHUNK = T * P
EPAD = E + CHUNK
COLS = -(-E // P)
FAR = 1 << 20
KC = D // P
FC = FF // P
HW = DH + 1
AW = H * HW
RW = AW + H + 1
SEG = T + 1
SCAN = H * SEG
NS = 128
BIG = 1.0e30
EPS = 1e-5
SCALE = DH ** -0.5
assert NG * GW == NW and NW % 2 == 1 and NS > NW + E // CHUNK + 2


class Count:

    def __init__(self, sem, per, primer=1):
        self.sem, self.per, self.primer = sem, per, primer

    def at(self, rnd, n):
        return rnd * self.per + (self.primer + n)


def declare(ctx, nc):
    def sb(name, shape, dt=F32):
        return ctx.enter_context(nc.sbuf_tensor(name, shape, dt))

    def ps(name, shape, dt=F32):
        return ctx.enter_context(nc.psum_tensor(name, shape, dt))

    def sem(name):
        return ctx.enter_context(nc.semaphore(name))

    return sb, ps, sem


def held(eng, count, value, passed):
    eng.wait_ge(count.sem, value)
    eng.sem_inc(passed, 1)


def node_stage(nc, t, keep):
    with ExitStack() as ctx:
        sb, ps, sem = declare(ctx, nc)
        x = sb("x", [P, GW, D])
        x1 = sb("x1", [P, GW, D])
        xh = sb("xh", [P, GW, D])
        xT = sb("xT", [P, GW, KC, P])
        kv = sb("kv", [P, GW, 2 * D])
        qf = sb("qf", [P, GW, D])
        qrest = sb("qrest", [P, GW, D])
        qpart = sb("qpart", [P, GW, 3, D], BF16)
        wraw = sb("wraw", [P, KC, 3 * D])
        w = sb("w", [P, KC, 3 * D])
        lng = sb("lng", [P, KC])
        lnb = sb("lnb", [P, KC])
        lnb_wide = sb("lnb_wide", [P, KC, P])
        brow = sb("brow", [P, 3 * D])
        bias = sb("bias", [P, 3 * D])
        be = sb("be", [P, DH])
        ones = sb("ones", [P, P])
        bn = sb("bn", [P, 2, GW, 6])
        mv = sb("mv", [P, 2, GW, 2])
        veps = sb("veps", [P, 2, GW])
        rstd = sb("rstd", [P, 2, GW])
        half = sb("half", [P, GW])
        dall = sb("dall", [P, COLS], I32)
        dallf = sb("dallf", [P, COLS])
        signs = sb("signs", [P, COLS])
        thr_i = sb("thr_i", [P, NW + 1], I32)
        thr = sb("thr", [P, NW + 1])
        tr = [ps(f"n_tr{i}", [P, D]) for i in range(2)]
        pkv = [ps(f"n_pkv{i}", [P, 2 * D]) for i in range(2)]
        pq = [ps(f"n_pq{i}", [P, D]) for i in range(2)]
        pb = [ps(f"n_pb{i}", [P, 512]) for i in range(2)]

        w_in, dst_in, iota_done, thr_done = sem("w_in"), sem("dst_in"), sem("iota_done"), sem("thr_done")
        ones_done, wide_done, bias_ps, wprep = sem("ones_done"), sem("wide_done"), sem("bias_ps"), sem("wprep")
        half_done, dallf_done, sign_done = sem("half_done"), sem("dallf_done"), sem("sign_done")
        ident_done = sem("ident_done")
        passed = sem("n_passed")
        x_in, x1_out, kv_out, q_out = sem("x_in"), sem("x1_out"), sem("kv_out"), sem("q_out")
        stored = Count(sem("stored"), 1)
        bnd = [Count(sem(f"bn_done{i}"), GW) for i in range(2)]
        mvd = [Count(sem(f"mv_done{i}"), GW) for i in range(2)]
        ved = [Count(sem(f"veps_done{i}"), 1) for i in range(2)]
        rsd = [Count(sem(f"rstd_done{i}"), 1) for i in range(2)]
        x1_done = Count(sem("x1_done"), GW)
        xh_done = Count(sem("xh_done"), GW)
        tr_ps = Count(sem("tr_ps"), GW)
        xT_done = Count(sem("xT_done"), GW)
        kv_ps = Count(sem("kv_ps"), GW)
        q_ps = Count(sem("q_ps"), GW)
        kv_done = Count(sem("kv_done"), GW)
        qf_done = Count(sem("qf_done"), GW)
        hi_done = Count(sem("hi_done"), GW)
        rest_done = Count(sem("rest_done"), GW)
        mid_done = Count(sem("mid_done"), GW)
        lo_done = Count(sem("lo_done"), GW)

        xv = t["x"].rearrange("(g i p) d -> p g i d", i=GW, p=P)
        x1v = t["x1"].rearrange("(g i p) d -> p g i d", i=GW, p=P)
        kvv = t["kv"].rearrange("(g i p) d -> p g i d", i=GW, p=P)
        qv = t["q"].rearrange("(g i p) d -> p g i d", i=GW, p=P)
        block = ctx.enter_context(nc.Block())

        @block.sync
        def _(sp):
            sp.sem_inc(stored.sem, 1)
            sp.dma_start(x[:].unsqueeze(1), xv[:, 0:1]).then_inc(x_in, 16)
            for n, name in enumerate(("Wk", "Wv", "Wq")):
                sp.dma_start(wraw[:, :, n * D:(n + 1) * D],
                             t[name].rearrange("(c p) n -> p c n", p=P)).then_inc(w_in, 16)
            for n, name in enumerate(("bk", "bv", "bq")):
                sp.dma_start(brow[:, n * D:(n + 1) * D],
                             t[name].rearrange("(a n) -> a n", a=1).broadcast_to([P, D])).then_inc(w_in, 16)
            sp.dma_start(be[:], t["be"].rearrange("(a n) -> a n", a=1).broadcast_to([P, DH])).then_inc(w_in, 16)
            with nc.allow_non_contiguous_dma(reason="256 numbers, once"):
                sp.dma_start(lng[:], t["ln1_g"].rearrange("(c p) -> p c", p=P)).then_inc(w_in, 16)
                sp.dma_start(lnb[:], t["ln1_b"].rearrange("(c p) -> p c", p=P)).then_inc(w_in, 16)
            sp.dma_start(dall[:], t["dst"][1:1 + P * COLS].rearrange("(p c) -> p c", p=P)).then_inc(dst_in, 16)

            def group(g, more):
                held(sp, x1_done, x1_done.at(g, GW), passed)
                sp.dma_start(x1v[:, bass.ds(g, 1)], x1[:].unsqueeze(1)).then_inc(x1_out, 16)
                if more:
                    sp.dma_start(x[:].unsqueeze(1), xv[:, bass.ds(g + 1, 1)]).then_inc(x_in, 16)
                held(sp, kv_done, kv_done.at(g, GW), passed)
                sp.dma_start(kvv[:, bass.ds(g, 1)], kv[:].unsqueeze(1)).then_inc(kv_out, 16)
                held(sp, lo_done, lo_done.at(g, GW), passed)
                sp.dma_start(qv[:, bass.ds(g, 1)], qpart[:].rearrange("p i c d -> p i (c d)").unsqueeze(1)
                             ).then_inc(q_out, 16)
                for s in (x1_out, kv_out, q_out):
                    sp.wait_ge(s, g * 16 + 16)
                sp.sem_inc(stored.sem, 1)

            with sp.Fori(0, NG - 1) as g:
                group(g, True)
            group(NG - 1, False)

        @block.gpsimd
        def _(pool):
            nc.gpsimd.memset(half[:], -0.5).then_inc(half_done, 1)
            nc.gpsimd.iota(thr_i[:], [[P, NW + 1]], base=0, channel_multiplier=0).then_inc(iota_done, 1)
            nc.gpsimd.memset(keep["ident"][:], 0.0).then_inc(ident_done, 1)
            pool.wait_ge(ident_done, 1)
            nc.gpsimd.affine_select(out=keep["ident"][:], in_=keep["ident"][:], compare_op=ALU.not_equal, fill=1.0,
                                    base=0, pattern=[[-1, P]], channel_multiplier=1).then_inc(ident_done, 1)
            for s in ved + rsd:
                pool.sem_inc(s.sem, 1)
            pool.wait_ge(half_done, 1)
            with pool.Fori(0, NG) as g:
                for n in range(2):
                    held(pool, mvd[n], mvd[n].at(g, GW), passed)
                    nc.gpsimd.tensor_scalar(veps[:, n, :], mv[:, n, :, 1], EPS, None, ALU.add
                                            ).then_inc(ved[n].sem, 1)
                    pool.wait_ge(ved[n].sem, ved[n].at(g, 1))
                    nc.gpsimd.tensor_tensor(rstd[:, n, :], veps[:, n, :], half[:], ALU.pow).then_inc(rsd[n].sem, 1)

        @block.scalar
        def _(act):
            for s in (xT_done, hi_done, mid_done):
                act.sem_inc(s.sem, 1)
            act.wait_ge(iota_done, 1)
            nc.scalar.activation(thr[:], thr_i[:], ACT.Copy, bias=-0.5).then_inc(thr_done, 1)
            act.wait_ge(thr_done, 1)
            act.wait_ge(dallf_done, 1)
            with act.Fori(0, NG) as g:
                for i in range(GW):
                    act.wait_ge(tr_ps.sem, tr_ps.at(g, i + 1))
                    act.wait_ge(q_ps.sem, q_ps.at(g, 0))
                    nc.scalar.activation(xT[:, i], tr[i % 2][:].rearrange("p (c n) -> p c n", c=KC), ACT.Copy
                                         ).then_inc(xT_done.sem, 1)
                for i in range(GW):
                    act.wait_ge(sign_done, g * GW + i) if i else None
                    nc.scalar.activation(signs[:], dallf[:], ACT.Sign, bias=thr[:, bass.ds(g * GW + i, 1)],
                                         scale=-1.0, accum_out=keep["below"][:, bass.ds(g * GW + i, 1)]
                                         ).then_inc(sign_done, 1)
                for i in range(GW):
                    act.wait_ge(qf_done.sem, qf_done.at(g, i + 1))
                    act.wait_ge(stored.sem, stored.at(g, 0))
                    nc.scalar.activation(qpart[:, i, 0], qf[:, i], ACT.Copy).then_inc(hi_done.sem, 1)
                for i in range(GW):
                    act.wait_ge(rest_done.sem, rest_done.at(g, i + 1))
                    nc.scalar.activation(qpart[:, i, 1], qrest[:, i], ACT.Copy).then_inc(mid_done.sem, 1)
                act.wait_ge(sign_done, g * GW + GW)
            nc.scalar.activation(signs[:], dallf[:], ACT.Sign, bias=thr[:, NW:NW + 1], scale=-1.0,
                                 accum_out=keep["below"][:, NW:NW + 1]).then_inc(sign_done, 1)

        @block.tensor
        def _(pe):
            for s in (tr_ps, kv_ps, q_ps):
                pe.sem_inc(s.sem, 1)
            pe.wait_ge(wide_done, KC)
            pe.wait_ge(w_in, 9 * 16)
            for c in range(KC):
                pe.matmul(pb[0][:, 0:512], lnb_wide[:, c], wraw[:, c, 0:512], start=c == 0, stop=c == KC - 1)
            for c in range(KC):
                last = pe.matmul(pb[1][:, 0:D], lnb_wide[:, c], wraw[:, c, 512:512 + D],
                                 start=c == 0, stop=c == KC - 1)
            last.then_inc(bias_ps, 1)
            pe.wait_ge(ident_done, 2)
            pe.wait_ge(wprep, KC + 4)
            with pe.Fori(0, NG) as g:
                for i in range(GW):
                    pe.wait_ge(xh_done.sem, xh_done.at(g, i + 1))
                    pe.wait_ge(xT_done.sem, xT_done.at(g, max(i - 1, 0)))
                    for c in range(KC):
                        last = pe.transpose(tr[i % 2][:, c * P:(c + 1) * P], xh[:, i, c * P:(c + 1) * P],
                                            keep["ident"][:])
                    last.then_inc(tr_ps.sem, 1)
                for i in range(GW):
                    pe.wait_ge(xT_done.sem, xT_done.at(g, i + 1))
                    pe.wait_ge(kv_done.sem, kv_done.at(g, max(i - 1, 0)))
                    for c in range(KC):
                        last = pe.matmul(pkv[i % 2][:], xT[:, i, c], w[:, c, 0:2 * D], start=c == 0,
                                         stop=c == KC - 1)
                    last.then_inc(kv_ps.sem, 1)
                    pe.wait_ge(qf_done.sem, qf_done.at(g, max(i - 1, 0)))
                    for c in range(KC):
                        last = pe.matmul(pq[i % 2][:], xT[:, i, c], w[:, c, 2 * D:3 * D], start=c == 0,
                                         stop=c == KC - 1)
                    last.then_inc(q_ps.sem, 1)

        @block.vector
        def _(dve):
            for s in (*bnd, *mvd, x1_done, xh_done, kv_done, qf_done, rest_done, lo_done):
                dve.sem_inc(s.sem, 1)
            nc.vector.memset(ones[:], 1.0).then_inc(ones_done, 1)
            dve.wait_ge(ones_done, 1)
            dve.wait_ge(w_in, 9 * 16)
            for c in range(KC):
                nc.vector.tensor_scalar(lnb_wide[:, c], ones[:], lnb[:, c:c + 1], None, ALU.mult
                                        ).then_inc(wide_done, 1)
            nc.vector.tensor_tensor(brow[:, 0:D].rearrange("p (h d) -> p h d", h=H),
                                    brow[:, 0:D].rearrange("p (h d) -> p h d", h=H),
                                    be[:].unsqueeze(1).broadcast_to([P, H, DH]), ALU.add).then_inc(wprep, 1)
            for c in range(KC):
                nc.vector.tensor_scalar(w[:, c], wraw[:, c], lng[:, c:c + 1], None, ALU.mult).then_inc(wprep, 1)
            dve.wait_ge(wprep, 1 + KC)
            dve.wait_ge(bias_ps, 1)
            nc.vector.tensor_tensor(bias[:, 0:512], brow[:, 0:512], pb[0][:], ALU.add).then_inc(wprep, 1)
            nc.vector.tensor_tensor(bias[:, 512:768], brow[:, 512:768], pb[1][:, 0:D], ALU.add).then_inc(wprep, 1)
            dve.wait_ge(dst_in, 16)
            nc.vector.tensor_copy(dallf[:], dall[:]).then_inc(dallf_done, 1)
            dve.wait_ge(wprep, 3 + KC)
            dve.sem_inc(wprep, 1)
            with dve.Fori(0, NG) as g:
                for n, (a, b, done) in enumerate(((x, x1, x1_done), (x1, xh, xh_done))):
                    for i in range(GW):
                        if n == 0:
                            dve.wait_ge(x_in, g * 16 + 16)
                        else:
                            dve.wait_ge(x1_done.sem, x1_done.at(g, i + 1))
                        nc.vector.bn_stats(bn[:, n, i], a[:, i]).then_inc(bnd[n].sem, 1)
                    for i in range(GW):
                        held(dve, bnd[n], bnd[n].at(g, i + 1), passed)
                        nc.vector.bn_aggr(mv[:, n, i], bn[:, n, i]).then_inc(mvd[n].sem, 1)
                    for i in range(GW):
                        dve.wait_ge(rsd[n].sem, rsd[n].at(g, 1))
                        if n == 0:
                            dve.wait_ge(stored.sem, stored.at(g, 0))
                        else:
                            dve.wait_ge(tr_ps.sem, tr_ps.at(g, 0))
                        nc.vector.tensor_scalar(b[:, i], a[:, i], mv[:, n, i, 0:1], rstd[:, n, i:i + 1],
                                                ALU.subtract, ALU.mult).then_inc(done.sem, 1)
                for i in range(GW):
                    dve.wait_ge(kv_ps.sem, kv_ps.at(g, i + 1))
                    nc.vector.tensor_tensor(kv[:, i], pkv[i % 2][:], bias[:, 0:2 * D], ALU.add
                                            ).then_inc(kv_done.sem, 1)
                    dve.wait_ge(q_ps.sem, q_ps.at(g, i + 1))
                    dve.wait_ge(hi_done.sem, hi_done.at(g, 0))
                    dve.wait_ge(rest_done.sem, rest_done.at(g, 0))
                    nc.vector.tensor_tensor(qf[:, i], pq[i % 2][:], bias[:, 2 * D:], ALU.add
                                            ).then_inc(qf_done.sem, 1)
                for i in range(GW):
                    dve.wait_ge(hi_done.sem, hi_done.at(g, i + 1))
                    dve.wait_ge(lo_done.sem, lo_done.at(g, 0))
                    nc.vector.tensor_tensor(qrest[:, i], qf[:, i], qpart[:, i, 0], ALU.subtract
                                            ).then_inc(rest_done.sem, 1)
                for i in range(GW):
                    dve.wait_ge(mid_done.sem, mid_done.at(g, i + 1))
                    nc.vector.tensor_tensor(qpart[:, i, 2], qrest[:, i], qpart[:, i, 1], ALU.subtract
                                            ).then_inc(lo_done.sem, 1)


def step_stage(nc, keep):
    with ExitStack() as ctx:
        sb, ps, sem = declare(ctx, nc)
        ones = sb("s_ones", [P, P])
        iota_i = sb("iota_i", [P, P], I32)
        kthr_i = sb("kthr_i", [NW, E // CHUNK + 1], I32)
        kthr = sb("kthr", [NW, E // CHUNK + 1])
        more = sb("more", [NW, E // CHUNK + 1])
        before = sb("before", [NW, NW])
        below = sb("belowc", [P, NW + 1])
        col = sb("col", [NW, 6])
        past = sb("past", [NW, NS])
        rows = sb("rows", [1, 2, NS])
        base_i = sb("base_i", [1, NS], I32)
        base = sb("base", [1, NS])
        pcol = ps("pcol", [NW, 4])
        prow = ps("prow", [1, 2 * NS + 1])
        pwide = ps("pwide", [P, NS])
        made, fixed, sums, done = sem("made"), sem("fixed"), sem("sums"), sem("rows_done")
        block = ctx.enter_context(nc.Block())
        RP, NEXT, CHUNKS, END, SPARE, FIRST = range(6)

        @block.gpsimd
        def _(pool):
            nc.gpsimd.iota(iota_i[:], [[1, P]], base=0, channel_multiplier=0).then_inc(made, 1)
            nc.gpsimd.iota(kthr_i[:], [[CHUNK, E // CHUNK + 1]], base=CHUNK, channel_multiplier=0).then_inc(made, 1)
            nc.gpsimd.iota(base_i[:], [[CHUNK, NS]], base=0, channel_multiplier=0).then_inc(made, 1)
            nc.gpsimd.memset(before[:], 1.0).then_inc(made, 1)
            nc.gpsimd.memset(keep["lastmask"][:], 1.0).then_inc(made, 1)
            pool.wait_ge(made, 5)
            nc.gpsimd.affine_select(out=before[:], in_=before[:], compare_op=ALU.is_gt, fill=0.0, base=0,
                                    pattern=[[1, NW]], channel_multiplier=-1).then_inc(made, 1)
            nc.gpsimd.affine_select(out=keep["lastmask"][:], in_=keep["lastmask"][:], compare_op=ALU.not_equal,
                                    fill=0.0, base=-(P - 1 + T - 1), pattern=[[1, T]], channel_multiplier=1
                                    ).then_inc(made, 1)

        @block.vector
        def _(dve):
            def link(ins):
                link.n += 1
                ins.then_inc(fixed, 1)
                dve.wait_ge(fixed, link.n)
            link.n = 0
            dve.wait_ge(made, 7)
            link(nc.vector.memset(ones[:], 1.0))
            link(nc.vector.tensor_scalar(below[:], keep["below"][:], float(COLS), 0.5, ALU.add, ALU.mult))
            link(nc.vector.tensor_copy(kthr[:], kthr_i[:]))
            link(nc.vector.tensor_copy(keep["iota"][:], iota_i[:]))
            link(nc.vector.tensor_copy(base[:], base_i[:]))
            dve.wait_ge(sums, 1)
            link(nc.vector.tensor_copy(col[:, RP:RP + 2], pcol[:, 0:2]))
            link(nc.vector.tensor_tensor(col[:, SPARE:SPARE + 1], col[:, NEXT:NEXT + 1], col[:, RP:RP + 1],
                                         ALU.subtract))
            link(nc.vector.tensor_scalar(more[:], kthr[:], col[:, SPARE:SPARE + 1], 1.0, ALU.is_lt, ALU.add,
                                         accum_out=col[:, CHUNKS:CHUNKS + 1]))
            dve.sem_inc(done, 1)
            dve.wait_ge(sums, 2)
            link(nc.vector.tensor_tensor(col[:, END:END + 1], pcol[:, 2:3], col[:, CHUNKS:CHUNKS + 1], ALU.add))
            link(nc.vector.scalar_tensor_tensor(out=col[:, FIRST:FIRST + 1], in0=col[:, CHUNKS:CHUNKS + 1],
                                                scalar=-float(CHUNK), in1=col[:, SPARE:SPARE + 1],
                                                op0=ALU.mult, op1=ALU.add))
            link(nc.vector.tensor_scalar(past[:], keep["iota"][0:NW, 0:NS], col[:, END:END + 1], None, ALU.is_ge))
            dve.sem_inc(done, 1)
            dve.wait_ge(sums, 3)
            link(nc.vector.tensor_tensor(rows[:, 0], prow[:, 0:NS], base[:], ALU.add))
            link(nc.vector.tensor_scalar(keep["table"][:, 0:NS], rows[:, 0], float(E), 0.0, ALU.min, ALU.max))
            link(nc.vector.tensor_scalar(keep["table"][:, NS:2 * NS], prow[:, NS:2 * NS], float(NW - 1), None,
                                         ALU.min))
            link(nc.vector.tensor_copy(keep["table"][:, 2 * NS:2 * NS + 1], prow[:, 2 * NS:2 * NS + 1]))
            link(nc.vector.tensor_scalar(keep["wbase"][:], pwide[:], float(NW - 1), float(P), ALU.min, ALU.mult))

        @block.tensor
        def _(pe):
            pe.wait_ge(fixed, 2)
            pe.matmul(pcol[:, 0:1], below[:, 0:NW], ones[:, 0:1], start=True, stop=True)
            pe.matmul(pcol[:, 1:2], below[:, 1:NW + 1], ones[:, 0:1], start=True, stop=True).then_inc(sums, 1)
            pe.wait_ge(done, 1)
            pe.wait_ge(fixed, 8)
            pe.matmul(pcol[:, 2:3], before[:], col[:, CHUNKS:CHUNKS + 1], start=True, stop=True).then_inc(sums, 1)
            pe.wait_ge(done, 2)
            pe.wait_ge(fixed, 11)
            pe.matmul(prow[:, 0:NS], col[:, FIRST:FIRST + 1], past[:], start=True, stop=True)
            pe.matmul(prow[:, NS:2 * NS], ones[0:NW, 0:1], past[:], start=True, stop=True)
            pe.matmul(prow[:, 2 * NS:2 * NS + 1], col[:, CHUNKS:CHUNKS + 1], ones[0:NW, 0:1], start=True, stop=True)
            pe.matmul(pwide[:], ones[0:NW, :], past[:], start=True, stop=True).then_inc(sums, 1)


def edge_stage(nc, t, keep):
    with ExitStack() as ctx:
        sb, ps, sem = declare(ctx, nc)
        acc, top, ident, iota = keep["acc"], keep["top"], keep["ident"], keep["iota"]
        src = [sb(f"src{i}", [P, T], I32) for i in range(2)]
        cur = [sb(f"cur{i}", [P, T], I32) for i in range(2)]
        nxt = [sb(f"nxt{i}", [P, T], I32) for i in range(2)]
        ew = [sb(f"ew{i}", [P, T]) for i in range(2)]
        ef = [sb(f"ef{i}", [P, T * ED]) for i in range(2)]
        qw = [sb(f"qw{i}", [P, 3, D], BF16) for i in range(2)]
        kv = [sb(f"kvg{i}", [P, T, 2 * D]) for i in range(2)]
        we2 = sb("we2", [P, 2 * DH])
        same = sb("same", [P, T])
        inside = sb("inside", [P, T])
        single = sb("single", [P, 1])
        pen = sb("pen", [P, T])
        pen1 = sb("pen1", [P, 1])
        local = sb("local", [P, T])
        last = sb("last", [P, T])
        ews = sb("ews", [P, T])
        hot = sb("hot", [P, T, P])
        hotT = [sb(f"hotT{i}", [P, 2 * P], BF16) for i in range(2)]
        efT = [sb(f"efT{i}", [P, P]) for i in range(2)]
        ke = [sb(f"ke{i}", [P, 2, H, DH]) for i in range(2)]
        pr = [sb(f"pr{i}", [P, 2, H, DH]) for i in range(2)]
        score = sb("score", [P, H, SEG])
        penH = sb("penH", [P, SCAN + 1])
        penZ = sb("penZ", [P, 2, H])
        penS = sb("penS", [H, 2 * P + 1])
        fwd = sb("fwd", [P, SCAN])
        segmax = sb("segmax", [P, SCAN])
        fwd2 = sb("fwd2", [P, SCAN])
        mx = sb("mx", [P, SCAN])
        across = sb("across", [H, 2 * P])
        across2 = sb("across2", [H, 2 * P])
        diff = sb("diff", [P, H, T])
        wv = sb("wv", [P, T, RW])
        absent = sb("absent", [P, 1])
        part = sb("part", [P, 3, H])
        shift = sb("shift", [P, 2, H])
        factor = sb("factor", [P, 2, H])
        scaled = sb("scaled", [P, AW])

        tr = [ps(f"e_tr{i}", [P, 3 * P]) for i in range(2)]
        qb = [ps(f"e_qb{i}", [P, 2 * D]) for i in range(2)]
        ep = [ps(f"e_ep{i}", [P, 2 * DH]) for i in range(2)]
        agg = ps("e_agg", [P, RW])
        turns = ps("e_turns", [P, 4 * P])
        seq = turns[0:H, :].rearrange("h (a n) -> h a n", a=2)
        back = turns[:, 2 * P:2 * P + 2 * H]

        src_in = [sem(f"src_in{i}") for i in range(2)]
        edge_in = [sem(f"edge_in{i}") for i in range(2)]
        q_in = [sem(f"q_in{i}") for i in range(2)]
        kv_in = [[sem(f"kv_in{i}_{j}") for j in range(PAIRS)] for i in range(2)]
        we_in, we_zero, setup = sem("we_in"), sem("we_zero"), sem("setup")
        passed = sem("e_passed")
        AHEAD = 2
        geo = Count(sem("geo"), 9)
        hot_done = Count(sem("hot_done"), 1)
        penH_done = Count(sem("penH_done"), 2)
        penS_ps = Count(sem("penS_ps"), 1)
        penS_done = Count(sem("penS_done"), 1)
        tr_ps2 = Count(sem("tr_ps2"), PAIRS)
        trcopy = Count(sem("trcopy"), 2 * PAIRS)
        ep_ps = Count(sem("ep_ps"), PAIRS)
        qb_ps = Count(sem("qb_ps"), PAIRS)
        ke_done = Count(sem("ke_done"), PAIRS)
        pr_done = Count(sem("pr_done"), PAIRS)
        red_done = Count(sem("red_done"), PAIRS, 1 + AHEAD * PAIRS)
        max_done = Count(sem("max_done"), 10)
        seq_ps = Count(sem("seq_ps"), 1)
        back_ps = Count(sem("back_ps"), 1)
        diff_done = Count(sem("diff_done"), 1)
        tail_done = Count(sem("tail_done"), 2)
        exp_done = Count(sem("exp_done"), 1)
        wv_done = Count(sem("wv_done"), PAIRS, 1 + AHEAD * PAIRS)
        agg_done = Count(sem("agg_done"), 1)
        merge = Count(sem("merge"), 9)
        factor_done = Count(sem("factor_done"), 1)

        def steps(eng, body):
            with eng.Fori(0, NW // 2) as u:
                body(u * 2, 0, u)
                body(u * 2 + 1, 1, u)
            body(NW - 1, 0, NW // 2)
            n = eng.value_load(keep["table"][0:1, 2 * NS:2 * NS + 1], min_val=NW, max_val=NS - 2)
            with eng.If(n > NW):
                with eng.Fori(NW // 2, n // 2) as u:
                    body(u * 2 + 1, 1, u)
                    body(u * 2 + 2, 0, u + 1)

        def window(eng, s):
            return eng.value_load(keep["table"][0:1, bass.ds(s + NS, 1)], min_val=0, max_val=NW - 1)

        block = ctx.enter_context(nc.Block())

        @block.sync
        def _(sp):
            sp.wait_ge(we_zero, 1)
            sp.dma_start(we2[0:ED, 0:DH], t["We"]).then_inc(we_in, 16)
            sp.dma_start(we2[ED:2 * ED, DH:2 * DH], t["We"]).then_inc(we_in, 16)

            def body(s, b, k):
                e0 = sp.value_load(keep["table"][0:1, bass.ds(s, 1)], min_val=0, max_val=E)
                w = window(sp, s)
                held(sp, red_done, red_done.at(s, 0) - PAIRS, passed)
                sp.dma_start(src[b][:], t["src"][bass.ds(e0, CHUNK)].rearrange("(p t) -> p t", t=T)
                             ).then_inc(src_in[b], 16)
                sp.dma_start(cur[b][:], t["dst"][bass.ds(e0 + 1, CHUNK)].rearrange("(p t) -> p t", t=T)
                             ).then_inc(edge_in[b], 16)
                sp.dma_start(nxt[b][:], t["dst"][bass.ds(e0 + 2, CHUNK)].rearrange("(p t) -> p t", t=T)
                             ).then_inc(edge_in[b], 16)
                sp.dma_start(ew[b][:], t["ew"][bass.ds(e0, CHUNK)].rearrange("(p t) -> p t", t=T)
                             ).then_inc(edge_in[b], 16)
                sp.dma_start(ef[b][:], t["ef"][bass.ds(e0, CHUNK), :].rearrange("(p t) n -> p (t n)", t=T)
                             ).then_inc(edge_in[b], 16)
                sp.dma_start(qw[b][:].rearrange("p c d -> p (c d)"), t["q"][bass.ds(w * P, P), :]
                             ).then_inc(q_in[b], 16)

            steps(sp, body)

        @block.gpsimd
        def _(pool):
            def body(s, b, k):
                pool.wait_ge(src_in[b], k * 16 + 16)
                for j in range(PAIRS):
                    held(pool, wv_done, wv_done.at(s, j + 1) - AHEAD * PAIRS, passed)
                    for i in (2 * j, 2 * j + 1):
                        pool.indirect_dma_start(kv[b][:, i, :], None, t["kv"][:, :],
                                                bass.IndirectOffsetOnAxis(ap=src[b][:, i:i + 1].bitcast(U32), axis=0)
                                                ).then_inc(kv_in[b][j], 16)

            steps(pool, body)

        @block.tensor
        def _(pe):
            for s in (penS_ps, tr_ps2, ep_ps, qb_ps, seq_ps, back_ps, agg_done):
                pe.sem_inc(s.sem, 1)
            pe.wait_ge(we_in, 32)

            def body(s, b, k):
                def turn(j):
                    pe.wait_ge(trcopy.sem, trcopy.at(s, 2 * max(j - 1, 0)))
                    for i in range(2):
                        pe.transpose(tr[j % 2][:, i * P:(i + 1) * P], hot[:, 2 * j + i], ident[:])
                    pe.transpose(tr[j % 2][:, 2 * P:3 * P], ef[b][:, j * P:(j + 1) * P], ident[:]
                                 ).then_inc(tr_ps2.sem, 1)

                pe.wait_ge(edge_in[b], k * 64 + 64)
                pe.wait_ge(hot_done.sem, hot_done.at(s, 1))
                turn(0)
                pe.wait_ge(q_in[b], k * 16 + 16)
                for j in range(PAIRS):
                    if j + 1 < PAIRS:
                        turn(j + 1)
                    pe.wait_ge(trcopy.sem, trcopy.at(s, 2 * j + 2))
                    pe.wait_ge(ke_done.sem, ke_done.at(s, max(j - 1, 0)))
                    pe.matmul(ep[j % 2][:], efT[j % 2][:], we2[:], start=True, stop=True).then_inc(ep_ps.sem, 1)
                    pe.wait_ge(pr_done.sem, pr_done.at(s, max(j - 1, 0)))
                    for i in range(2):
                        for c in range(3):
                            m = pe.matmul(qb[j % 2][:, i * D:(i + 1) * D], hotT[j % 2][:, i * P:(i + 1) * P],
                                          qw[b][:, c, :], start=c == 0, stop=c == 2)
                    m.then_inc(qb_ps.sem, 1)
                pe.wait_ge(penH_done.sem, penH_done.at(s, 2))
                for i in range(2):
                    m = pe.transpose(seq[:, 1, i:2 * P:2], penZ[:, i, :], ident[:])
                m.then_inc(penS_ps.sem, 1)
                pe.wait_ge(penS_done.sem, penS_done.at(s, 1))
                pe.wait_ge(max_done.sem, max_done.at(s, 3))
                sm = segmax[:].rearrange("p (h t) -> p h t", h=H)
                for i, c in enumerate((0, T - 1)):
                    m = pe.transpose(seq[:, 0, i:2 * P:2], sm[:, :, c], ident[:])
                m.then_inc(seq_ps.sem, 1)
                held(pe, max_done, max_done.at(s, 5), passed)
                for i in range(2):
                    m = pe.transpose(back[:, i * H:(i + 1) * H], across2[:, i:2 * P:2], ident[0:H, 0:H])
                m.then_inc(back_ps.sem, 1)
                pe.wait_ge(merge.sem, merge.at(s, 0))
                pe.wait_ge(tail_done.sem, tail_done.at(s, 2))
                for i in range(T):
                    pe.wait_ge(wv_done.sem, wv_done.at(s, i // 2 + 1))
                    m = pe.matmul(agg[:], hot[:, i], wv[:, i], start=i == 0, stop=i == T - 1)
                m.then_inc(agg_done.sem, 1)

            steps(pe, body)

        @block.scalar
        def _(act):
            for s in (penH_done, penS_done, trcopy, exp_done, factor_done):
                act.sem_inc(s.sem, 1)
            act.wait_ge(setup, 4)

            def body(s, b, k):
                ph = penH[:, 0:SCAN].rearrange("p (h t) -> p h t", h=H)
                act.wait_ge(geo.sem, geo.at(s, 9))
                nc.scalar.activation(ph[:, :, 1:T], pen[:, 0:T - 1].unsqueeze(1).broadcast_to([P, H, T - 1]),
                                     ACT.Copy).then_inc(penH_done.sem, 1)
                nc.scalar.activation(penZ[:, 0, :], pen1[:].broadcast_to([P, H]), ACT.Copy)
                nc.scalar.activation(penZ[:, 1, :], pen[:, T - 1:T].broadcast_to([P, H]), ACT.Copy
                                     ).then_inc(penH_done.sem, 1)
                for j in range(PAIRS):
                    act.wait_ge(tr_ps2.sem, tr_ps2.at(s, j + 1))
                    act.wait_ge(qb_ps.sem, qb_ps.at(s, max(j - 1, 0)))
                    nc.scalar.activation(efT[j % 2][:], tr[j % 2][:, 2 * P:3 * P], ACT.Copy).then_inc(trcopy.sem, 1)
                    nc.scalar.activation(hotT[j % 2][:], tr[j % 2][:, 0:2 * P], ACT.Copy).then_inc(trcopy.sem, 1)
                act.wait_ge(penS_ps.sem, penS_ps.at(s, 1))
                nc.scalar.activation(penS[:, 1:2 * P + 1], seq[:, 1, :], ACT.Copy).then_inc(penS_done.sem, 1)
                act.wait_ge(diff_done.sem, diff_done.at(s, 1))
                act.wait_ge(agg_done.sem, agg_done.at(s, 0))
                wh = wv[:, :, 0:AW].rearrange("p t (h d) -> p h t d", h=H)
                nc.scalar.activation(wh[:, :, :, DH], diff[:], ACT.Exp).then_inc(exp_done.sem, 1)
                act.wait_ge(merge.sem, merge.at(s, 5))
                nc.scalar.activation(factor[:], shift[:], ACT.Exp).then_inc(factor_done.sem, 1)

            steps(act, body)

        @block.vector
        def _(dve):
            nc.vector.memset(we2[:], 0.0).then_inc(we_zero, 1)
            for s in (geo, hot_done, ke_done, pr_done, max_done, diff_done, tail_done, merge):
                dve.sem_inc(s.sem, s.primer)
            dve.sem_inc(red_done.sem, red_done.primer)
            dve.sem_inc(wv_done.sem, wv_done.primer)
            nc.vector.memset(score[:], 0.0).then_inc(setup, 1)
            nc.vector.memset(penH[:], -BIG).then_inc(setup, 1)
            nc.vector.memset(penS[:], -BIG).then_inc(setup, 1)
            nc.vector.memset(acc[:], 0.0).then_inc(setup, 1)
            nc.vector.memset(top[:], -BIG).then_inc(setup, 1)
            dve.wait_ge(setup, 5)

            def body(s, b, k):
                w = window(dve, s)
                dve.wait_ge(edge_in[b], k * 64 + 64)
                dve.wait_ge(agg_done.sem, agg_done.at(s, 0))
                dve.wait_ge(penS_done.sem, penS_done.at(s, 0))
                nc.vector.tensor_tensor(same[:], cur[b][:], nxt[b][:], ALU.is_equal).then_inc(geo.sem, 1)
                nc.vector.tensor_scalar(local[:], cur[b][:], keep["wbase"][:, bass.ds(s, 1)], None, ALU.subtract
                                        ).then_inc(geo.sem, 1)
                nc.vector.tensor_tensor(single[:], cur[b][:, 0:1], cur[b][:, T - 1:T], ALU.is_equal
                                        ).then_inc(geo.sem, 1)
                nc.vector.tensor_scalar(ews[:], ew[b][:], SCALE, None, ALU.mult).then_inc(geo.sem, 1)
                dve.wait_ge(geo.sem, geo.at(s, 1))
                nc.vector.tensor_tensor(inside[:], same[:], keep["lastmask"][:], ALU.mult).then_inc(geo.sem, 1)
                dve.wait_ge(geo.sem, geo.at(s, 2))
                nc.vector.tensor_tensor(hot[:], iota[:].unsqueeze(1).broadcast_to([P, T, P]),
                                        local[:].unsqueeze(2).broadcast_to([P, T, P]), ALU.is_equal
                                        ).then_inc(hot_done.sem, 1)
                dve.wait_ge(geo.sem, geo.at(s, 5))
                nc.vector.tensor_scalar(pen[:], inside[:], -1.0, BIG, ALU.add, ALU.mult).then_inc(geo.sem, 1)
                nc.vector.tensor_scalar(pen1[:], single[:], -1.0, BIG, ALU.add, ALU.mult).then_inc(geo.sem, 1)
                nc.vector.tensor_scalar(last[:], inside[:], -1.0, 1.0, ALU.mult, ALU.add).then_inc(geo.sem, 1)
                dve.wait_ge(geo.sem, geo.at(s, 8))
                dve.sem_inc(geo.sem, 1)

                for j in range(PAIRS + 2):
                    if j < PAIRS:
                        dve.wait_ge(kv_in[b][j], k * 32 + 32)
                        dve.wait_ge(ep_ps.sem, ep_ps.at(s, j + 1))
                        dve.wait_ge(pr_done.sem, pr_done.at(s, max(j - 1, 0)))
                        nc.vector.tensor_tensor(
                            ke[j % 2][:],
                            kv[b][:, 2 * j:2 * j + 2, 0:D].rearrange("p t (h d) -> p t h d", h=H),
                            ep[j % 2][:].rearrange("p (t d) -> p t d", t=2).unsqueeze(2)
                              .broadcast_to([P, 2, H, DH]), ALU.add).then_inc(ke_done.sem, 1)
                    if 0 <= j - 1 < PAIRS:
                        n = j - 1
                        dve.wait_ge(ke_done.sem, ke_done.at(s, n + 1))
                        dve.wait_ge(qb_ps.sem, qb_ps.at(s, n + 1))
                        dve.wait_ge(red_done.sem, red_done.at(s, max(n - 1, 0)))
                        nc.vector.tensor_tensor(pr[n % 2][:], ke[n % 2][:],
                                                qb[n % 2][:].rearrange("p (t h d) -> p t h d", t=2, h=H), ALU.mult
                                                ).then_inc(pr_done.sem, 1)
                    if j >= 2:
                        n = j - 2
                        dve.wait_ge(pr_done.sem, pr_done.at(s, n + 1))
                        nc.vector.tensor_reduce(score[:, :, 2 * n:2 * n + 2].rearrange("p h t -> p t h"),
                                                pr[n % 2][:], AX.X, ALU.add).then_inc(red_done.sem, 1)
                dve.wait_ge(red_done.sem, red_done.at(s, PAIRS))
                nc.vector.tensor_tensor(score[:, :, 0:T], score[:, :, 0:T],
                                        ews[:].unsqueeze(1).broadcast_to([P, H, T]), ALU.mult
                                        ).then_inc(max_done.sem, 1)

                flat = score[:].rearrange("p h t -> p (h t)")
                dve.wait_ge(max_done.sem, max_done.at(s, 1))
                dve.wait_ge(penH_done.sem, penH_done.at(s, 2))
                nc.vector.tensor_tensor_scan(fwd[:], penH[:, 0:SCAN], flat, -BIG, ALU.add, ALU.max
                                             ).then_inc(max_done.sem, 1)
                dve.wait_ge(max_done.sem, max_done.at(s, 2))
                nc.vector.tensor_tensor_scan(segmax[:, ::-1], penH[:, SCAN:0:-1], fwd[:, ::-1], -BIG,
                                             ALU.add, ALU.max).then_inc(max_done.sem, 1)
                dve.wait_ge(seq_ps.sem, seq_ps.at(s, 1))
                dve.wait_ge(penS_done.sem, penS_done.at(s, 1))
                nc.vector.tensor_tensor_scan(across[:], penS[:, 0:2 * P], seq[:, 0, :], -BIG, ALU.add, ALU.max
                                             ).then_inc(max_done.sem, 1)
                dve.wait_ge(max_done.sem, max_done.at(s, 4))
                nc.vector.tensor_tensor_scan(across2[:, ::-1], penS[:, 2 * P:0:-1], across[:, ::-1], -BIG,
                                             ALU.add, ALU.max).then_inc(max_done.sem, 1)
                sm = segmax[:].rearrange("p (h t) -> p h t", h=H)
                dve.wait_ge(back_ps.sem, back_ps.at(s, 1))
                for i, c in enumerate((0, T - 1)):
                    nc.vector.tensor_tensor(sm[:, :, c], sm[:, :, c], back[:, i * H:(i + 1) * H], ALU.max
                                            ).then_inc(max_done.sem, 1)
                dve.wait_ge(max_done.sem, max_done.at(s, 7))
                nc.vector.tensor_tensor_scan(fwd2[:], penH[:, 0:SCAN], segmax[:], -BIG, ALU.add, ALU.max
                                             ).then_inc(max_done.sem, 1)
                dve.wait_ge(max_done.sem, max_done.at(s, 8))
                nc.vector.tensor_tensor_scan(mx[:, ::-1], penH[:, SCAN:0:-1], fwd2[:, ::-1], -BIG,
                                             ALU.add, ALU.max).then_inc(max_done.sem, 1)
                dve.wait_ge(max_done.sem, max_done.at(s, 9))
                mxh = mx[:].rearrange("p (h t) -> p h t", h=H)
                nc.vector.tensor_tensor(diff[:], score[:, :, 0:T], mxh[:, :, 0:T], ALU.subtract
                                        ).then_inc(diff_done.sem, 1)
                dve.sem_inc(max_done.sem, 1)
                nc.vector.tensor_tensor(wv[:, :, AW:AW + H].rearrange("p t h -> p h t"), mxh[:, :, 0:T],
                                        last[:].unsqueeze(1).broadcast_to([P, H, T]), ALU.mult
                                        ).then_inc(tail_done.sem, 1)
                nc.vector.tensor_copy(wv[:, :, AW + H:RW], last[:].unsqueeze(2)).then_inc(tail_done.sem, 1)
                dve.wait_ge(exp_done.sem, exp_done.at(s, 1))
                for j in range(PAIRS):
                    o = wv[:, 2 * j:2 * j + 2, 0:AW].rearrange("p t (h d) -> p t h d", h=H)
                    nc.vector.tensor_tensor(
                        o[:, :, :, 0:DH], kv[b][:, 2 * j:2 * j + 2, D:2 * D].rearrange("p t (h d) -> p t h d", h=H),
                        o[:, :, :, DH:HW].broadcast_to([P, 2, H, DH]), ALU.mult).then_inc(wv_done.sem, 1)

                dve.wait_ge(agg_done.sem, agg_done.at(s, 1))
                old = top[:, bass.ds(w, 1), :].rearrange("p a h -> p (a h)")
                sums = acc[:, bass.ds(w, 1), :].rearrange("p a n -> p (a n)")
                nc.vector.tensor_scalar(absent[:], agg[:, AW + H:RW], -1.0, BIG, ALU.add, ALU.mult
                                        ).then_inc(merge.sem, 1)
                dve.wait_ge(merge.sem, merge.at(s, 1))
                nc.vector.tensor_scalar(part[:, 0], agg[:, AW:AW + H], absent[:], None, ALU.add
                                        ).then_inc(merge.sem, 1)
                dve.wait_ge(merge.sem, merge.at(s, 2))
                nc.vector.tensor_tensor(part[:, 1], part[:, 0], old, ALU.max).then_inc(merge.sem, 1)
                dve.wait_ge(merge.sem, merge.at(s, 3))
                nc.vector.tensor_tensor(shift[:, 0], old, part[:, 1], ALU.subtract).then_inc(merge.sem, 1)
                nc.vector.tensor_tensor(shift[:, 1], part[:, 0], part[:, 1], ALU.subtract).then_inc(merge.sem, 1)
                dve.wait_ge(factor_done.sem, factor_done.at(s, 1))
                nc.vector.tensor_tensor(scaled[:].rearrange("p (h d) -> p h d", h=H),
                                        agg[:, 0:AW].rearrange("p (h d) -> p h d", h=H),
                                        factor[:, 1].unsqueeze(2).broadcast_to([P, H, HW]), ALU.mult
                                        ).then_inc(merge.sem, 1)
                nc.vector.tensor_copy(old, part[:, 1]).then_inc(merge.sem, 1)
                sums3 = sums.rearrange("p (h d) -> p h d", h=H)
                nc.vector.tensor_tensor(sums3, sums3, factor[:, 0].unsqueeze(2).broadcast_to([P, H, HW]), ALU.mult
                                        ).then_inc(merge.sem, 1)
                dve.wait_ge(merge.sem, merge.at(s, 8))
                nc.vector.tensor_tensor(sums, sums, scaled[:], ALU.add).then_inc(merge.sem, 1)

            steps(dve, body)


def output_stage(nc, t, keep):
    with ExitStack() as ctx:
        sb, ps, sem = declare(ctx, nc)
        acc, ident = keep["acc"], keep["ident"]
        x = sb("o_x", [P, GW, D])
        x1 = sb("o_x1", [P, GW, D])
        att = sb("att", [P, GW, D])
        norm = [att, sb("norm1", [P, GW, D]), sb("norm2", [P, GW, D])]
        T3 = [sb(f"o_T{i}", [P, GW, KC, P]) for i in range(2)]
        inv = sb("inv", [P, GW, H])
        res = [sb(f"res{i}", [P, GW, D]) for i in range(2)]
        hT = sb("hT", [P, GW, FC, P], F32)
        out = x1
        wo, wf = sb("wo", [P, KC, D]), sb("wf", [P, KC, D])
        w1, w2 = sb("w1", [P, KC, FF]), sb("w2", [P, FC, D])
        rows = sb("o_rows", [P, 3, D])
        ab = sb("ab", [P, 2])
        lng, lnb, b1 = sb("o_lng", [P, KC]), sb("o_lnb", [P, KC]), sb("b1", [P, FC])
        bn, mv = sb("o_bn", [P, 2, GW, 6]), sb("o_mv", [P, 2, GW, 2])
        veps, rstd = sb("o_veps", [P, 2, GW]), sb("o_rstd", [P, 2, GW])
        half = sb("o_half", [P, GW])
        tr = [ps(f"o_tr{i}", [P, D]) for i in range(2)]
        mm = [ps(f"o_mm{i}", [P, D]) for i in range(2)]
        ph = [ps(f"o_h{i}", [P, FC, P]) for i in range(2)]

        w_in, wprep, b1_ps, half_done = sem("o_w_in"), sem("o_wprep"), sem("b1_ps"), sem("o_half_done")
        x_in, out_dma, passed = sem("o_x_in"), sem("out_dma"), sem("o_passed")
        stored = Count(sem("o_stored"), 1)
        inv_done = Count(sem("inv_done"), 2)
        nrm_done = [Count(sem(f"nrm_done{i}"), GW) for i in range(3)]
        tr_ps = Count(sem("o_tr_ps"), 3 * GW)
        T_done = Count(sem("o_T_done"), 3 * GW)
        mm_ps = Count(sem("mm_ps"), 3 * GW)
        bnd = [Count(sem(f"o_bn_done{i}"), GW) for i in range(2)]
        mvd = [Count(sem(f"o_mv_done{i}"), GW) for i in range(2)]
        ved = [Count(sem(f"o_veps_done{i}"), 1) for i in range(2)]
        rsd = [Count(sem(f"o_rstd_done{i}"), 1) for i in range(2)]
        pre_done = Count(sem("pre_done"), 4 * GW)
        res_done = [Count(sem(f"res_done{i}"), GW) for i in range(2)]
        out_done = Count(sem("out_done"), GW)
        h_ps = Count(sem("h_ps"), GW)
        gelu_done = Count(sem("gelu_done"), GW)

        xv = t["x"].rearrange("(g i p) d -> p g i d", i=GW, p=P)
        x1v = t["x1"].rearrange("(g i p) d -> p g i d", i=GW, p=P)
        ov = t["out"].rearrange("(g i p) d -> p g i d", i=GW, p=P)
        block = ctx.enter_context(nc.Block())

        @block.sync
        def _(sp):
            sp.sem_inc(stored.sem, 1)
            for name, dst in (("Wo", wo), ("WfT", wf), ("W1", w1), ("W2", w2)):
                sp.dma_start(dst[:], t[name].rearrange("(c p) n -> p c n", p=P)).then_inc(w_in, 16)
            for n, name in enumerate(("bo", "b2", "bf")):
                sp.dma_start(rows[:, n], t[name].rearrange("(a n) -> a n", a=1).broadcast_to([P, D])
                             ).then_inc(w_in, 16)
            for n, name in enumerate(("alpha", "beta")):
                sp.dma_start(ab[:, n:n + 1], t[name].rearrange("(a n) -> a n", a=1).broadcast_to([P, 1])
                             ).then_inc(w_in, 16)
            with nc.allow_non_contiguous_dma(reason="short vectors, once"):
                for name, dst in (("ln2_g", lng), ("ln2_b", lnb), ("b1", b1)):
                    sp.dma_start(dst[:], t[name].rearrange("(c p) -> p c", p=P)).then_inc(w_in, 16)
            with sp.Fori(0, NG) as g:
                sp.dma_start(x[:].unsqueeze(1), xv[:, bass.ds(g, 1)]).then_inc(x_in, 16)
                sp.dma_start(x1[:].unsqueeze(1), x1v[:, bass.ds(g, 1)]).then_inc(x_in, 16)
                held(sp, out_done, out_done.at(g, GW), passed)
                sp.dma_start(ov[:, bass.ds(g, 1)], out[:].unsqueeze(1)).then_inc(out_dma, 16)
                sp.wait_ge(out_dma, g * 16 + 16)
                sp.sem_inc(stored.sem, 1)

        @block.gpsimd
        def _(pool):
            for s in (*ved, *rsd, pre_done):
                pool.sem_inc(s.sem, 1)
            nc.gpsimd.memset(half[:], -0.5).then_inc(half_done, 1)
            pool.wait_ge(half_done, 1)
            pool.wait_ge(wprep, KC + 4 + KC + FC + 1)

            def rsqrt(g, n):
                held(pool, mvd[n], mvd[n].at(g, GW), passed)
                nc.gpsimd.tensor_scalar(veps[:, n, :], mv[:, n, :, 1], EPS, None, ALU.add).then_inc(ved[n].sem, 1)
                pool.wait_ge(ved[n].sem, ved[n].at(g, 1))
                nc.gpsimd.tensor_tensor(rstd[:, n, :], veps[:, n, :], half[:], ALU.pow).then_inc(rsd[n].sem, 1)

            with pool.Fori(0, NG) as g:
                pool.wait_ge(x_in, g * 32 + 32)
                for i in range(GW):
                    nc.gpsimd.tensor_tensor(x1[:, i], x1[:, i], rows[:, 0], ALU.add).then_inc(pre_done.sem, 1)
                for i in range(GW):
                    nc.gpsimd.tensor_tensor(x[:, i], x[:, i], rows[:, 1], ALU.add).then_inc(pre_done.sem, 1)
                rsqrt(g, 0)
                for i in range(GW):
                    pool.wait_ge(res_done[0].sem, res_done[0].at(g, i + 1))
                    pool.wait_ge(pre_done.sem, pre_done.at(g, GW + i + 1))
                    nc.gpsimd.tensor_tensor(x[:, i], x[:, i], res[0][:, i], ALU.add).then_inc(pre_done.sem, 1)
                rsqrt(g, 1)
                for i in range(GW):
                    pool.wait_ge(res_done[1].sem, res_done[1].at(g, i + 1))
                    nc.gpsimd.tensor_tensor(x1[:, i], res[1][:, i], rows[:, 2], ALU.add).then_inc(pre_done.sem, 1)

        @block.scalar
        def _(act):
            for s in (T_done, gelu_done):
                act.sem_inc(s.sem, 1)
            act.wait_ge(wprep, KC + 4 + KC + FC + 1)
            with act.Fori(0, NG) as g:
                for n in range(3):
                    for i in range(GW):
                        act.wait_ge(tr_ps.sem, tr_ps.at(g, n * GW + i + 1))
                        if n == 1:
                            act.wait_ge(h_ps.sem, h_ps.at(g, 0))
                        elif n == 0:
                            act.wait_ge(mm_ps.sem, mm_ps.at(g, 0))
                        else:
                            act.wait_ge(mm_ps.sem, mm_ps.at(g, i + 1))
                        nc.scalar.activation(T3[n % 2][:, i], tr[i % 2][:].rearrange("p (c n) -> p c n", c=KC),
                                             ACT.Copy).then_inc(T_done.sem, 1)
                    if n == 1:
                        for i in range(GW):
                            act.wait_ge(h_ps.sem, h_ps.at(g, i + 1))
                            act.wait_ge(mm_ps.sem, mm_ps.at(g, 0))
                            for c in range(FC):
                                m = nc.scalar.activation(hT[:, i, c], ph[i % 2][:, c], ACT.Gelu, bias=b1[:, c:c + 1])
                            m.then_inc(gelu_done.sem, 1)

        @block.tensor
        def _(pe):
            for s in (tr_ps, mm_ps, h_ps):
                pe.sem_inc(s.sem, 1)
            pe.wait_ge(w_in, 12 * 16)
            for f in range(FC):
                for c in range(KC):
                    m = pe.matmul(mm[0][:, f:f + 1], w1[:, c, f * P:(f + 1) * P], lnb[:, c:c + 1],
                                  start=c == 0, stop=c == KC - 1)
            m.then_inc(b1_ps, 1)
            pe.wait_ge(wprep, KC + 4 + KC + FC + 1)

            def turn(g, n):
                for i in range(GW):
                    pe.wait_ge(nrm_done[n].sem, nrm_done[n].at(g, i + 1))
                    pe.wait_ge(T_done.sem, T_done.at(g, max(n * GW + i - 1, 0)))
                    for c in range(KC):
                        m = pe.transpose(tr[i % 2][:, c * P:(c + 1) * P], norm[n][:, i, c * P:(c + 1) * P], ident[:])
                    m.then_inc(tr_ps.sem, 1)

            with pe.Fori(0, NG) as g:
                turn(g, 0)
                for i in range(GW):
                    pe.wait_ge(T_done.sem, T_done.at(g, i + 1))
                    pe.wait_ge(res_done[0].sem, res_done[0].at(g, max(i - 1, 0)))
                    pe.wait_ge(out_done.sem, out_done.at(g, 0))
                    for c in range(KC):
                        m = pe.matmul(mm[i % 2][:], T3[0][:, i, c], wo[:, c], start=c == 0, stop=c == KC - 1)
                    m.then_inc(mm_ps.sem, 1)
                turn(g, 1)
                for i in range(GW):
                    pe.wait_ge(T_done.sem, T_done.at(g, GW + i + 1))
                    pe.wait_ge(gelu_done.sem, gelu_done.at(g, max(i - 1, 0)))
                    for f in range(FC):
                        for c in range(KC):
                            m = pe.matmul(ph[i % 2][:, f], w1[:, c, f * P:(f + 1) * P], T3[1][:, i, c],
                                          start=c == 0, stop=c == KC - 1)
                    m.then_inc(h_ps.sem, 1)
                for i in range(GW):
                    pe.wait_ge(gelu_done.sem, gelu_done.at(g, i + 1))
                    pe.wait_ge(res_done[0].sem, res_done[0].at(g, GW))
                    pe.wait_ge(res_done[1].sem, res_done[1].at(g, max(i - 1, 0)))
                    for f in range(FC):
                        m = pe.matmul(mm[i % 2][:], hT[:, i, f], w2[:, f], start=f == 0, stop=f == FC - 1)
                    m.then_inc(mm_ps.sem, 1)
                turn(g, 2)
                for i in range(GW):
                    pe.wait_ge(T_done.sem, T_done.at(g, 2 * GW + i + 1))
                    pe.wait_ge(res_done[1].sem, res_done[1].at(g, GW))
                    pe.wait_ge(out_done.sem, out_done.at(g, max(i - 1, 0)))
                    for c in range(KC):
                        m = pe.matmul(mm[i % 2][:], T3[0][:, i, c], wf[:, c], start=c == 0, stop=c == KC - 1)
                    m.then_inc(mm_ps.sem, 1)

        @block.vector
        def _(dve):
            for s in (inv_done, *nrm_done, *bnd, *mvd, *res_done, out_done):
                dve.sem_inc(s.sem, 1)
            dve.wait_ge(w_in, 12 * 16)
            for c in range(KC):
                nc.vector.tensor_scalar(wo[:, c], wo[:, c], ab[:, 0:1], None, ALU.mult).then_inc(wprep, 1)
            for n in range(2):
                nc.vector.tensor_scalar(rows[:, n], rows[:, n], ab[:, n:n + 1], None, ALU.mult).then_inc(wprep, 1)
            for f in range(FC):
                nc.vector.tensor_scalar(w2[:, f], w2[:, f], ab[:, 1:2], None, ALU.mult).then_inc(wprep, 1)
            dve.wait_ge(b1_ps, 1)
            nc.vector.tensor_tensor(b1[:], b1[:], mm[0][:, 0:FC], ALU.add).then_inc(wprep, 1)
            for c in range(KC):
                nc.vector.tensor_scalar(w1[:, c], w1[:, c], lng[:, c:c + 1], None, ALU.mult).then_inc(wprep, 1)
            dve.wait_ge(wprep, KC + 2 + FC + 1 + KC)
            dve.sem_inc(wprep, 2)

            def stats(g, n):
                for i in range(GW):
                    dve.wait_ge(res_done[n].sem, res_done[n].at(g, i + 1))
                    nc.vector.bn_stats(bn[:, n, i], res[n][:, i]).then_inc(bnd[n].sem, 1)
                for i in range(GW):
                    held(dve, bnd[n], bnd[n].at(g, i + 1), passed)
                    nc.vector.bn_aggr(mv[:, n, i], bn[:, n, i]).then_inc(mvd[n].sem, 1)
                for i in range(GW):
                    dve.wait_ge(rsd[n].sem, rsd[n].at(g, 1))
                    nc.vector.tensor_scalar(norm[n + 1][:, i], res[n][:, i], mv[:, n, i, 0:1], rstd[:, n, i:i + 1],
                                            ALU.subtract, ALU.mult).then_inc(nrm_done[n + 1].sem, 1)

            with dve.Fori(0, NG) as g:
                a4 = acc[:, bass.ds(g * GW, GW), :].rearrange("p i (h d) -> p i h d", h=H)
                nc.vector.tensor_scalar(inv[:], a4[:, :, :, DH], 1e-30, None, ALU.max).then_inc(inv_done.sem, 1)
                dve.wait_ge(inv_done.sem, inv_done.at(g, 1))
                nc.vector.reciprocal(inv[:], inv[:]).then_inc(inv_done.sem, 1)
                dve.wait_ge(inv_done.sem, inv_done.at(g, 2))
                for i in range(GW):
                    ai = acc[:, bass.ds(g * GW + i, 1), :].rearrange("p a (h d) -> p (a h) d", h=H)
                    nc.vector.tensor_tensor(att[:, i].rearrange("p (h d) -> p h d", h=H), ai[:, :, 0:DH],
                                            inv[:, i].unsqueeze(2).broadcast_to([P, H, DH]), ALU.mult
                                            ).then_inc(nrm_done[0].sem, 1)
                for i in range(GW):
                    dve.wait_ge(mm_ps.sem, mm_ps.at(g, i + 1))
                    dve.wait_ge(pre_done.sem, pre_done.at(g, i + 1))
                    nc.vector.tensor_tensor(res[0][:, i], mm[i % 2][:], x1[:, i], ALU.add
                                            ).then_inc(res_done[0].sem, 1)
                stats(g, 0)
                for i in range(GW):
                    dve.wait_ge(mm_ps.sem, mm_ps.at(g, GW + i + 1))
                    dve.wait_ge(pre_done.sem, pre_done.at(g, 2 * GW + i + 1))
                    nc.vector.tensor_tensor(res[1][:, i], mm[i % 2][:], x[:, i], ALU.add
                                            ).then_inc(res_done[1].sem, 1)
                stats(g, 1)
                for i in range(GW):
                    dve.wait_ge(mm_ps.sem, mm_ps.at(g, 2 * GW + i + 1))
                    dve.wait_ge(pre_done.sem, pre_done.at(g, 3 * GW + i + 1))
                    nc.vector.tensor_tensor(out[:, i], mm[i % 2][:], x1[:, i], ALU.add
                                            ).then_inc(out_done.sem, 1)


def build(nc, t):
    with ExitStack() as ctx:
        sb, _, _ = declare(ctx, nc)
        keep = {
            "ident": sb("ident", [P, P]),
            "iota": sb("iota", [P, P]),
            "below": sb("below", [P, NW + 1]),
            "table": sb("table", [1, 2 * NS + 1], I32),
            "wbase": sb("wbase", [P, NS]),
            "lastmask": sb("lastmask", [P, T]),
        }
        node_stage(nc, t, keep)
        step_stage(nc, keep)
        keep["acc"] = sb("acc", [P, NW, AW])
        keep["top"] = sb("top", [P, NW, H])
        edge_stage(nc, t, keep)
        output_stage(nc, t, keep)


def kernel(x, src, dst, edge_attr_64, edge_weight, **w):
    import numpy as np
    import concourse.bacc as bacc
    from concourse.bass_utils import run_bass_kernel_spmd

    def rows(a, before, after, fill):
        a = np.asarray(a)
        wide = [(before, after)] + [(0, 0)] * (a.ndim - 1)
        return np.pad(a, wide, constant_values=fill)

    arrays = {
        "x": rows(x, 0, NPAD - N, 0),
        "src": rows(src, 0, CHUNK + 2, 0),
        "dst": rows(dst, 1, CHUNK + 2, FAR),
        "ef": rows(edge_attr_64, 0, CHUNK, 0),
        "ew": rows(edge_weight, 0, CHUNK, 0),
        "WfT": np.ascontiguousarray(np.asarray(w["L0_ffn_weight"]).T),
        "bf": np.asarray(w["L0_ffn_bias"]),
    }
    for name in ("Wq", "bq", "Wk", "bk", "Wv", "bv", "We", "be", "Wo", "bo", "ln1_g", "ln1_b", "ln2_g", "ln2_b",
                 "W1", "b1", "W2", "b2", "alpha", "beta"):
        arrays[name] = np.asarray(w[f"L0_gnn_{name}"])

    nc = bacc.Bacc("TRN2", target_bir_lowering=False, num_devices=1)
    t = {name: nc.dram_tensor(f"in_{name}", a.shape, mybir.dt.from_np(a.dtype), kind="ExternalInput").ap()
         for name, a in arrays.items()}
    t["x1"] = nc.dram_tensor("x1_table", (NPAD, D), F32).ap()
    t["kv"] = nc.dram_tensor("kv_table", (NPAD, 2 * D), F32).ap()
    t["q"] = nc.dram_tensor("q_table", (NPAD, 3 * D), BF16).ap()
    t["out"] = nc.dram_tensor("out", (NPAD, D), F32, kind="ExternalOutput").ap()
    build(nc, t)
    r = run_bass_kernel_spmd(nc, [{f"in_{name}": a for name, a in arrays.items()}], core_ids=[0])
    return r.results[0]["out"][:N]
```

```python
from contextlib import ExitStack

import concourse.bass as bass
from concourse import mybir

ALU = mybir.AluOpType
ACT = mybir.ActivationFunctionType
AX = mybir.AxisListType
F32 = mybir.dt.float32
BF16 = mybir.dt.bfloat16
I32 = mybir.dt.int32
U32 = mybir.dt.uint32

P = 128
N, E, D, H, ED, FF = 6250, 106250, 256, 8, 64, 1024
DH = D // H
NW = -(-N // P)
NPAD = NW * P
GW = 7
NG = NW // GW
T = 18
PAIRS = T // 2
CHUNK = T * P
EPAD = E + CHUNK
COLS = -(-E // P)
FAR = 1 << 20
KC = D // P
FC = FF // P
HW = DH + 1
AW = H * HW
RW = AW + H + 1
SEG = T + 1
SCAN = H * SEG
NS = 128
BIG = 1.0e30
EPS = 1e-5
SCALE = DH ** -0.5
assert NG * GW == NW and NW % 2 == 1 and NS > NW + E // CHUNK + 2


class Count:

    def __init__(self, sem, per, primer=1):
        self.sem, self.per, self.primer = sem, per, primer

    def at(self, rnd, n):
        return rnd * self.per + (self.primer + n)


def declare(ctx, nc):
    def sb(name, shape, dt=F32):
        return ctx.enter_context(nc.sbuf_tensor(name, shape, dt))

    def ps(name, shape, dt=F32):
        return ctx.enter_context(nc.psum_tensor(name, shape, dt))

    def sem(name):
        return ctx.enter_context(nc.semaphore(name))

    return sb, ps, sem


def held(eng, count, value, passed):
    eng.wait_ge(count.sem, value)
    eng.sem_inc(passed, 1)


def node_stage(nc, t, keep):
    with ExitStack() as ctx:
        sb, ps, sem = declare(ctx, nc)
        x = sb("x", [P, GW, D])
        x1 = sb("x1", [P, GW, D])
        xh = sb("xh", [P, GW, D])
        xT = sb("xT", [P, GW, KC, P])
        kv = sb("kv", [P, GW, 2 * D])
        qf = sb("qf", [P, GW, D])
        qrest = sb("qrest", [P, GW, D])
        qpart = sb("qpart", [P, GW, 3, D], BF16)
        wraw = sb("wraw", [P, KC, 3 * D])
        w = sb("w", [P, KC, 3 * D])
        lng = sb("lng", [P, KC])
        lnb = sb("lnb", [P, KC])
        lnb_wide = sb("lnb_wide", [P, KC, P])
        brow = sb("brow", [P, 3 * D])
        bias = sb("bias", [P, 3 * D])
        be = sb("be", [P, DH])
        ones = sb("ones", [P, P])
        bn = sb("bn", [P, 2, GW, 6])
        mv = sb("mv", [P, 2, GW, 2])
        veps = sb("veps", [P, 2, GW])
        rstd = sb("rstd", [P, 2, GW])
        half = sb("half", [P, GW])
        dall = sb("dall", [P, COLS], I32)
        dallf = sb("dallf", [P, COLS])
        signs = sb("signs", [P, COLS])
        thr_i = sb("thr_i", [P, NW + 1], I32)
        thr = sb("thr", [P, NW + 1])
        tr = [ps(f"n_tr{i}", [P, D]) for i in range(2)]
        pkv = [ps(f"n_pkv{i}", [P, 2 * D]) for i in range(2)]
        pq = [ps(f"n_pq{i}", [P, D]) for i in range(2)]
        pb = [ps(f"n_pb{i}", [P, 512]) for i in range(2)]

        w_in, dst_in, iota_done, thr_done = sem("w_in"), sem("dst_in"), sem("iota_done"), sem("thr_done")
        ones_done, wide_done, bias_ps, wprep = sem("ones_done"), sem("wide_done"), sem("bias_ps"), sem("wprep")
        half_done, dallf_done, sign_done = sem("half_done"), sem("dallf_done"), sem("sign_done")
        ident_done = sem("ident_done")
        passed = sem("n_passed")
        x_in, x1_out, kv_out, q_out = sem("x_in"), sem("x1_out"), sem("kv_out"), sem("q_out")
        stored = Count(sem("stored"), 1)
        bnd = [Count(sem(f"bn_done{i}"), GW) for i in range(2)]
        mvd = [Count(sem(f"mv_done{i}"), GW) for i in range(2)]
        ved = [Count(sem(f"veps_done{i}"), 1) for i in range(2)]
        rsd = [Count(sem(f"rstd_done{i}"), 1) for i in range(2)]
        x1_done = Count(sem("x1_done"), GW)
        xh_done = Count(sem("xh_done"), GW)
        tr_ps = Count(sem("tr_ps"), GW)
        xT_done = Count(sem("xT_done"), GW)
        kv_ps = Count(sem("kv_ps"), GW)
        q_ps = Count(sem("q_ps"), GW)
        kv_done = Count(sem("kv_done"), GW)
        qf_done = Count(sem("qf_done"), GW)
        hi_done = Count(sem("hi_done"), GW)
        rest_done = Count(sem("rest_done"), GW)
        mid_done = Count(sem("mid_done"), GW)
        lo_done = Count(sem("lo_done"), GW)

        xv = t["x"].rearrange("(g i p) d -> p g i d", i=GW, p=P)
        x1v = t["x1"].rearrange("(g i p) d -> p g i d", i=GW, p=P)
        kvv = t["kv"].rearrange("(g i p) d -> p g i d", i=GW, p=P)
        qv = t["q"].rearrange("(g i p) d -> p g i d", i=GW, p=P)
        block = ctx.enter_context(nc.Block())

        @block.sync
        def _(sp):
            sp.sem_inc(stored.sem, 1)
            sp.dma_start(x[:].unsqueeze(1), xv[:, 0:1]).then_inc(x_in, 16)
            for n, name in enumerate(("Wk", "Wv", "Wq")):
                sp.dma_start(wraw[:, :, n * D:(n + 1) * D],
                             t[name].rearrange("(c p) n -> p c n", p=P)).then_inc(w_in, 16)
            for n, name in enumerate(("bk", "bv", "bq")):
                sp.dma_start(brow[:, n * D:(n + 1) * D],
                             t[name].rearrange("(a n) -> a n", a=1).broadcast_to([P, D])).then_inc(w_in, 16)
            sp.dma_start(be[:], t["be"].rearrange("(a n) -> a n", a=1).broadcast_to([P, DH])).then_inc(w_in, 16)
            with nc.allow_non_contiguous_dma(reason="256 numbers, once"):
                sp.dma_start(lng[:], t["ln1_g"].rearrange("(c p) -> p c", p=P)).then_inc(w_in, 16)
                sp.dma_start(lnb[:], t["ln1_b"].rearrange("(c p) -> p c", p=P)).then_inc(w_in, 16)
            sp.dma_start(dall[:], t["dst"][1:1 + P * COLS].rearrange("(p c) -> p c", p=P)).then_inc(dst_in, 16)

            def group(g, more):
                held(sp, x1_done, x1_done.at(g, GW), passed)
                sp.dma_start(x1v[:, bass.ds(g, 1)], x1[:].unsqueeze(1)).then_inc(x1_out, 16)
                if more:
                    sp.dma_start(x[:].unsqueeze(1), xv[:, bass.ds(g + 1, 1)]).then_inc(x_in, 16)
                held(sp, kv_done, kv_done.at(g, GW), passed)
                sp.dma_start(kvv[:, bass.ds(g, 1)], kv[:].unsqueeze(1)).then_inc(kv_out, 16)
                held(sp, lo_done, lo_done.at(g, GW), passed)
                sp.dma_start(qv[:, bass.ds(g, 1)], qpart[:].rearrange("p i c d -> p i (c d)").unsqueeze(1)
                             ).then_inc(q_out, 16)
                for s in (x1_out, kv_out, q_out):
                    sp.wait_ge(s, g * 16 + 16)
                sp.sem_inc(stored.sem, 1)

            with sp.Fori(0, NG - 1) as g:
                group(g, True)
            group(NG - 1, False)

        @block.gpsimd
        def _(pool):
            nc.gpsimd.memset(half[:], -0.5).then_inc(half_done, 1)
            nc.gpsimd.iota(thr_i[:], [[P, NW + 1]], base=0, channel_multiplier=0).then_inc(iota_done, 1)
            nc.gpsimd.memset(keep["ident"][:], 0.0).then_inc(ident_done, 1)
            pool.wait_ge(ident_done, 1)
            nc.gpsimd.affine_select(out=keep["ident"][:], in_=keep["ident"][:], compare_op=ALU.not_equal, fill=1.0,
                                    base=0, pattern=[[-1, P]], channel_multiplier=1).then_inc(ident_done, 1)
            for s in ved + rsd:
                pool.sem_inc(s.sem, 1)
            pool.wait_ge(half_done, 1)
            with pool.Fori(0, NG) as g:
                for n in range(2):
                    held(pool, mvd[n], mvd[n].at(g, GW), passed)
                    nc.gpsimd.tensor_scalar(veps[:, n, :], mv[:, n, :, 1], EPS, None, ALU.add
                                            ).then_inc(ved[n].sem, 1)
                    pool.wait_ge(ved[n].sem, ved[n].at(g, 1))
                    nc.gpsimd.tensor_tensor(rstd[:, n, :], veps[:, n, :], half[:], ALU.pow).then_inc(rsd[n].sem, 1)

        @block.scalar
        def _(act):
            for s in (xT_done, hi_done, mid_done):
                act.sem_inc(s.sem, 1)
            act.wait_ge(iota_done, 1)
            nc.scalar.activation(thr[:], thr_i[:], ACT.Copy, bias=-0.5).then_inc(thr_done, 1)
            act.wait_ge(thr_done, 1)
            act.wait_ge(dallf_done, 1)
            with act.Fori(0, NG) as g:
                for i in range(GW):
                    act.wait_ge(tr_ps.sem, tr_ps.at(g, i + 1))
                    act.wait_ge(q_ps.sem, q_ps.at(g, 0))
                    nc.scalar.activation(xT[:, i], tr[i % 2][:].rearrange("p (c n) -> p c n", c=KC), ACT.Copy
                                         ).then_inc(xT_done.sem, 1)
                for i in range(GW):
                    act.wait_ge(sign_done, g * GW + i) if i else None
                    nc.scalar.activation(signs[:], dallf[:], ACT.Sign, bias=thr[:, bass.ds(g * GW + i, 1)],
                                         scale=-1.0, accum_out=keep["below"][:, bass.ds(g * GW + i, 1)]
                                         ).then_inc(sign_done, 1)
                for i in range(GW):
                    act.wait_ge(qf_done.sem, qf_done.at(g, i + 1))
                    act.wait_ge(stored.sem, stored.at(g, 0))
                    nc.scalar.activation(qpart[:, i, 0], qf[:, i], ACT.Copy).then_inc(hi_done.sem, 1)
                for i in range(GW):
                    act.wait_ge(rest_done.sem, rest_done.at(g, i + 1))
                    nc.scalar.activation(qpart[:, i, 1], qrest[:, i], ACT.Copy).then_inc(mid_done.sem, 1)
                act.wait_ge(sign_done, g * GW + GW)
            nc.scalar.activation(signs[:], dallf[:], ACT.Sign, bias=thr[:, NW:NW + 1], scale=-1.0,
                                 accum_out=keep["below"][:, NW:NW + 1]).then_inc(sign_done, 1)

        @block.tensor
        def _(pe):
            for s in (tr_ps, kv_ps, q_ps):
                pe.sem_inc(s.sem, 1)
            pe.wait_ge(wide_done, KC)
            pe.wait_ge(w_in, 9 * 16)
            for c in range(KC):
                pe.matmul(pb[0][:, 0:512], lnb_wide[:, c], wraw[:, c, 0:512], start=c == 0, stop=c == KC - 1)
            for c in range(KC):
                last = pe.matmul(pb[1][:, 0:D], lnb_wide[:, c], wraw[:, c, 512:512 + D],
                                 start=c == 0, stop=c == KC - 1)
            last.then_inc(bias_ps, 1)
            pe.wait_ge(ident_done, 2)
            pe.wait_ge(wprep, KC + 4)
            with pe.Fori(0, NG) as g:
                for i in range(GW):
                    pe.wait_ge(xh_done.sem, xh_done.at(g, i + 1))
                    pe.wait_ge(xT_done.sem, xT_done.at(g, max(i - 1, 0)))
                    for c in range(KC):
                        last = pe.transpose(tr[i % 2][:, c * P:(c + 1) * P], xh[:, i, c * P:(c + 1) * P],
                                            keep["ident"][:])
                    last.then_inc(tr_ps.sem, 1)
                for i in range(GW):
                    pe.wait_ge(xT_done.sem, xT_done.at(g, i + 1))
                    pe.wait_ge(kv_done.sem, kv_done.at(g, max(i - 1, 0)))
                    for c in range(KC):
                        last = pe.matmul(pkv[i % 2][:], xT[:, i, c], w[:, c, 0:2 * D], start=c == 0,
                                         stop=c == KC - 1)
                    last.then_inc(kv_ps.sem, 1)
                    pe.wait_ge(qf_done.sem, qf_done.at(g, max(i - 1, 0)))
                    for c in range(KC):
                        last = pe.matmul(pq[i % 2][:], xT[:, i, c], w[:, c, 2 * D:3 * D], start=c == 0,
                                         stop=c == KC - 1)
                    last.then_inc(q_ps.sem, 1)

        @block.vector
        def _(dve):
            for s in (*bnd, *mvd, x1_done, xh_done, kv_done, qf_done, rest_done, lo_done):
                dve.sem_inc(s.sem, 1)
            nc.vector.memset(ones[:], 1.0).then_inc(ones_done, 1)
            dve.wait_ge(ones_done, 1)
            dve.wait_ge(w_in, 9 * 16)
            for c in range(KC):
                nc.vector.tensor_scalar(lnb_wide[:, c], ones[:], lnb[:, c:c + 1], None, ALU.mult
                                        ).then_inc(wide_done, 1)
            nc.vector.tensor_tensor(brow[:, 0:D].rearrange("p (h d) -> p h d", h=H),
                                    brow[:, 0:D].rearrange("p (h d) -> p h d", h=H),
                                    be[:].unsqueeze(1).broadcast_to([P, H, DH]), ALU.add).then_inc(wprep, 1)
            for c in range(KC):
                nc.vector.tensor_scalar(w[:, c], wraw[:, c], lng[:, c:c + 1], None, ALU.mult).then_inc(wprep, 1)
            dve.wait_ge(wprep, 1 + KC)
            dve.wait_ge(bias_ps, 1)
            nc.vector.tensor_tensor(bias[:, 0:512], brow[:, 0:512], pb[0][:], ALU.add).then_inc(wprep, 1)
            nc.vector.tensor_tensor(bias[:, 512:768], brow[:, 512:768], pb[1][:, 0:D], ALU.add).then_inc(wprep, 1)
            dve.wait_ge(dst_in, 16)
            nc.vector.tensor_copy(dallf[:], dall[:]).then_inc(dallf_done, 1)
            dve.wait_ge(wprep, 3 + KC)
            dve.sem_inc(wprep, 1)
            with dve.Fori(0, NG) as g:
                for n, (a, b, done) in enumerate(((x, x1, x1_done), (x1, xh, xh_done))):
                    for i in range(GW):
                        if n == 0:
                            dve.wait_ge(x_in, g * 16 + 16)
                        else:
                            dve.wait_ge(x1_done.sem, x1_done.at(g, i + 1))
                        nc.vector.bn_stats(bn[:, n, i], a[:, i]).then_inc(bnd[n].sem, 1)
                    for i in range(GW):
                        held(dve, bnd[n], bnd[n].at(g, i + 1), passed)
                        nc.vector.bn_aggr(mv[:, n, i], bn[:, n, i]).then_inc(mvd[n].sem, 1)
                    for i in range(GW):
                        dve.wait_ge(rsd[n].sem, rsd[n].at(g, 1))
                        if n == 0:
                            dve.wait_ge(stored.sem, stored.at(g, 0))
                        else:
                            dve.wait_ge(tr_ps.sem, tr_ps.at(g, 0))
                        nc.vector.tensor_scalar(b[:, i], a[:, i], mv[:, n, i, 0:1], rstd[:, n, i:i + 1],
                                                ALU.subtract, ALU.mult).then_inc(done.sem, 1)
                for i in range(GW):
                    dve.wait_ge(kv_ps.sem, kv_ps.at(g, i + 1))
                    nc.vector.tensor_tensor(kv[:, i], pkv[i % 2][:], bias[:, 0:2 * D], ALU.add
                                            ).then_inc(kv_done.sem, 1)
                    dve.wait_ge(q_ps.sem, q_ps.at(g, i + 1))
                    dve.wait_ge(hi_done.sem, hi_done.at(g, 0))
                    dve.wait_ge(rest_done.sem, rest_done.at(g, 0))
                    nc.vector.tensor_tensor(qf[:, i], pq[i % 2][:], bias[:, 2 * D:], ALU.add
                                            ).then_inc(qf_done.sem, 1)
                for i in range(GW):
                    dve.wait_ge(hi_done.sem, hi_done.at(g, i + 1))
                    dve.wait_ge(lo_done.sem, lo_done.at(g, 0))
                    nc.vector.tensor_tensor(qrest[:, i], qf[:, i], qpart[:, i, 0], ALU.subtract
                                            ).then_inc(rest_done.sem, 1)
                for i in range(GW):
                    dve.wait_ge(mid_done.sem, mid_done.at(g, i + 1))
                    nc.vector.tensor_tensor(qpart[:, i, 2], qrest[:, i], qpart[:, i, 1], ALU.subtract
                                            ).then_inc(lo_done.sem, 1)


def step_stage(nc, keep):
    with ExitStack() as ctx:
        sb, ps, sem = declare(ctx, nc)
        ones = sb("s_ones", [P, P])
        iota_i = sb("iota_i", [P, P], I32)
        kthr_i = sb("kthr_i", [NW, E // CHUNK + 1], I32)
        kthr = sb("kthr", [NW, E // CHUNK + 1])
        more = sb("more", [NW, E // CHUNK + 1])
        before = sb("before", [NW, NW])
        below = sb("belowc", [P, NW + 1])
        col = sb("col", [NW, 6])
        past = sb("past", [NW, NS])
        rows = sb("rows", [1, 2, NS])
        base_i = sb("base_i", [1, NS], I32)
        base = sb("base", [1, NS])
        pcol = ps("pcol", [NW, 4])
        prow = ps("prow", [1, 2 * NS + 1])
        pwide = ps("pwide", [P, NS])
        made, fixed, sums, done = sem("made"), sem("fixed"), sem("sums"), sem("rows_done")
        block = ctx.enter_context(nc.Block())
        RP, NEXT, CHUNKS, END, SPARE, FIRST = range(6)

        @block.gpsimd
        def _(pool):
            nc.gpsimd.iota(iota_i[:], [[1, P]], base=0, channel_multiplier=0).then_inc(made, 1)
            nc.gpsimd.iota(kthr_i[:], [[CHUNK, E // CHUNK + 1]], base=CHUNK, channel_multiplier=0).then_inc(made, 1)
            nc.gpsimd.iota(base_i[:], [[CHUNK, NS]], base=0, channel_multiplier=0).then_inc(made, 1)
            nc.gpsimd.memset(before[:], 1.0).then_inc(made, 1)
            nc.gpsimd.memset(keep["lastmask"][:], 1.0).then_inc(made, 1)
            pool.wait_ge(made, 5)
            nc.gpsimd.affine_select(out=before[:], in_=before[:], compare_op=ALU.is_gt, fill=0.0, base=0,
                                    pattern=[[1, NW]], channel_multiplier=-1).then_inc(made, 1)
            nc.gpsimd.affine_select(out=keep["lastmask"][:], in_=keep["lastmask"][:], compare_op=ALU.not_equal,
                                    fill=0.0, base=-(P - 1 + T - 1), pattern=[[1, T]], channel_multiplier=1
                                    ).then_inc(made, 1)

        @block.vector
        def _(dve):
            def link(ins):
                link.n += 1
                ins.then_inc(fixed, 1)
                dve.wait_ge(fixed, link.n)
            link.n = 0
            dve.wait_ge(made, 7)
            link(nc.vector.memset(ones[:], 1.0))
            link(nc.vector.tensor_scalar(below[:], keep["below"][:], float(COLS), 0.5, ALU.add, ALU.mult))
            link(nc.vector.tensor_copy(kthr[:], kthr_i[:]))
            link(nc.vector.tensor_copy(keep["iota"][:], iota_i[:]))
            link(nc.vector.tensor_copy(base[:], base_i[:]))
            dve.wait_ge(sums, 1)
            link(nc.vector.tensor_copy(col[:, RP:RP + 2], pcol[:, 0:2]))
            link(nc.vector.tensor_tensor(col[:, SPARE:SPARE + 1], col[:, NEXT:NEXT + 1], col[:, RP:RP + 1],
                                         ALU.subtract))
            link(nc.vector.tensor_scalar(more[:], kthr[:], col[:, SPARE:SPARE + 1], 1.0, ALU.is_lt, ALU.add,
                                         accum_out=col[:, CHUNKS:CHUNKS + 1]))
            dve.sem_inc(done, 1)
            dve.wait_ge(sums, 2)
            link(nc.vector.tensor_tensor(col[:, END:END + 1], pcol[:, 2:3], col[:, CHUNKS:CHUNKS + 1], ALU.add))
            link(nc.vector.scalar_tensor_tensor(out=col[:, FIRST:FIRST + 1], in0=col[:, CHUNKS:CHUNKS + 1],
                                                scalar=-float(CHUNK), in1=col[:, SPARE:SPARE + 1],
                                                op0=ALU.mult, op1=ALU.add))
            link(nc.vector.tensor_scalar(past[:], keep["iota"][0:NW, 0:NS], col[:, END:END + 1], None, ALU.is_ge))
            dve.sem_inc(done, 1)
            dve.wait_ge(sums, 3)
            link(nc.vector.tensor_tensor(rows[:, 0], prow[:, 0:NS], base[:], ALU.add))
            link(nc.vector.tensor_scalar(keep["table"][:, 0:NS], rows[:, 0], float(E), 0.0, ALU.min, ALU.max))
            link(nc.vector.tensor_scalar(keep["table"][:, NS:2 * NS], prow[:, NS:2 * NS], float(NW - 1), None,
                                         ALU.min))
            link(nc.vector.tensor_copy(keep["table"][:, 2 * NS:2 * NS + 1], prow[:, 2 * NS:2 * NS + 1]))
            link(nc.vector.tensor_scalar(keep["wbase"][:], pwide[:], float(NW - 1), float(P), ALU.min, ALU.mult))

        @block.tensor
        def _(pe):
            pe.wait_ge(fixed, 2)
            pe.matmul(pcol[:, 0:1], below[:, 0:NW], ones[:, 0:1], start=True, stop=True)
            pe.matmul(pcol[:, 1:2], below[:, 1:NW + 1], ones[:, 0:1], start=True, stop=True).then_inc(sums, 1)
            pe.wait_ge(done, 1)
            pe.wait_ge(fixed, 8)
            pe.matmul(pcol[:, 2:3], before[:], col[:, CHUNKS:CHUNKS + 1], start=True, stop=True).then_inc(sums, 1)
            pe.wait_ge(done, 2)
            pe.wait_ge(fixed, 11)
            pe.matmul(prow[:, 0:NS], col[:, FIRST:FIRST + 1], past[:], start=True, stop=True)
            pe.matmul(prow[:, NS:2 * NS], ones[0:NW, 0:1], past[:], start=True, stop=True)
            pe.matmul(prow[:, 2 * NS:2 * NS + 1], col[:, CHUNKS:CHUNKS + 1], ones[0:NW, 0:1], start=True, stop=True)
            pe.matmul(pwide[:], ones[0:NW, :], past[:], start=True, stop=True).then_inc(sums, 1)


def edge_stage(nc, t, keep):
    with ExitStack() as ctx:
        sb, ps, sem = declare(ctx, nc)
        acc, top, ident, iota = keep["acc"], keep["top"], keep["ident"], keep["iota"]
        src = [sb(f"src{i}", [P, T], I32) for i in range(2)]
        cur = [sb(f"cur{i}", [P, T], I32) for i in range(2)]
        nxt = [sb(f"nxt{i}", [P, T], I32) for i in range(2)]
        ew = [sb(f"ew{i}", [P, T]) for i in range(2)]
        ef = [sb(f"ef{i}", [P, T * ED]) for i in range(2)]
        qw = [sb(f"qw{i}", [P, 3, D], BF16) for i in range(2)]
        kv = [sb(f"kvg{i}", [P, T, 2 * D]) for i in range(2)]
        we2 = sb("we2", [P, 2 * DH])
        same = sb("same", [P, T])
        inside = sb("inside", [P, T])
        single = sb("single", [P, 1])
        pen = sb("pen", [P, T])
        pen1 = sb("pen1", [P, 1])
        local = sb("local", [P, T])
        last = [sb(f"last{i}", [P, T]) for i in range(2)]
        ews = [sb(f"ews{i}", [P, T]) for i in range(2)]
        hot = [sb(f"hot{i}", [P, T, P], BF16) for i in range(2)]
        hot32 = sb("hot32", [P, T, P])
        identh = sb("identh", [P, P], BF16)
        hotT = [sb(f"hotT{i}", [P, 2 * P], BF16) for i in range(2)]
        efT = [sb(f"efT{i}", [P, P]) for i in range(2)]
        ke = [sb(f"ke{i}", [P, 2, H, DH]) for i in range(2)]
        pr = [sb(f"pr{i}", [P, 2, H, DH]) for i in range(2)]
        score = [sb(f"score{i}", [P, H, SEG]) for i in range(2)]
        penH = [sb(f"penH{i}", [P, SCAN + 1]) for i in range(2)]
        penZ = sb("penZ", [P, 2, H])
        penS = [sb(f"penS{i}", [H, 2 * P + 1]) for i in range(2)]
        fwd = sb("fwd", [P, SCAN])
        segmax = sb("segmax", [P, SCAN])
        fwd2 = sb("fwd2", [P, SCAN])
        mx = sb("mx", [P, SCAN])
        across = sb("across", [H, 2 * P])
        across2 = sb("across2", [H, 2 * P])
        diff = sb("diff", [P, H, T])
        wv = sb("wv", [P, T, RW])
        absent = sb("absent", [P, 1])
        part = sb("part", [P, 3, H])
        shift = sb("shift", [P, 2, H])
        factor = sb("factor", [P, 2, H])
        scaled = sb("scaled", [P, AW])

        tr = [ps(f"e_tr{i}", [P, 2 * P]) for i in range(2)]
        trf = [a[:, 0:P] for a in tr]
        trh = [a[:, P:2 * P].bitcast(BF16) for a in tr]
        qb = [ps(f"e_qb{i}", [P, 2 * D]) for i in range(2)]
        ep = [ps(f"e_ep{i}", [P, 2 * DH]) for i in range(2)]
        agg = ps("e_agg", [P, RW])
        turns = ps("e_turns", [P, 4 * P])
        seq = turns[0:H, :].rearrange("h (a n) -> h a n", a=2)
        back = turns[:, 2 * P:2 * P + 2 * H]

        src_in = [sem(f"src_in{i}") for i in range(2)]
        edge_in = [sem(f"edge_in{i}") for i in range(2)]
        q_in = [sem(f"q_in{i}") for i in range(2)]
        kv_in = [[sem(f"kv_in{i}_{j}") for j in range(PAIRS)] for i in range(2)]
        we_in, we_zero, setup = sem("we_in"), sem("we_zero"), sem("setup")
        passed = sem("e_passed")
        AHEAD = 2
        geo = Count(sem("geo"), 9)
        hot_done = Count(sem("hot_done"), 1)
        hot32_done = Count(sem("hot32_done"), 1)
        penH_done = Count(sem("penH_done"), 2)
        penS_ps = Count(sem("penS_ps"), 1)
        penS_done = Count(sem("penS_done"), 1)
        tr_ps2 = Count(sem("tr_ps2"), PAIRS)
        trcopy = Count(sem("trcopy"), 2 * PAIRS)
        ep_ps = Count(sem("ep_ps"), PAIRS)
        qb_ps = Count(sem("qb_ps"), PAIRS)
        ke_done = Count(sem("ke_done"), PAIRS)
        pr_done = Count(sem("pr_done"), PAIRS)
        red_done = Count(sem("red_done"), PAIRS, 1 + AHEAD * PAIRS)
        max_done = Count(sem("max_done"), 10)
        seq_ps = Count(sem("seq_ps"), 1)
        back_ps = Count(sem("back_ps"), 1)
        diff_done = Count(sem("diff_done"), 1)
        tail_done = Count(sem("tail_done"), 2)
        exp_done = Count(sem("exp_done"), 1)
        wv_done = Count(sem("wv_done"), PAIRS, 1 + AHEAD * PAIRS)
        agg_done = Count(sem("agg_done"), 1)
        merge = Count(sem("merge"), 9)
        factor_done = Count(sem("factor_done"), 1)

        def steps(eng, body):
            body(0, 0, 0, None)
            with eng.Fori(0, NW // 2) as u:
                body(u * 2 + 1, 1, u, u * 2)
                body(u * 2 + 2, 0, u + 1, u * 2 + 1)
            n = eng.value_load(keep["table"][0:1, 2 * NS:2 * NS + 1], min_val=NW, max_val=NS - 2)
            with eng.If(n > NW):
                with eng.Fori(NW // 2, n // 2) as u:
                    body(u * 2 + 1, 1, u, u * 2)
                    body(u * 2 + 2, 0, u + 1, u * 2 + 1)
            return n // 2 * 2

        def window(eng, s):
            return eng.value_load(keep["table"][0:1, bass.ds(s + NS, 1)], min_val=0, max_val=NW - 1)

        block = ctx.enter_context(nc.Block())

        @block.sync
        def _(sp):
            sp.wait_ge(we_zero, 1)
            sp.dma_start(we2[0:ED, 0:DH], t["We"]).then_inc(we_in, 16)
            sp.dma_start(we2[ED:2 * ED, DH:2 * DH], t["We"]).then_inc(we_in, 16)

            def load(s, b, k, x):
                e0 = sp.value_load(keep["table"][0:1, bass.ds(s, 1)], min_val=0, max_val=E)
                w = window(sp, s)
                held(sp, red_done, red_done.at(s, 0) - PAIRS, passed)
                sp.dma_start(src[b][:], t["src"][bass.ds(e0, CHUNK)].rearrange("(p t) -> p t", t=T)
                             ).then_inc(src_in[b], 16)
                sp.dma_start(cur[b][:], t["dst"][bass.ds(e0 + 1, CHUNK)].rearrange("(p t) -> p t", t=T)
                             ).then_inc(edge_in[b], 16)
                sp.dma_start(nxt[b][:], t["dst"][bass.ds(e0 + 2, CHUNK)].rearrange("(p t) -> p t", t=T)
                             ).then_inc(edge_in[b], 16)
                sp.dma_start(ew[b][:], t["ew"][bass.ds(e0, CHUNK)].rearrange("(p t) -> p t", t=T)
                             ).then_inc(edge_in[b], 16)
                sp.dma_start(ef[b][:], t["ef"][bass.ds(e0, CHUNK), :].rearrange("(p t) n -> p (t n)", t=T)
                             ).then_inc(edge_in[b], 16)
                sp.dma_start(qw[b][:].rearrange("p c d -> p (c d)"), t["q"][bass.ds(w * P, P), :]
                             ).then_inc(q_in[b], 16)

            final = steps(sp, load)
            load(final + 1, 1, final // 2, None)
            for s, inc in ((src_in[1], 16), (edge_in[1], 64), (q_in[1], 16)):
                sp.wait_ge(s, final // 2 * inc + inc)
                sp.sem_inc(passed, 1)

        @block.gpsimd
        def _(pool):
            def gather(s, b, k, x):
                pool.wait_ge(src_in[b], k * 16 + 16)
                for j in range(PAIRS):
                    held(pool, wv_done, wv_done.at(s, j + 1) - AHEAD * PAIRS, passed)
                    for i in (2 * j, 2 * j + 1):
                        pool.indirect_dma_start(kv[b][:, i, :], None, t["kv"][:, :],
                                                bass.IndirectOffsetOnAxis(ap=src[b][:, i:i + 1].bitcast(U32), axis=0)
                                                ).then_inc(kv_in[b][j], 16)

            steps(pool, gather)

        @block.tensor
        def _(pe):
            for s in (penS_ps, tr_ps2, ep_ps, qb_ps, seq_ps, back_ps, agg_done):
                pe.sem_inc(s.sem, 1)
            pe.wait_ge(we_in, 32)

            def turn(s, b, j):
                pe.wait_ge(trcopy.sem, trcopy.at(s, 2 * max(j - 1, 0)))
                for i in range(2):
                    pe.transpose(trh[j % 2][:, i * P:(i + 1) * P], hot[b][:, 2 * j + i], identh[:])
                pe.transpose(trf[j % 2][:], ef[b][:, j * P:(j + 1) * P], ident[:]).then_inc(tr_ps2.sem, 1)

            def spread(s, b, j):
                pe.wait_ge(trcopy.sem, trcopy.at(s, 2 * j + 2))
                pe.wait_ge(ke_done.sem, ke_done.at(s, max(j - 1, 0)))
                pe.matmul(ep[j % 2][:], efT[j % 2][:], we2[:], start=True, stop=True).then_inc(ep_ps.sem, 1)
                pe.wait_ge(pr_done.sem, pr_done.at(s, max(j - 1, 0)))
                for i in range(2):
                    for c in range(3):
                        m = pe.matmul(qb[j % 2][:, i * D:(i + 1) * D], hotT[j % 2][:, i * P:(i + 1) * P],
                                      qw[b][:, c, :], start=c == 0, stop=c == 2)
                m.then_inc(qb_ps.sem, 1)

            def penalty_rows(s, x):
                pe.wait_ge(penH_done.sem, penH_done.at(s, 2))
                if x is not None:
                    pe.wait_ge(max_done.sem, max_done.at(x, 7))
                for i in range(2):
                    m = pe.transpose(seq[:, 1, i:2 * P:2], penZ[:, i, :], ident[:])
                m.then_inc(penS_ps.sem, 1)

            def max_rows(x):
                pe.wait_ge(penS_done.sem, penS_done.at(x, 1))
                pe.wait_ge(max_done.sem, max_done.at(x, 3))
                sm = segmax[:].rearrange("p (h t) -> p h t", h=H)
                for i, c in enumerate((0, T - 1)):
                    m = pe.transpose(seq[:, 0, i:2 * P:2], sm[:, :, c], ident[:])
                m.then_inc(seq_ps.sem, 1)

            def max_cols(x):
                held(pe, max_done, max_done.at(x, 5), passed)
                for i in range(2):
                    m = pe.transpose(back[:, i * H:(i + 1) * H], across2[:, i:2 * P:2], ident[0:H, 0:H])
                m.then_inc(back_ps.sem, 1)

            def node_sums(x, j):
                if j == 0:
                    pe.wait_ge(merge.sem, merge.at(x, 0))
                    pe.wait_ge(tail_done.sem, tail_done.at(x, 2))
                    pe.wait_ge(hot32_done.sem, hot32_done.at(x, 1))
                pe.wait_ge(wv_done.sem, wv_done.at(x, j + 1))
                for i in (2 * j, 2 * j + 1):
                    m = pe.matmul(agg[:], hot32[:, i], wv[:, i], start=i == 0, stop=i == T - 1)
                if j == PAIRS - 1:
                    m.then_inc(agg_done.sem, 1)

            def body(s, b, k, x):
                pe.wait_ge(edge_in[b], k * 64 + 64)
                pe.wait_ge(hot_done.sem, hot_done.at(s, 1))
                turn(s, b, 0)
                pe.wait_ge(q_in[b], k * 16 + 16)
                for j in range(PAIRS):
                    if j + 1 < PAIRS:
                        turn(s, b, j + 1)
                    spread(s, b, j)
                    if j == 5:
                        penalty_rows(s, x)
                    if x is not None:
                        if j == 2:
                            max_rows(x)
                        if j == 4:
                            max_cols(x)
                        if j == 7:
                            node_sums(x, 0)
                if x is not None:
                    for j in range(1, PAIRS):
                        node_sums(x, j)

            final = steps(pe, body)
            max_rows(final)
            max_cols(final)
            for j in range(PAIRS):
                node_sums(final, j)

        @block.scalar
        def _(act):
            for s in (penH_done, penS_done, trcopy, exp_done, factor_done, hot32_done):
                act.sem_inc(s.sem, 1)
            act.wait_ge(setup, 8)

            def penalties(s, b):
                ph = penH[b][:, 0:SCAN].rearrange("p (h t) -> p h t", h=H)
                act.wait_ge(geo.sem, geo.at(s, 9))
                nc.scalar.activation(ph[:, :, 1:T], pen[:, 0:T - 1].unsqueeze(1).broadcast_to([P, H, T - 1]),
                                     ACT.Copy).then_inc(penH_done.sem, 1)
                nc.scalar.activation(penZ[:, 0, :], pen1[:].broadcast_to([P, H]), ACT.Copy)
                nc.scalar.activation(penZ[:, 1, :], pen[:, T - 1:T].broadcast_to([P, H]), ACT.Copy
                                     ).then_inc(penH_done.sem, 1)

            def copies(s, j):
                act.wait_ge(tr_ps2.sem, tr_ps2.at(s, j + 1))
                act.wait_ge(qb_ps.sem, qb_ps.at(s, max(j - 1, 0)))
                nc.scalar.activation(efT[j % 2][:], trf[j % 2][:], ACT.Copy).then_inc(trcopy.sem, 1)
                nc.scalar.activation(hotT[j % 2][:], trh[j % 2][:], ACT.Copy).then_inc(trcopy.sem, 1)

            def widen(x, xb):
                act.wait_ge(agg_done.sem, agg_done.at(x, 0))
                nc.scalar.activation(hot32[:], hot[xb][:], ACT.Copy).then_inc(hot32_done.sem, 1)

            def exponent(x):
                act.wait_ge(diff_done.sem, diff_done.at(x, 1))
                act.wait_ge(agg_done.sem, agg_done.at(x, 0))
                wh = wv[:, :, 0:AW].rearrange("p t (h d) -> p h t d", h=H)
                nc.scalar.activation(wh[:, :, :, DH], diff[:], ACT.Exp).then_inc(exp_done.sem, 1)

            def factors(x):
                act.wait_ge(merge.sem, merge.at(x, 5))
                nc.scalar.activation(factor[:], shift[:], ACT.Exp).then_inc(factor_done.sem, 1)

            def body(s, b, k, x):
                penalties(s, b)
                for j in range(PAIRS):
                    copies(s, j)
                    if j == 7:
                        act.wait_ge(penS_ps.sem, penS_ps.at(s, 1))
                        nc.scalar.activation(penS[b][:, 1:2 * P + 1], seq[:, 1, :], ACT.Copy
                                             ).then_inc(penS_done.sem, 1)
                    if x is not None:
                        if j == 3:
                            widen(x, 1 - b)
                        if j == 6:
                            exponent(x)
                if x is not None:
                    factors(x)

            final = steps(act, body)
            widen(final, 0)
            exponent(final)
            factors(final)

        @block.vector
        def _(dve):
            nc.vector.memset(we2[:], 0.0).then_inc(we_zero, 1)
            for s in (geo, hot_done, ke_done, pr_done, max_done, diff_done, tail_done, merge):
                dve.sem_inc(s.sem, s.primer)
            dve.sem_inc(red_done.sem, red_done.primer)
            dve.sem_inc(wv_done.sem, wv_done.primer)
            nc.vector.memset(acc[:], 0.0).then_inc(setup, 1)
            nc.vector.memset(top[:], -BIG).then_inc(setup, 1)
            for i in range(2):
                nc.vector.memset(score[i][:], 0.0).then_inc(setup, 1)
                nc.vector.memset(penH[i][:], -BIG).then_inc(setup, 1)
                nc.vector.memset(penS[i][:], -BIG).then_inc(setup, 1)
            nc.vector.tensor_copy(identh[:], ident[:]).then_inc(setup, 1)
            dve.wait_ge(setup, 9)

            def positions(s, b, k, first=False):
                dve.wait_ge(edge_in[b], k * 64 + 64)
                dve.wait_ge(penH_done.sem, penH_done.at(s, 0))
                nc.vector.tensor_tensor(same[:], cur[b][:], nxt[b][:], ALU.is_equal).then_inc(geo.sem, 1)
                nc.vector.tensor_scalar(local[:], cur[b][:], keep["wbase"][:, bass.ds(s, 1)], None, ALU.subtract
                                        ).then_inc(geo.sem, 1)
                nc.vector.tensor_tensor(single[:], cur[b][:, 0:1], cur[b][:, T - 1:T], ALU.is_equal
                                        ).then_inc(geo.sem, 1)
                nc.vector.tensor_scalar(ews[b][:], ew[b][:], SCALE, None, ALU.mult).then_inc(geo.sem, 1)
                dve.wait_ge(geo.sem, geo.at(s, 1))
                nc.vector.tensor_tensor(inside[:], same[:], keep["lastmask"][:], ALU.mult).then_inc(geo.sem, 1)
                dve.wait_ge(geo.sem, geo.at(s, 2))
                dve.wait_ge(hot32_done.sem, hot32_done.at(s - 1, 0) if not first else 1)
                nc.vector.tensor_tensor(hot[b][:], iota[:].unsqueeze(1).broadcast_to([P, T, P]),
                                        local[:].unsqueeze(2).broadcast_to([P, T, P]), ALU.is_equal
                                        ).then_inc(hot_done.sem, 1)
                dve.wait_ge(geo.sem, geo.at(s, 5))
                nc.vector.tensor_scalar(pen[:], inside[:], -1.0, BIG, ALU.add, ALU.mult).then_inc(geo.sem, 1)
                nc.vector.tensor_scalar(pen1[:], single[:], -1.0, BIG, ALU.add, ALU.mult).then_inc(geo.sem, 1)
                nc.vector.tensor_scalar(last[b][:], inside[:], -1.0, 1.0, ALU.mult, ALU.add).then_inc(geo.sem, 1)
                dve.wait_ge(geo.sem, geo.at(s, 8))
                dve.sem_inc(geo.sem, 1)

            def key(s, b, k, j):
                dve.wait_ge(kv_in[b][j], k * 32 + 32)
                dve.wait_ge(ep_ps.sem, ep_ps.at(s, j + 1))
                dve.wait_ge(pr_done.sem, pr_done.at(s, max(j - 1, 0)))
                nc.vector.tensor_tensor(
                    ke[j % 2][:], kv[b][:, 2 * j:2 * j + 2, 0:D].rearrange("p t (h d) -> p t h d", h=H),
                    ep[j % 2][:].rearrange("p (t d) -> p t d", t=2).unsqueeze(2).broadcast_to([P, 2, H, DH]),
                    ALU.add).then_inc(ke_done.sem, 1)

            def product(s, j):
                dve.wait_ge(ke_done.sem, ke_done.at(s, j + 1))
                dve.wait_ge(qb_ps.sem, qb_ps.at(s, j + 1))
                dve.wait_ge(red_done.sem, red_done.at(s, max(j - 1, 0)))
                nc.vector.tensor_tensor(pr[j % 2][:], ke[j % 2][:],
                                        qb[j % 2][:].rearrange("p (t h d) -> p t h d", t=2, h=H), ALU.mult
                                        ).then_inc(pr_done.sem, 1)

            def reduce(s, b, j):
                dve.wait_ge(pr_done.sem, pr_done.at(s, j + 1))
                nc.vector.tensor_reduce(score[b][:, :, 2 * j:2 * j + 2].rearrange("p h t -> p t h"),
                                        pr[j % 2][:], AX.X, ALU.add).then_inc(red_done.sem, 1)

            def scale_scores(x, xb):
                dve.wait_ge(red_done.sem, red_done.at(x, PAIRS))
                nc.vector.tensor_tensor(score[xb][:, :, 0:T], score[xb][:, :, 0:T],
                                        ews[xb][:].unsqueeze(1).broadcast_to([P, H, T]), ALU.mult
                                        ).then_inc(max_done.sem, 1)

            def scan(x, n, out, pens, values, forward):
                dve.wait_ge(max_done.sem, max_done.at(x, n - 1))
                size = out.shape[1]
                if forward:
                    m = nc.vector.tensor_tensor_scan(out[:], pens[:, 0:size], values, -BIG, ALU.add, ALU.max)
                else:
                    m = nc.vector.tensor_tensor_scan(out[:, ::-1], pens[:, size:0:-1], values[:, ::-1], -BIG,
                                                     ALU.add, ALU.max)
                m.then_inc(max_done.sem, 1)

            def forward_max(x, xb):
                dve.wait_ge(penH_done.sem, penH_done.at(x, 2))
                scan(x, 2, fwd, penH[xb], score[xb][:].rearrange("p h t -> p (h t)"), True)

            def backward_max(x, xb):
                scan(x, 3, segmax, penH[xb], fwd[:], False)

            def across_forward(x, xb):
                dve.wait_ge(seq_ps.sem, seq_ps.at(x, 1))
                scan(x, 4, across, penS[xb], seq[:, 0, :], True)

            def across_backward(x, xb):
                scan(x, 5, across2, penS[xb], across[:], False)

            def join_ends(x):
                sm = segmax[:].rearrange("p (h t) -> p h t", h=H)
                dve.wait_ge(back_ps.sem, back_ps.at(x, 1))
                for i, c in enumerate((0, T - 1)):
                    nc.vector.tensor_tensor(sm[:, :, c], sm[:, :, c], back[:, i * H:(i + 1) * H], ALU.max
                                            ).then_inc(max_done.sem, 1)

            mxh = mx[:].rearrange("p (h t) -> p h t", h=H)

            def differences(x, xb):
                dve.wait_ge(max_done.sem, max_done.at(x, 9))
                nc.vector.tensor_tensor(diff[:], score[xb][:, :, 0:T], mxh[:, :, 0:T], ALU.subtract
                                        ).then_inc(diff_done.sem, 1)
                dve.sem_inc(max_done.sem, 1)

            def tails(x, xb):
                dve.wait_ge(agg_done.sem, agg_done.at(x, 0))
                nc.vector.tensor_tensor(wv[:, :, AW:AW + H].rearrange("p t h -> p h t"), mxh[:, :, 0:T],
                                        last[xb][:].unsqueeze(1).broadcast_to([P, H, T]), ALU.mult
                                        ).then_inc(tail_done.sem, 1)
                nc.vector.tensor_copy(wv[:, :, AW + H:RW], last[xb][:].unsqueeze(2)).then_inc(tail_done.sem, 1)

            def weigh(x, xb, j):
                if j == 0:
                    dve.wait_ge(exp_done.sem, exp_done.at(x, 1))
                o = wv[:, 2 * j:2 * j + 2, 0:AW].rearrange("p t (h d) -> p t h d", h=H)
                nc.vector.tensor_tensor(
                    o[:, :, :, 0:DH], kv[xb][:, 2 * j:2 * j + 2, D:2 * D].rearrange("p t (h d) -> p t h d", h=H),
                    o[:, :, :, DH:HW].broadcast_to([P, 2, H, DH]), ALU.mult).then_inc(wv_done.sem, 1)

            def merge_step(x):
                w = window(dve, x)
                dve.wait_ge(agg_done.sem, agg_done.at(x, 1))
                old = top[:, bass.ds(w, 1), :].rearrange("p a h -> p (a h)")
                sums = acc[:, bass.ds(w, 1), :].rearrange("p a n -> p (a n)")
                nc.vector.tensor_scalar(absent[:], agg[:, AW + H:RW], -1.0, BIG, ALU.add, ALU.mult
                                        ).then_inc(merge.sem, 1)
                dve.wait_ge(merge.sem, merge.at(x, 1))
                nc.vector.tensor_scalar(part[:, 0], agg[:, AW:AW + H], absent[:], None, ALU.add
                                        ).then_inc(merge.sem, 1)
                dve.wait_ge(merge.sem, merge.at(x, 2))
                nc.vector.tensor_tensor(part[:, 1], part[:, 0], old, ALU.max).then_inc(merge.sem, 1)
                dve.wait_ge(merge.sem, merge.at(x, 3))
                nc.vector.tensor_tensor(shift[:, 0], old, part[:, 1], ALU.subtract).then_inc(merge.sem, 1)
                nc.vector.tensor_tensor(shift[:, 1], part[:, 0], part[:, 1], ALU.subtract).then_inc(merge.sem, 1)
                dve.wait_ge(factor_done.sem, factor_done.at(x, 1))
                nc.vector.tensor_tensor(scaled[:].rearrange("p (h d) -> p h d", h=H),
                                        agg[:, 0:AW].rearrange("p (h d) -> p h d", h=H),
                                        factor[:, 1].unsqueeze(2).broadcast_to([P, H, HW]), ALU.mult
                                        ).then_inc(merge.sem, 1)
                nc.vector.tensor_copy(old, part[:, 1]).then_inc(merge.sem, 1)
                sums3 = sums.rearrange("p (h d) -> p h d", h=H)
                nc.vector.tensor_tensor(sums3, sums3, factor[:, 0].unsqueeze(2).broadcast_to([P, H, HW]), ALU.mult
                                        ).then_inc(merge.sem, 1)
                dve.wait_ge(merge.sem, merge.at(x, 8))
                nc.vector.tensor_tensor(sums, sums, scaled[:], ALU.add).then_inc(merge.sem, 1)

            def softmax_part(x, xb, place):
                if place == (0, 0):
                    scale_scores(x, xb)
                if place == (1, 0):
                    forward_max(x, xb)
                if place == (1, 1):
                    backward_max(x, xb)
                if place == (3, 0):
                    across_forward(x, xb)
                if place == (3, 1):
                    across_backward(x, xb)
                if place == (4, 2):
                    join_ends(x)
                if place == (5, 0):
                    scan(x, 8, fwd2, penH[xb], segmax[:], True)
                if place == (5, 1):
                    scan(x, 9, mx, penH[xb], fwd2[:], False)
                if place == (5, 2):
                    differences(x, xb)
                if place == (6, 0):
                    tails(x, xb)
                if place in WEIGH:
                    weigh(x, xb, WEIGH.index(place))

            WEIGH = [(6, 2), (7, 0), (7, 1), (7, 2), (8, 0), (8, 1), (8, 2), (9, 1), (9, 2)]

            def body(s, b, k, x):
                for j in range(PAIRS + 2):
                    if j < PAIRS:
                        key(s, b, k, j)
                    if x is not None:
                        softmax_part(x, 1 - b, (j, 0))
                    if 0 <= j - 1 < PAIRS:
                        product(s, j - 1)
                    if x is not None:
                        softmax_part(x, 1 - b, (j, 1))
                    if j >= 2:
                        reduce(s, b, j - 2)
                    if x is not None:
                        softmax_part(x, 1 - b, (j, 2))
                positions(s + 1, 1 - b, k if b == 0 else k + 1)
                if x is not None:
                    merge_step(x)

            positions(0, 0, 0, first=True)
            final = steps(dve, body)
            for j in range(PAIRS + 2):
                for i in range(3):
                    softmax_part(final, 0, (j, i))
            merge_step(final)


def output_stage(nc, t, keep):
    with ExitStack() as ctx:
        sb, ps, sem = declare(ctx, nc)
        acc, ident = keep["acc"], keep["ident"]
        x = sb("o_x", [P, GW, D])
        x1 = sb("o_x1", [P, GW, D])
        att = sb("att", [P, GW, D])
        norm = [att, sb("norm1", [P, GW, D]), sb("norm2", [P, GW, D])]
        T3 = [sb(f"o_T{i}", [P, GW, KC, P]) for i in range(2)]
        inv = sb("inv", [P, GW, H])
        res = [sb(f"res{i}", [P, GW, D]) for i in range(2)]
        hT = sb("hT", [P, GW, FC, P], F32)
        out = x1
        wo, wf = sb("wo", [P, KC, D]), sb("wf", [P, KC, D])
        w1, w2 = sb("w1", [P, KC, FF]), sb("w2", [P, FC, D])
        rows = sb("o_rows", [P, 3, D])
        ab = sb("ab", [P, 2])
        lng, lnb, b1 = sb("o_lng", [P, KC]), sb("o_lnb", [P, KC]), sb("b1", [P, FC])
        bn, mv = sb("o_bn", [P, 2, GW, 6]), sb("o_mv", [P, 2, GW, 2])
        veps, rstd = sb("o_veps", [P, 2, GW]), sb("o_rstd", [P, 2, GW])
        half = sb("o_half", [P, GW])
        tr = [ps(f"o_tr{i}", [P, D]) for i in range(2)]
        mm = [ps(f"o_mm{i}", [P, D]) for i in range(2)]
        ph = [ps(f"o_h{i}", [P, FC, P]) for i in range(2)]

        w_in, wprep, b1_ps, half_done = sem("o_w_in"), sem("o_wprep"), sem("b1_ps"), sem("o_half_done")
        x_in, out_dma, passed = sem("o_x_in"), sem("out_dma"), sem("o_passed")
        stored = Count(sem("o_stored"), 1)
        inv_done = Count(sem("inv_done"), 2)
        nrm_done = [Count(sem(f"nrm_done{i}"), GW) for i in range(3)]
        tr_ps = Count(sem("o_tr_ps"), 3 * GW)
        T_done = Count(sem("o_T_done"), 3 * GW)
        mm_ps = Count(sem("mm_ps"), 3 * GW)
        bnd = [Count(sem(f"o_bn_done{i}"), GW) for i in range(2)]
        mvd = [Count(sem(f"o_mv_done{i}"), GW) for i in range(2)]
        ved = [Count(sem(f"o_veps_done{i}"), 1) for i in range(2)]
        rsd = [Count(sem(f"o_rstd_done{i}"), 1) for i in range(2)]
        pre_done = Count(sem("pre_done"), 4 * GW)
        res_done = [Count(sem(f"res_done{i}"), GW) for i in range(2)]
        out_done = Count(sem("out_done"), GW)
        h_ps = Count(sem("h_ps"), GW)
        gelu_done = Count(sem("gelu_done"), GW)

        xv = t["x"].rearrange("(g i p) d -> p g i d", i=GW, p=P)
        x1v = t["x1"].rearrange("(g i p) d -> p g i d", i=GW, p=P)
        ov = t["out"].rearrange("(g i p) d -> p g i d", i=GW, p=P)
        block = ctx.enter_context(nc.Block())

        @block.sync
        def _(sp):
            sp.sem_inc(stored.sem, 1)
            for name, dst in (("Wo", wo), ("WfT", wf), ("W1", w1), ("W2", w2)):
                sp.dma_start(dst[:], t[name].rearrange("(c p) n -> p c n", p=P)).then_inc(w_in, 16)
            for n, name in enumerate(("bo", "b2", "bf")):
                sp.dma_start(rows[:, n], t[name].rearrange("(a n) -> a n", a=1).broadcast_to([P, D])
                             ).then_inc(w_in, 16)
            for n, name in enumerate(("alpha", "beta")):
                sp.dma_start(ab[:, n:n + 1], t[name].rearrange("(a n) -> a n", a=1).broadcast_to([P, 1])
                             ).then_inc(w_in, 16)
            with nc.allow_non_contiguous_dma(reason="short vectors, once"):
                for name, dst in (("ln2_g", lng), ("ln2_b", lnb), ("b1", b1)):
                    sp.dma_start(dst[:], t[name].rearrange("(c p) -> p c", p=P)).then_inc(w_in, 16)
            with sp.Fori(0, NG) as g:
                sp.dma_start(x[:].unsqueeze(1), xv[:, bass.ds(g, 1)]).then_inc(x_in, 16)
                sp.dma_start(x1[:].unsqueeze(1), x1v[:, bass.ds(g, 1)]).then_inc(x_in, 16)
                held(sp, out_done, out_done.at(g, GW), passed)
                sp.dma_start(ov[:, bass.ds(g, 1)], out[:].unsqueeze(1)).then_inc(out_dma, 16)
                sp.wait_ge(out_dma, g * 16 + 16)
                sp.sem_inc(stored.sem, 1)

        @block.gpsimd
        def _(pool):
            for s in (*ved, *rsd, pre_done):
                pool.sem_inc(s.sem, 1)
            nc.gpsimd.memset(half[:], -0.5).then_inc(half_done, 1)
            pool.wait_ge(half_done, 1)
            pool.wait_ge(wprep, KC + 4 + KC + FC + 1)

            def rsqrt(g, n):
                held(pool, mvd[n], mvd[n].at(g, GW), passed)
                nc.gpsimd.tensor_scalar(veps[:, n, :], mv[:, n, :, 1], EPS, None, ALU.add).then_inc(ved[n].sem, 1)
                pool.wait_ge(ved[n].sem, ved[n].at(g, 1))
                nc.gpsimd.tensor_tensor(rstd[:, n, :], veps[:, n, :], half[:], ALU.pow).then_inc(rsd[n].sem, 1)

            with pool.Fori(0, NG) as g:
                pool.wait_ge(x_in, g * 32 + 32)
                for i in range(GW):
                    nc.gpsimd.tensor_tensor(x1[:, i], x1[:, i], rows[:, 0], ALU.add).then_inc(pre_done.sem, 1)
                for i in range(GW):
                    nc.gpsimd.tensor_tensor(x[:, i], x[:, i], rows[:, 1], ALU.add).then_inc(pre_done.sem, 1)
                rsqrt(g, 0)
                for i in range(GW):
                    pool.wait_ge(res_done[0].sem, res_done[0].at(g, i + 1))
                    pool.wait_ge(pre_done.sem, pre_done.at(g, GW + i + 1))
                    nc.gpsimd.tensor_tensor(x[:, i], x[:, i], res[0][:, i], ALU.add).then_inc(pre_done.sem, 1)
                rsqrt(g, 1)
                for i in range(GW):
                    pool.wait_ge(res_done[1].sem, res_done[1].at(g, i + 1))
                    nc.gpsimd.tensor_tensor(x1[:, i], res[1][:, i], rows[:, 2], ALU.add).then_inc(pre_done.sem, 1)

        @block.scalar
        def _(act):
            for s in (T_done, gelu_done):
                act.sem_inc(s.sem, 1)
            act.wait_ge(wprep, KC + 4 + KC + FC + 1)
            with act.Fori(0, NG) as g:
                for n in range(3):
                    for i in range(GW):
                        act.wait_ge(tr_ps.sem, tr_ps.at(g, n * GW + i + 1))
                        if n == 1:
                            act.wait_ge(h_ps.sem, h_ps.at(g, 0))
                        elif n == 0:
                            act.wait_ge(mm_ps.sem, mm_ps.at(g, 0))
                        else:
                            act.wait_ge(mm_ps.sem, mm_ps.at(g, i + 1))
                        nc.scalar.activation(T3[n % 2][:, i], tr[i % 2][:].rearrange("p (c n) -> p c n", c=KC),
                                             ACT.Copy).then_inc(T_done.sem, 1)
                    if n == 1:
                        for i in range(GW):
                            act.wait_ge(h_ps.sem, h_ps.at(g, i + 1))
                            act.wait_ge(mm_ps.sem, mm_ps.at(g, 0))
                            for c in range(FC):
                                m = nc.scalar.activation(hT[:, i, c], ph[i % 2][:, c], ACT.Gelu, bias=b1[:, c:c + 1])
                            m.then_inc(gelu_done.sem, 1)

        @block.tensor
        def _(pe):
            for s in (tr_ps, mm_ps, h_ps):
                pe.sem_inc(s.sem, 1)
            pe.wait_ge(w_in, 12 * 16)
            for f in range(FC):
                for c in range(KC):
                    m = pe.matmul(mm[0][:, f:f + 1], w1[:, c, f * P:(f + 1) * P], lnb[:, c:c + 1],
                                  start=c == 0, stop=c == KC - 1)
            m.then_inc(b1_ps, 1)
            pe.wait_ge(wprep, KC + 4 + KC + FC + 1)

            def turn(g, n):
                for i in range(GW):
                    pe.wait_ge(nrm_done[n].sem, nrm_done[n].at(g, i + 1))
                    pe.wait_ge(T_done.sem, T_done.at(g, max(n * GW + i - 1, 0)))
                    for c in range(KC):
                        m = pe.transpose(tr[i % 2][:, c * P:(c + 1) * P], norm[n][:, i, c * P:(c + 1) * P], ident[:])
                    m.then_inc(tr_ps.sem, 1)

            with pe.Fori(0, NG) as g:
                turn(g, 0)
                for i in range(GW):
                    pe.wait_ge(T_done.sem, T_done.at(g, i + 1))
                    pe.wait_ge(res_done[0].sem, res_done[0].at(g, max(i - 1, 0)))
                    pe.wait_ge(out_done.sem, out_done.at(g, 0))
                    for c in range(KC):
                        m = pe.matmul(mm[i % 2][:], T3[0][:, i, c], wo[:, c], start=c == 0, stop=c == KC - 1)
                    m.then_inc(mm_ps.sem, 1)
                turn(g, 1)
                for i in range(GW):
                    pe.wait_ge(T_done.sem, T_done.at(g, GW + i + 1))
                    pe.wait_ge(gelu_done.sem, gelu_done.at(g, max(i - 1, 0)))
                    for f in range(FC):
                        for c in range(KC):
                            m = pe.matmul(ph[i % 2][:, f], w1[:, c, f * P:(f + 1) * P], T3[1][:, i, c],
                                          start=c == 0, stop=c == KC - 1)
                    m.then_inc(h_ps.sem, 1)
                for i in range(GW):
                    pe.wait_ge(gelu_done.sem, gelu_done.at(g, i + 1))
                    pe.wait_ge(res_done[0].sem, res_done[0].at(g, GW))
                    pe.wait_ge(res_done[1].sem, res_done[1].at(g, max(i - 1, 0)))
                    for f in range(FC):
                        m = pe.matmul(mm[i % 2][:], hT[:, i, f], w2[:, f], start=f == 0, stop=f == FC - 1)
                    m.then_inc(mm_ps.sem, 1)
                turn(g, 2)
                for i in range(GW):
                    pe.wait_ge(T_done.sem, T_done.at(g, 2 * GW + i + 1))
                    pe.wait_ge(res_done[1].sem, res_done[1].at(g, GW))
                    pe.wait_ge(out_done.sem, out_done.at(g, max(i - 1, 0)))
                    for c in range(KC):
                        m = pe.matmul(mm[i % 2][:], T3[0][:, i, c], wf[:, c], start=c == 0, stop=c == KC - 1)
                    m.then_inc(mm_ps.sem, 1)

        @block.vector
        def _(dve):
            for s in (inv_done, *nrm_done, *bnd, *mvd, *res_done, out_done):
                dve.sem_inc(s.sem, 1)
            dve.wait_ge(w_in, 12 * 16)
            for c in range(KC):
                nc.vector.tensor_scalar(wo[:, c], wo[:, c], ab[:, 0:1], None, ALU.mult).then_inc(wprep, 1)
            for n in range(2):
                nc.vector.tensor_scalar(rows[:, n], rows[:, n], ab[:, n:n + 1], None, ALU.mult).then_inc(wprep, 1)
            for f in range(FC):
                nc.vector.tensor_scalar(w2[:, f], w2[:, f], ab[:, 1:2], None, ALU.mult).then_inc(wprep, 1)
            dve.wait_ge(b1_ps, 1)
            nc.vector.tensor_tensor(b1[:], b1[:], mm[0][:, 0:FC], ALU.add).then_inc(wprep, 1)
            for c in range(KC):
                nc.vector.tensor_scalar(w1[:, c], w1[:, c], lng[:, c:c + 1], None, ALU.mult).then_inc(wprep, 1)
            dve.wait_ge(wprep, KC + 2 + FC + 1 + KC)
            dve.sem_inc(wprep, 2)

            def stats(g, n):
                for i in range(GW):
                    dve.wait_ge(res_done[n].sem, res_done[n].at(g, i + 1))
                    nc.vector.bn_stats(bn[:, n, i], res[n][:, i]).then_inc(bnd[n].sem, 1)
                for i in range(GW):
                    held(dve, bnd[n], bnd[n].at(g, i + 1), passed)
                    nc.vector.bn_aggr(mv[:, n, i], bn[:, n, i]).then_inc(mvd[n].sem, 1)
                for i in range(GW):
                    dve.wait_ge(rsd[n].sem, rsd[n].at(g, 1))
                    nc.vector.tensor_scalar(norm[n + 1][:, i], res[n][:, i], mv[:, n, i, 0:1], rstd[:, n, i:i + 1],
                                            ALU.subtract, ALU.mult).then_inc(nrm_done[n + 1].sem, 1)

            with dve.Fori(0, NG) as g:
                a4 = acc[:, bass.ds(g * GW, GW), :].rearrange("p i (h d) -> p i h d", h=H)
                nc.vector.tensor_scalar(inv[:], a4[:, :, :, DH], 1e-30, None, ALU.max).then_inc(inv_done.sem, 1)
                dve.wait_ge(inv_done.sem, inv_done.at(g, 1))
                nc.vector.reciprocal(inv[:], inv[:]).then_inc(inv_done.sem, 1)
                dve.wait_ge(inv_done.sem, inv_done.at(g, 2))
                for i in range(GW):
                    ai = acc[:, bass.ds(g * GW + i, 1), :].rearrange("p a (h d) -> p (a h) d", h=H)
                    nc.vector.tensor_tensor(att[:, i].rearrange("p (h d) -> p h d", h=H), ai[:, :, 0:DH],
                                            inv[:, i].unsqueeze(2).broadcast_to([P, H, DH]), ALU.mult
                                            ).then_inc(nrm_done[0].sem, 1)
                for i in range(GW):
                    dve.wait_ge(mm_ps.sem, mm_ps.at(g, i + 1))
                    dve.wait_ge(pre_done.sem, pre_done.at(g, i + 1))
                    nc.vector.tensor_tensor(res[0][:, i], mm[i % 2][:], x1[:, i], ALU.add
                                            ).then_inc(res_done[0].sem, 1)
                stats(g, 0)
                for i in range(GW):
                    dve.wait_ge(mm_ps.sem, mm_ps.at(g, GW + i + 1))
                    dve.wait_ge(pre_done.sem, pre_done.at(g, 2 * GW + i + 1))
                    nc.vector.tensor_tensor(res[1][:, i], mm[i % 2][:], x[:, i], ALU.add
                                            ).then_inc(res_done[1].sem, 1)
                stats(g, 1)
                for i in range(GW):
                    dve.wait_ge(mm_ps.sem, mm_ps.at(g, 2 * GW + i + 1))
                    dve.wait_ge(pre_done.sem, pre_done.at(g, 3 * GW + i + 1))
                    nc.vector.tensor_tensor(out[:, i], mm[i % 2][:], x1[:, i], ALU.add
                                            ).then_inc(out_done.sem, 1)


def build(nc, t):
    with ExitStack() as ctx:
        sb, _, _ = declare(ctx, nc)
        keep = {
            "ident": sb("ident", [P, P]),
            "iota": sb("iota", [P, P]),
            "below": sb("below", [P, NW + 1]),
            "table": sb("table", [1, 2 * NS + 1], I32),
            "wbase": sb("wbase", [P, NS]),
            "lastmask": sb("lastmask", [P, T]),
        }
        node_stage(nc, t, keep)
        step_stage(nc, keep)
        keep["acc"] = sb("acc", [P, NW, AW])
        keep["top"] = sb("top", [P, NW, H])
        edge_stage(nc, t, keep)
        output_stage(nc, t, keep)


def kernel(x, src, dst, edge_attr_64, edge_weight, **w):
    import numpy as np
    import concourse.bacc as bacc
    from concourse.bass_utils import run_bass_kernel_spmd

    def rows(a, before, after, fill):
        a = np.asarray(a)
        wide = [(before, after)] + [(0, 0)] * (a.ndim - 1)
        return np.pad(a, wide, constant_values=fill)

    arrays = {
        "x": rows(x, 0, NPAD - N, 0),
        "src": rows(src, 0, CHUNK + 2, 0),
        "dst": rows(dst, 1, CHUNK + 2, FAR),
        "ef": rows(edge_attr_64, 0, CHUNK, 0),
        "ew": rows(edge_weight, 0, CHUNK, 0),
        "WfT": np.ascontiguousarray(np.asarray(w["L0_ffn_weight"]).T),
        "bf": np.asarray(w["L0_ffn_bias"]),
    }
    for name in ("Wq", "bq", "Wk", "bk", "Wv", "bv", "We", "be", "Wo", "bo", "ln1_g", "ln1_b", "ln2_g", "ln2_b",
                 "W1", "b1", "W2", "b2", "alpha", "beta"):
        arrays[name] = np.asarray(w[f"L0_gnn_{name}"])

    nc = bacc.Bacc("TRN2", target_bir_lowering=False, num_devices=1)
    t = {name: nc.dram_tensor(f"in_{name}", a.shape, mybir.dt.from_np(a.dtype), kind="ExternalInput").ap()
         for name, a in arrays.items()}
    t["x1"] = nc.dram_tensor("x1_table", (NPAD, D), F32).ap()
    t["kv"] = nc.dram_tensor("kv_table", (NPAD, 2 * D), F32).ap()
    t["q"] = nc.dram_tensor("q_table", (NPAD, 3 * D), BF16).ap()
    t["out"] = nc.dram_tensor("out", (NPAD, D), F32, kind="ExternalOutput").ap()
    build(nc, t)
    r = run_bass_kernel_spmd(nc, [{f"in_{name}": a for name, a in arrays.items()}], core_ids=[0])
    return r.results[0]["out"][:N]
```

```python
from contextlib import ExitStack

import concourse.bass as bass
from concourse import mybir

ALU = mybir.AluOpType
ACT = mybir.ActivationFunctionType
AX = mybir.AxisListType
F32 = mybir.dt.float32
BF16 = mybir.dt.bfloat16
I32 = mybir.dt.int32
U32 = mybir.dt.uint32

P = 128
N, E, D, H, ED, FF = 6250, 106250, 256, 8, 64, 1024
DH = D // H
NW = -(-N // P)
NPAD = NW * P
GW = 7
NG = NW // GW
T = 18
PAIRS = T // 2
CHUNK = T * P
EPAD = E + CHUNK
COLS = -(-E // P)
FAR = 1 << 20
KC = D // P
FC = FF // P
HW = DH + 1
AW = H * HW
RW = AW + H + 1
SEG = T + 1
SCAN = H * SEG
LAG = 3
NS = 128
BIG = 1.0e30
EPS = 1e-5
SCALE = DH ** -0.5
assert NG * GW == NW and NW % 2 == 1 and NS > NW + E // CHUNK + 2 * LAG


class Count:

    def __init__(self, sem, per, primer=1):
        self.sem, self.per, self.primer = sem, per, primer

    def at(self, rnd, n):
        return rnd * self.per + (self.primer + n)


def declare(ctx, nc):
    def sb(name, shape, dt=F32):
        return ctx.enter_context(nc.sbuf_tensor(name, shape, dt))

    def ps(name, shape, dt=F32):
        return ctx.enter_context(nc.psum_tensor(name, shape, dt))

    def sem(name):
        return ctx.enter_context(nc.semaphore(name))

    return sb, ps, sem


def held(eng, count, value, passed):
    eng.wait_ge(count.sem, value)
    eng.sem_inc(passed, 1)


def node_stage(nc, t, keep):
    with ExitStack() as ctx:
        sb, ps, sem = declare(ctx, nc)
        x = sb("x", [P, GW, D])
        x1 = sb("x1", [P, GW, D])
        xh = sb("xh", [P, GW, D])
        xT = sb("xT", [P, GW, KC, P])
        kv = sb("kv", [P, GW, 2 * D])
        qf = sb("qf", [P, GW, D])
        qrest = sb("qrest", [P, GW, D])
        qpart = sb("qpart", [P, GW, 3, D], BF16)
        wraw = sb("wraw", [P, KC, 3 * D])
        w = sb("w", [P, KC, 3 * D])
        lng = sb("lng", [P, KC])
        lnb = sb("lnb", [P, KC])
        lnb_wide = sb("lnb_wide", [P, KC, P])
        brow = sb("brow", [P, 3 * D])
        bias = sb("bias", [P, 3 * D])
        be = sb("be", [P, DH])
        later = sb("later", [P, 2, D])
        ab = sb("ab", [P, 2])
        xb = sb("xb", [P, GW, D])
        x1b = sb("x1b", [P, GW, D])
        ones = sb("ones", [P, P])
        bn = sb("bn", [P, 2, GW, 6])
        mv = sb("mv", [P, 2, GW, 2])
        veps = sb("veps", [P, 2, GW])
        rstd = sb("rstd", [P, 2, GW])
        half = sb("half", [P, GW])
        dall = sb("dall", [P, COLS], I32)
        dallf = sb("dallf", [P, COLS])
        signs = sb("signs", [P, COLS])
        thr_i = sb("thr_i", [P, NW + 1], I32)
        thr = sb("thr", [P, NW + 1])
        tr = [ps(f"n_tr{i}", [P, D]) for i in range(2)]
        pkv = [ps(f"n_pkv{i}", [P, 2 * D]) for i in range(2)]
        pq = [ps(f"n_pq{i}", [P, D]) for i in range(2)]
        pb = [ps(f"n_pb{i}", [P, 512]) for i in range(2)]

        w_in, dst_in, iota_done, thr_done = sem("w_in"), sem("dst_in"), sem("iota_done"), sem("thr_done")
        ones_done, wide_done, bias_ps, wprep = sem("ones_done"), sem("wide_done"), sem("bias_ps"), sem("wprep")
        half_done, dallf_done, sign_done = sem("half_done"), sem("dallf_done"), sem("sign_done")
        ident_done = sem("ident_done")
        passed = sem("n_passed")
        x_in, xb_out, x1_out, kv_out, q_out = sem("x_in"), sem("xb_out"), sem("x1_out"), sem("kv_out"), sem("q_out")
        res_done = Count(sem("n_res_done"), 2 * GW)
        stored = Count(sem("stored"), 1)
        res_stored = Count(sem("res_stored"), 1)
        bnd = [Count(sem(f"bn_done{i}"), GW) for i in range(2)]
        mvd = [Count(sem(f"mv_done{i}"), GW) for i in range(2)]
        ved = [Count(sem(f"veps_done{i}"), 1) for i in range(2)]
        rsd = [Count(sem(f"rstd_done{i}"), 1) for i in range(2)]
        x1_done = Count(sem("x1_done"), GW)
        xh_done = Count(sem("xh_done"), GW)
        tr_ps = Count(sem("tr_ps"), GW)
        xT_done = Count(sem("xT_done"), GW)
        kv_ps = Count(sem("kv_ps"), GW)
        q_ps = Count(sem("q_ps"), GW)
        kv_done = Count(sem("kv_done"), GW)
        qf_done = Count(sem("qf_done"), GW)
        hi_done = Count(sem("hi_done"), GW)
        rest_done = Count(sem("rest_done"), GW)
        mid_done = Count(sem("mid_done"), GW)
        lo_done = Count(sem("lo_done"), GW)

        xv = t["x"].rearrange("(g i p) d -> p g i d", i=GW, p=P)
        x1v = t["x1b"].rearrange("(g i p) d -> p g i d", i=GW, p=P)
        xbv = t["xb"].rearrange("(g i p) d -> p g i d", i=GW, p=P)
        kvv = t["kv"].rearrange("(g i p) d -> p g i d", i=GW, p=P)
        qv = t["q"].rearrange("(g i p) d -> p g i d", i=GW, p=P)
        block = ctx.enter_context(nc.Block())

        @block.sync
        def _(sp):
            sp.sem_inc(stored.sem, 1)
            sp.sem_inc(res_stored.sem, 1)
            sp.sem_inc(kv_out, 1)
            sp.dma_start(x[:].unsqueeze(1), xv[:, 0:1]).then_inc(x_in, 16)
            for n, name in enumerate(("Wk", "Wv", "Wq")):
                sp.dma_start(wraw[:, :, n * D:(n + 1) * D],
                             t[name].rearrange("(c p) n -> p c n", p=P)).then_inc(w_in, 16)
            for n, name in enumerate(("bk", "bv", "bq")):
                sp.dma_start(brow[:, n * D:(n + 1) * D],
                             t[name].rearrange("(a n) -> a n", a=1).broadcast_to([P, D])).then_inc(w_in, 16)
            sp.dma_start(be[:], t["be"].rearrange("(a n) -> a n", a=1).broadcast_to([P, DH])).then_inc(w_in, 16)
            with nc.allow_non_contiguous_dma(reason="256 numbers, once"):
                sp.dma_start(lng[:], t["ln1_g"].rearrange("(c p) -> p c", p=P)).then_inc(w_in, 16)
                sp.dma_start(lnb[:], t["ln1_b"].rearrange("(c p) -> p c", p=P)).then_inc(w_in, 16)
            for n, (name, by) in enumerate((("bo", "alpha"), ("b2", "beta"))):
                sp.dma_start(later[:, n], t[name].rearrange("(a n) -> a n", a=1).broadcast_to([P, D])
                             ).then_inc(w_in, 16)
                sp.dma_start(ab[:, n:n + 1], t[by].rearrange("(a n) -> a n", a=1).broadcast_to([P, 1])
                             ).then_inc(w_in, 16)
            sp.dma_start(dall[:], t["dst"][1:1 + P * COLS].rearrange("(p c) -> p c", p=P)).then_inc(dst_in, 16)

            def group(g, more):
                for i in range(GW):
                    if i == 0 and more:
                        held(sp, res_done, res_done.at(g, GW), passed)
                        sp.dma_start(x[:].unsqueeze(1), xv[:, bass.ds(g + 1, 1)]).then_inc(x_in, 16)
                    if i == 2:
                        held(sp, res_done, res_done.at(g, 2 * GW), passed)
                        sp.dma_start(xbv[:, bass.ds(g, 1)], xb[:].unsqueeze(1)).then_inc(xb_out, 16)
                        sp.dma_start(x1v[:, bass.ds(g, 1)], x1b[:].unsqueeze(1)).then_inc(x1_out, 16)
                    held(sp, kv_done, kv_done.at(g, i + 1), passed)
                    sp.dma_start(kvv[:, bass.ds(g, 1), i:i + 1], kv[:, i:i + 1].unsqueeze(1)).then_inc(kv_out, 16)
                sp.wait_ge(xb_out, g * 16 + 16)
                sp.wait_ge(x1_out, g * 16 + 16)
                sp.sem_inc(res_stored.sem, 1)
                held(sp, lo_done, lo_done.at(g, GW), passed)
                sp.dma_start(qv[:, bass.ds(g, 1)], qpart[:].rearrange("p i c d -> p i (c d)").unsqueeze(1)
                             ).then_inc(q_out, 16)
                sp.wait_ge(q_out, g * 16 + 16)
                sp.sem_inc(stored.sem, 1)

            with sp.Fori(0, NG - 1) as g:
                group(g, True)
            group(NG - 1, False)
            sp.wait_ge(kv_out, NG * GW * 16 + 1)

        @block.gpsimd
        def _(pool):
            nc.gpsimd.memset(half[:], -0.5).then_inc(half_done, 1)
            nc.gpsimd.iota(thr_i[:], [[P, NW + 1]], base=0, channel_multiplier=0).then_inc(iota_done, 1)
            nc.gpsimd.memset(keep["ident"][:], 0.0).then_inc(ident_done, 1)
            pool.wait_ge(ident_done, 1)
            nc.gpsimd.affine_select(out=keep["ident"][:], in_=keep["ident"][:], compare_op=ALU.not_equal, fill=1.0,
                                    base=0, pattern=[[-1, P]], channel_multiplier=1).then_inc(ident_done, 1)
            for s in (*ved, *rsd, res_done):
                pool.sem_inc(s.sem, 1)
            pool.wait_ge(half_done, 1)
            pool.wait_ge(wprep, KC + 6)
            with pool.Fori(0, NG) as g:
                for n in range(2):
                    held(pool, mvd[n], mvd[n].at(g, GW), passed)
                    nc.gpsimd.tensor_scalar(veps[:, n, :], mv[:, n, :, 1], EPS, None, ALU.add
                                            ).then_inc(ved[n].sem, 1)
                    pool.wait_ge(ved[n].sem, ved[n].at(g, 1))
                    nc.gpsimd.tensor_tensor(rstd[:, n, :], veps[:, n, :], half[:], ALU.pow).then_inc(rsd[n].sem, 1)
                pool.wait_ge(res_stored.sem, res_stored.at(g, 0))
                for i in range(GW):
                    nc.gpsimd.tensor_tensor(xb[:, i], x[:, i], later[:, 1], ALU.add).then_inc(res_done.sem, 1)
                for i in range(GW):
                    nc.gpsimd.tensor_tensor(x1b[:, i], x1[:, i], later[:, 0], ALU.add).then_inc(res_done.sem, 1)

        @block.scalar
        def _(act):
            for s in (xT_done, hi_done, mid_done):
                act.sem_inc(s.sem, 1)
            act.wait_ge(iota_done, 1)
            nc.scalar.activation(thr[:], thr_i[:], ACT.Copy, bias=-0.5).then_inc(thr_done, 1)
            act.wait_ge(thr_done, 1)
            act.wait_ge(dallf_done, 1)
            with act.Fori(0, NG) as g:
                for i in range(GW):
                    act.wait_ge(tr_ps.sem, tr_ps.at(g, i + 1))
                    act.wait_ge(q_ps.sem, q_ps.at(g, 0))
                    nc.scalar.activation(xT[:, i], tr[i % 2][:].rearrange("p (c n) -> p c n", c=KC), ACT.Copy
                                         ).then_inc(xT_done.sem, 1)
                for i in range(GW):
                    act.wait_ge(sign_done, g * GW + i) if i else None
                    nc.scalar.activation(signs[:], dallf[:], ACT.Sign, bias=thr[:, bass.ds(g * GW + i, 1)],
                                         scale=-1.0, accum_out=keep["below"][:, bass.ds(g * GW + i, 1)]
                                         ).then_inc(sign_done, 1)
                for i in range(GW):
                    act.wait_ge(qf_done.sem, qf_done.at(g, i + 1))
                    act.wait_ge(stored.sem, stored.at(g, 0))
                    nc.scalar.activation(qpart[:, i, 0], qf[:, i], ACT.Copy).then_inc(hi_done.sem, 1)
                for i in range(GW):
                    act.wait_ge(rest_done.sem, rest_done.at(g, i + 1))
                    nc.scalar.activation(qpart[:, i, 1], qrest[:, i], ACT.Copy).then_inc(mid_done.sem, 1)
                act.wait_ge(sign_done, g * GW + GW)
            nc.scalar.activation(signs[:], dallf[:], ACT.Sign, bias=thr[:, NW:NW + 1], scale=-1.0,
                                 accum_out=keep["below"][:, NW:NW + 1]).then_inc(sign_done, 1)

        @block.tensor
        def _(pe):
            for s in (tr_ps, kv_ps, q_ps):
                pe.sem_inc(s.sem, 1)
            pe.wait_ge(wide_done, KC)
            pe.wait_ge(w_in, 13 * 16)
            for c in range(KC):
                pe.matmul(pb[0][:, 0:512], lnb_wide[:, c], wraw[:, c, 0:512], start=c == 0, stop=c == KC - 1)
            for c in range(KC):
                last = pe.matmul(pb[1][:, 0:D], lnb_wide[:, c], wraw[:, c, 512:512 + D],
                                 start=c == 0, stop=c == KC - 1)
            last.then_inc(bias_ps, 1)
            pe.wait_ge(ident_done, 2)
            pe.wait_ge(wprep, KC + 6)
            with pe.Fori(0, NG) as g:
                for i in range(GW):
                    pe.wait_ge(xh_done.sem, xh_done.at(g, i + 1))
                    pe.wait_ge(xT_done.sem, xT_done.at(g, max(i - 1, 0)))
                    for c in range(KC):
                        last = pe.transpose(tr[i % 2][:, c * P:(c + 1) * P], xh[:, i, c * P:(c + 1) * P],
                                            keep["ident"][:])
                    last.then_inc(tr_ps.sem, 1)
                for i in range(GW):
                    pe.wait_ge(xT_done.sem, xT_done.at(g, i + 1))
                    pe.wait_ge(kv_done.sem, kv_done.at(g, max(i - 1, 0)))
                    for c in range(KC):
                        last = pe.matmul(pkv[i % 2][:], xT[:, i, c], w[:, c, 0:2 * D], start=c == 0,
                                         stop=c == KC - 1)
                    last.then_inc(kv_ps.sem, 1)
                    pe.wait_ge(qf_done.sem, qf_done.at(g, max(i - 1, 0)))
                    for c in range(KC):
                        last = pe.matmul(pq[i % 2][:], xT[:, i, c], w[:, c, 2 * D:3 * D], start=c == 0,
                                         stop=c == KC - 1)
                    last.then_inc(q_ps.sem, 1)

        @block.vector
        def _(dve):
            for s in (*bnd, *mvd, x1_done, xh_done, kv_done, qf_done, rest_done, lo_done):
                dve.sem_inc(s.sem, 1)
            nc.vector.memset(ones[:], 1.0).then_inc(ones_done, 1)
            dve.wait_ge(ones_done, 1)
            dve.wait_ge(w_in, 13 * 16)
            for c in range(KC):
                nc.vector.tensor_scalar(lnb_wide[:, c], ones[:], lnb[:, c:c + 1], None, ALU.mult
                                        ).then_inc(wide_done, 1)
            nc.vector.tensor_tensor(brow[:, 0:D].rearrange("p (h d) -> p h d", h=H),
                                    brow[:, 0:D].rearrange("p (h d) -> p h d", h=H),
                                    be[:].unsqueeze(1).broadcast_to([P, H, DH]), ALU.add).then_inc(wprep, 1)
            for c in range(KC):
                nc.vector.tensor_scalar(w[:, c], wraw[:, c], lng[:, c:c + 1], None, ALU.mult).then_inc(wprep, 1)
            dve.wait_ge(wprep, 1 + KC)
            dve.wait_ge(bias_ps, 1)
            nc.vector.tensor_tensor(bias[:, 0:512], brow[:, 0:512], pb[0][:], ALU.add).then_inc(wprep, 1)
            nc.vector.tensor_tensor(bias[:, 512:768], brow[:, 512:768], pb[1][:, 0:D], ALU.add).then_inc(wprep, 1)
            dve.wait_ge(dst_in, 16)
            nc.vector.tensor_copy(dallf[:], dall[:]).then_inc(dallf_done, 1)
            for n in range(2):
                nc.vector.tensor_scalar(later[:, n], later[:, n], ab[:, n:n + 1], None, ALU.mult).then_inc(wprep, 1)
            dve.wait_ge(wprep, 5 + KC)
            dve.sem_inc(wprep, 1)
            def measure(g, n, a):
                for i in range(GW):
                    if n == 0:
                        dve.wait_ge(x_in, g * 16 + 16)
                    else:
                        dve.wait_ge(x1_done.sem, x1_done.at(g, i + 1))
                    nc.vector.bn_stats(bn[:, n, i], a[:, i]).then_inc(bnd[n].sem, 1)
                for i in range(GW):
                    held(dve, bnd[n], bnd[n].at(g, i + 1), passed)
                    nc.vector.bn_aggr(mv[:, n, i], bn[:, n, i]).then_inc(mvd[n].sem, 1)

            def normalise(g, n, a, b, done):
                for i in range(GW):
                    dve.wait_ge(rsd[n].sem, rsd[n].at(g, 1))
                    if n == 0:
                        dve.wait_ge(res_done.sem, res_done.at(g, 0))
                    else:
                        dve.wait_ge(tr_ps.sem, tr_ps.at(g, 0))
                    nc.vector.tensor_scalar(b[:, i], a[:, i], mv[:, n, i, 0:1], rstd[:, n, i:i + 1],
                                            ALU.subtract, ALU.mult).then_inc(done.sem, 1)

            def norms(g, place):
                if place == 1:
                    measure(g, 0, x)
                if place == 3:
                    normalise(g, 0, x, x1, x1_done)
                    measure(g, 1, x1)
                if place == 5:
                    normalise(g, 1, x1, xh, xh_done)

            def group(g, more):
                dve.wait_ge(kv_out, g * (GW * 16) + 1)
                dve.sem_inc(passed, 1)
                for i in range(GW):
                    dve.wait_ge(kv_ps.sem, kv_ps.at(g, i + 1))
                    nc.vector.tensor_tensor(kv[:, i], pkv[i % 2][:], bias[:, 0:2 * D], ALU.add
                                            ).then_inc(kv_done.sem, 1)
                    dve.wait_ge(q_ps.sem, q_ps.at(g, i + 1))
                    dve.wait_ge(hi_done.sem, hi_done.at(g, 0))
                    dve.wait_ge(rest_done.sem, rest_done.at(g, 0))
                    nc.vector.tensor_tensor(qf[:, i], pq[i % 2][:], bias[:, 2 * D:], ALU.add
                                            ).then_inc(qf_done.sem, 1)
                    if more:
                        norms(g + 1, i)
                for i in range(GW):
                    dve.wait_ge(hi_done.sem, hi_done.at(g, i + 1))
                    dve.wait_ge(lo_done.sem, lo_done.at(g, 0))
                    nc.vector.tensor_tensor(qrest[:, i], qf[:, i], qpart[:, i, 0], ALU.subtract
                                            ).then_inc(rest_done.sem, 1)
                for i in range(GW):
                    dve.wait_ge(mid_done.sem, mid_done.at(g, i + 1))
                    nc.vector.tensor_tensor(qpart[:, i, 2], qrest[:, i], qpart[:, i, 1], ALU.subtract
                                            ).then_inc(lo_done.sem, 1)

            for place in range(GW):
                norms(0, place)
            with dve.Fori(0, NG - 1) as g:
                group(g, True)
            group(NG - 1, False)


def step_stage(nc, keep):
    with ExitStack() as ctx:
        sb, ps, sem = declare(ctx, nc)
        ones = sb("s_ones", [P, P])
        iota_i = sb("iota_i", [P, P], I32)
        kthr_i = sb("kthr_i", [NW, E // CHUNK + 1], I32)
        kthr = sb("kthr", [NW, E // CHUNK + 1])
        more = sb("more", [NW, E // CHUNK + 1])
        before = sb("before", [NW, NW])
        below = sb("belowc", [P, NW + 1])
        col = sb("col", [NW, 6])
        past = sb("past", [NW, NS])
        rows = sb("rows", [1, 2, NS])
        base_i = sb("base_i", [1, NS], I32)
        base = sb("base", [1, NS])
        fresh = sb("fresh_same", [P, NS - 1])
        pcol = ps("pcol", [NW, 4])
        prow = ps("prow", [1, 2 * NS + 1])
        pwide = ps("pwide", [P, NS])
        made, fixed, sums, done = sem("made"), sem("fixed"), sem("sums"), sem("rows_done")
        block = ctx.enter_context(nc.Block())
        RP, NEXT, CHUNKS, END, SPARE, FIRST = range(6)

        @block.gpsimd
        def _(pool):
            nc.gpsimd.iota(iota_i[:], [[1, P]], base=0, channel_multiplier=0).then_inc(made, 1)
            nc.gpsimd.iota(kthr_i[:], [[CHUNK, E // CHUNK + 1]], base=CHUNK, channel_multiplier=0).then_inc(made, 1)
            nc.gpsimd.iota(base_i[:], [[CHUNK, NS]], base=0, channel_multiplier=0).then_inc(made, 1)
            nc.gpsimd.memset(before[:], 1.0).then_inc(made, 1)
            nc.gpsimd.memset(keep["lastmask"][:], 1.0).then_inc(made, 1)
            pool.wait_ge(made, 5)
            nc.gpsimd.affine_select(out=before[:], in_=before[:], compare_op=ALU.is_gt, fill=0.0, base=0,
                                    pattern=[[1, NW]], channel_multiplier=-1).then_inc(made, 1)
            nc.gpsimd.affine_select(out=keep["lastmask"][:], in_=keep["lastmask"][:], compare_op=ALU.not_equal,
                                    fill=0.0, base=-(P - 1 + T - 1), pattern=[[1, T]], channel_multiplier=1
                                    ).then_inc(made, 1)

        @block.vector
        def _(dve):
            def link(ins):
                link.n += 1
                ins.then_inc(fixed, 1)
                dve.wait_ge(fixed, link.n)
            link.n = 0
            dve.wait_ge(made, 7)
            link(nc.vector.memset(ones[:], 1.0))
            link(nc.vector.tensor_scalar(below[:], keep["below"][:], float(COLS), 0.5, ALU.add, ALU.mult))
            link(nc.vector.tensor_copy(kthr[:], kthr_i[:]))
            link(nc.vector.tensor_copy(keep["iota"][:], iota_i[:]))
            link(nc.vector.tensor_copy(base[:], base_i[:]))
            dve.wait_ge(sums, 1)
            link(nc.vector.tensor_copy(col[:, RP:RP + 2], pcol[:, 0:2]))
            link(nc.vector.tensor_tensor(col[:, SPARE:SPARE + 1], col[:, NEXT:NEXT + 1], col[:, RP:RP + 1],
                                         ALU.subtract))
            link(nc.vector.tensor_scalar(more[:], kthr[:], col[:, SPARE:SPARE + 1], 1.0, ALU.is_lt, ALU.add,
                                         accum_out=col[:, CHUNKS:CHUNKS + 1]))
            dve.sem_inc(done, 1)
            dve.wait_ge(sums, 2)
            link(nc.vector.tensor_tensor(col[:, END:END + 1], pcol[:, 2:3], col[:, CHUNKS:CHUNKS + 1], ALU.add))
            link(nc.vector.scalar_tensor_tensor(out=col[:, FIRST:FIRST + 1], in0=col[:, CHUNKS:CHUNKS + 1],
                                                scalar=-float(CHUNK), in1=col[:, SPARE:SPARE + 1],
                                                op0=ALU.mult, op1=ALU.add))
            link(nc.vector.tensor_scalar(past[:], keep["iota"][0:NW, 0:NS], col[:, END:END + 1], None, ALU.is_ge))
            dve.sem_inc(done, 1)
            dve.wait_ge(sums, 3)
            link(nc.vector.tensor_tensor(rows[:, 0], prow[:, 0:NS], base[:], ALU.add))
            link(nc.vector.tensor_scalar(keep["table"][:, 0:NS], rows[:, 0], float(E), 0.0, ALU.min, ALU.max))
            link(nc.vector.tensor_scalar(keep["table"][:, NS:2 * NS], prow[:, NS:2 * NS], float(NW - 1), None,
                                         ALU.min))
            link(nc.vector.tensor_copy(keep["table"][:, 2 * NS:2 * NS + 1], prow[:, 2 * NS:2 * NS + 1]))
            link(nc.vector.tensor_scalar(keep["wbase"][:], pwide[:], float(NW - 1), float(P), ALU.min, ALU.mult))
            link(nc.vector.memset(keep["lag"][:], 0))
            link(nc.vector.tensor_copy(keep["lag"][:, LAG:NS], keep["table"][:, NS:2 * NS - LAG]))
            link(nc.vector.memset(keep["fresh"][:], -4 * BIG))
            link(nc.vector.tensor_tensor(fresh[:], keep["wbase"][:, 1:NS], keep["wbase"][:, 0:NS - 1], ALU.is_equal))
            link(nc.vector.tensor_scalar(keep["fresh"][:, 2:NS], fresh[:, 0:NS - 2], -1.0, 4 * BIG, ALU.add, ALU.mult))

        @block.tensor
        def _(pe):
            pe.wait_ge(fixed, 2)
            pe.matmul(pcol[:, 0:1], below[:, 0:NW], ones[:, 0:1], start=True, stop=True)
            pe.matmul(pcol[:, 1:2], below[:, 1:NW + 1], ones[:, 0:1], start=True, stop=True).then_inc(sums, 1)
            pe.wait_ge(done, 1)
            pe.wait_ge(fixed, 8)
            pe.matmul(pcol[:, 2:3], before[:], col[:, CHUNKS:CHUNKS + 1], start=True, stop=True).then_inc(sums, 1)
            pe.wait_ge(done, 2)
            pe.wait_ge(fixed, 11)
            pe.matmul(prow[:, 0:NS], col[:, FIRST:FIRST + 1], past[:], start=True, stop=True)
            pe.matmul(prow[:, NS:2 * NS], ones[0:NW, 0:1], past[:], start=True, stop=True)
            pe.matmul(prow[:, 2 * NS:2 * NS + 1], col[:, CHUNKS:CHUNKS + 1], ones[0:NW, 0:1], start=True, stop=True)
            pe.matmul(pwide[:], ones[0:NW, :], past[:], start=True, stop=True).then_inc(sums, 1)


def edge_stage(nc, t, keep):
    with ExitStack() as ctx:
        sb, ps, sem = declare(ctx, nc)
        ident, iota = keep["ident"], keep["iota"]
        src = [sb(f"src{i}", [P, T], I32) for i in range(2)]
        cur = [sb(f"cur{i}", [P, T], I32) for i in range(2)]
        nxt = [sb(f"nxt{i}", [P, T], I32) for i in range(2)]
        ew = [sb(f"ew{i}", [P, T]) for i in range(2)]
        ef = [sb(f"ef{i}", [P, T * ED]) for i in range(2)]
        qw = [sb(f"qw{i}", [P, 3, D], BF16) for i in range(2)]
        kv = [sb(f"kvg{i}", [P, T, 2 * D]) for i in range(2)]
        we2 = sb("we2", [P, 2 * DH])
        same = sb("same", [P, T])
        inside = sb("inside", [P, T])
        single = sb("single", [P, 1])
        pen = sb("pen", [P, T])
        pen1 = sb("pen1", [P, 1])
        local = sb("local", [P, T])
        last = [sb(f"last{i}", [P, T]) for i in range(2)]
        ews = [sb(f"ews{i}", [P, T]) for i in range(2)]
        hot = [sb(f"hot{i}", [P, T, P], BF16) for i in range(2)]
        hot32 = sb("hot32", [P, T, P])
        identh = sb("identh", [P, P], BF16)
        hotT = [sb(f"hotT{i}", [P, 2 * P], BF16) for i in range(2)]
        efT = [sb(f"efT{i}", [P, P]) for i in range(2)]
        ke = [sb(f"ke{i}", [P, 2, H, DH]) for i in range(2)]
        pr = [sb(f"pr{i}", [P, 2, H, DH]) for i in range(2)]
        score = [sb(f"score{i}", [P, H, SEG]) for i in range(2)]
        penH = [sb(f"penH{i}", [P, SCAN + 1]) for i in range(2)]
        penZ = sb("penZ", [P, 2, H])
        penS = [sb(f"penS{i}", [H, 2 * P + 1]) for i in range(2)]
        fwd = sb("fwd", [P, SCAN])
        segmax = sb("segmax", [P, SCAN])
        fwd2 = sb("fwd2", [P, SCAN])
        mx = sb("mx", [P, SCAN])
        across = sb("across", [H, 2 * P])
        across2 = sb("across2", [H, 2 * P])
        diff = sb("diff", [P, H, T])
        wv = sb("wv", [P, T, RW])
        absent = sb("absent", [P, 1])
        part = sb("part", [P, 3, H])
        shift = sb("shift", [P, 2, H])
        factor = sb("factor", [P, 2, H])
        scaled = sb("scaled", [P, AW])
        sums = sb("sums", [P, AW])
        top = sb("top", [P, H])
        wo, wf = sb("wo", [P, KC, D]), sb("wf", [P, KC, D])
        w1, w2 = sb("w1", [P, KC, FF]), sb("w2", [P, FC, D])
        bf = sb("bf", [1, D])
        ones = sb("e_ones", [1, P])
        zeros = sb("e_zeros", [1, RW])
        oab = sb("oab", [P, 2])
        lng, lnb, b1 = sb("o_lng", [P, KC]), sb("o_lnb", [P, KC]), sb("b1", [P, FC])
        xb, x1b = sb("o_xb", [P, D]), sb("o_x1b", [P, D])
        inv = sb("inv", [P, H])
        att = sb("att", [P, D])
        attT = sb("attT", [P, KC, P])
        res = sb("res", [P, 2, D])
        xr = sb("xr", [P, D])
        norm = sb("norm", [P, 2, D])
        normT = sb("normT", [P, 2, KC, P])
        hT = sb("hT", [P, FC, P])
        out = sb("o_out", [P, D])
        bn, mv = sb("o_bn", [P, 2, 6]), sb("o_mv", [P, 2, 2])
        veps, rstd, half = sb("o_veps", [P, 2]), sb("o_rstd", [P, 2]), sb("o_half", [P, 2])

        tr = [ps(f"e_tr{i}", [P, 2 * P + 2 * DH]) for i in range(2)]
        trf = [a[:, 0:P] for a in tr]
        trh = [a[:, P:2 * P].bitcast(BF16) for a in tr]
        qb = [ps(f"e_qb{i}", [P, 2 * D]) for i in range(2)]
        ep = [a[:, 2 * P:2 * P + 2 * DH] for a in tr]
        mm = [ps(f"e_mm{i}", [P, 2, D]) for i in range(2)]
        agg = ps("e_agg", [P, RW])
        turns = ps("e_turns", [P, 4 * P])
        seq = turns[0:H, :].rearrange("h (a n) -> h a n", a=2)
        back = turns[:, 2 * P:2 * P + 2 * H]

        src_in = [sem(f"src_in{i}") for i in range(2)]
        edge_in = [sem(f"edge_in{i}") for i in range(2)]
        q_in = [sem(f"q_in{i}") for i in range(2)]
        kv_in = [[sem(f"kv_in{i}_{j}") for j in range(PAIRS)] for i in range(2)]
        we_in, we_zero, setup = sem("we_in"), sem("we_zero"), sem("setup")
        passed = sem("e_passed")
        SETUP = 14
        OWPREP = 2 * KC + FC + 1
        AHEAD = 2
        geo = Count(sem("geo"), 8)
        last_done = Count(sem("last_done"), 1)
        hot_done = Count(sem("hot_done"), 1)
        hot32_done = Count(sem("hot32_done"), 3)
        penH_done = Count(sem("penH_done"), 2)
        penS_ps = Count(sem("penS_ps"), 1)
        penS_done = Count(sem("penS_done"), 1)
        tr_ps2 = Count(sem("tr_ps2"), PAIRS)
        trcopy = Count(sem("trcopy"), 2 * PAIRS)
        ep_ps = Count(sem("ep_ps"), PAIRS)
        qb_ps = Count(sem("qb_ps"), PAIRS, 1 + PAIRS)
        ke_done = Count(sem("ke_done"), PAIRS, 1 + PAIRS)
        pr_done = Count(sem("pr_done"), PAIRS)
        red_done = Count(sem("red_done"), PAIRS, 1 + AHEAD * PAIRS)
        max_done = Count(sem("max_done"), 10)
        seq_ps = Count(sem("seq_ps"), 1)
        back_ps = Count(sem("back_ps"), 1)
        diff_done = Count(sem("diff_done"), 1)
        tail_done = Count(sem("tail_done"), 2)
        exp_done = Count(sem("exp_done"), 1)
        wv_done = Count(sem("wv_done"), PAIRS, 1 + AHEAD * PAIRS)
        agg_done = Count(sem("agg_done"), 1)
        merge = Count(sem("merge"), 9)
        factor_done = Count(sem("factor_done"), 1)
        ow_in, owprep, b1_ps, half_done = sem("ow_in"), sem("owprep"), sem("b1_ps"), sem("o_half_done")
        x_in, out_dma = sem("o_x_in"), sem("out_dma")
        out_free = Count(sem("out_free"), 1)
        inv_done = Count(sem("inv_done"), 2)
        att_done = Count(sem("att_done"), 1)
        w2_ps = Count(sem("w2_ps"), 1)
        attT_ps = Count(sem("attT_ps"), 1)
        attT_done = Count(sem("attT_done"), 1)
        wo_ps = Count(sem("wo_ps"), 1)
        res_done = Count(sem("res_done"), 2)
        bn_done = Count(sem("o_bn_done"), 2)
        mv_done = Count(sem("o_mv_done"), 2)
        veps_done = Count(sem("o_veps_done"), 1)
        rstd_done = Count(sem("o_rstd_done"), 1)
        xr_done = Count(sem("xr_done"), 1)
        norm_done = Count(sem("norm_done"), 2)
        normT_ps = Count(sem("normT_ps"), 1)
        normT_done = Count(sem("normT_done"), 1)
        wf_ps = Count(sem("wf_ps"), 1)
        out_done = Count(sem("out_done"), 1)
        h_ps = Count(sem("h_ps"), 2)
        gelu_done = Count(sem("gelu_done"), 2)

        def steps(eng, body):
            body(0, 0, 0, None)
            with eng.Fori(0, NW // 2) as u:
                body(u * 2 + 1, 1, u, u * 2)
                body(u * 2 + 2, 0, u + 1, u * 2 + 1)
            n = eng.value_load(keep["table"][0:1, 2 * NS:2 * NS + 1], min_val=NW, max_val=NS - 2 * LAG - 2)
            with eng.If(n > NW):
                with eng.Fori(NW // 2, n // 2) as u:
                    body(u * 2 + 1, 1, u, u * 2)
                    body(u * 2 + 2, 0, u + 1, u * 2 + 1)
            return n // 2 * 2

        block = ctx.enter_context(nc.Block())

        @block.sync
        def _(sp):
            sp.wait_ge(we_zero, 1)
            sp.dma_start(we2[0:ED, 0:DH], t["We"]).then_inc(we_in, 16)
            sp.dma_start(we2[ED:2 * ED, DH:2 * DH], t["We"]).then_inc(we_in, 16)

            sp.dma_start(bf[:], t["bf"].rearrange("(a n) -> a n", a=1)).then_inc(ow_in, 16)
            for name, dst in (("Wo", wo), ("WfT", wf), ("W1", w1), ("W2", w2)):
                sp.dma_start(dst[:], t[name].rearrange("(c p) n -> p c n", p=P)).then_inc(ow_in, 16)
            for n, name in enumerate(("alpha", "beta")):
                sp.dma_start(oab[:, n:n + 1], t[name].rearrange("(a n) -> a n", a=1).broadcast_to([P, 1])
                             ).then_inc(ow_in, 16)
            with nc.allow_non_contiguous_dma(reason="short vectors, once"):
                for name, dst in (("ln2_g", lng), ("ln2_b", lnb), ("b1", b1)):
                    sp.dma_start(dst[:], t[name].rearrange("(c p) -> p c", p=P)).then_inc(ow_in, 16)

            def load(s, b):
                e0 = sp.value_load(keep["table"][0:1, bass.ds(s, 1)], min_val=0, max_val=E)
                w = sp.value_load(keep["table"][0:1, bass.ds(s + NS, 1)], min_val=0, max_val=NW - 1)
                held(sp, ke_done, ke_done.at(s, 0) - PAIRS, passed)
                held(sp, qb_ps, qb_ps.at(s, 0) - PAIRS, passed)
                sp.dma_start(src[b][:], t["src"][bass.ds(e0, CHUNK)].rearrange("(p t) -> p t", t=T)
                             ).then_inc(src_in[b], 16)
                sp.dma_start(cur[b][:], t["dst"][bass.ds(e0 + 1, CHUNK)].rearrange("(p t) -> p t", t=T)
                             ).then_inc(edge_in[b], 16)
                sp.dma_start(nxt[b][:], t["dst"][bass.ds(e0 + 2, CHUNK)].rearrange("(p t) -> p t", t=T)
                             ).then_inc(edge_in[b], 16)
                sp.dma_start(ew[b][:], t["ew"][bass.ds(e0, CHUNK)].rearrange("(p t) -> p t", t=T)
                             ).then_inc(edge_in[b], 16)
                sp.dma_start(ef[b][:], t["ef"][bass.ds(e0, CHUNK), :].rearrange("(p t) n -> p (t n)", t=T)
                             ).then_inc(edge_in[b], 16)
                sp.dma_start(qw[b][:].rearrange("p c d -> p (c d)"), t["q"][bass.ds(w * P, P), :]
                             ).then_inc(q_in[b], 16)

            def layers(y):
                wa = sp.value_load(keep["lag"][0:1, bass.ds(y + 2, 1)], min_val=0, max_val=NW - 1)
                wc = sp.value_load(keep["lag"][0:1, bass.ds(y, 1)], min_val=0, max_val=NW - 1)
                sp.wait_ge(out_dma, y * 16 + 1)
                sp.sem_inc(out_free.sem, 1)
                held(sp, xr_done, xr_done.at(y, 0), passed)
                sp.dma_start(x1b[:], t["x1b"][bass.ds(wa * P, P), :]).then_inc(x_in, 16)
                sp.dma_start(xb[:], t["xb"][bass.ds(wa * P, P), :]).then_inc(x_in, 16)
                held(sp, out_done, out_done.at(y, 1), passed)
                sp.dma_start(t["out"][bass.ds(wc * P, P), :], out[:]).then_inc(out_dma, 16)

            sp.sem_inc(out_dma, 1)

            def body(s, b, k, x):
                load(s + 1, 1 - b)
                if x is not None:
                    layers(x)

            load(0, 0)
            final = steps(sp, body)
            for y in range(LAG + 1):
                layers(final + y)
            sp.wait_ge(x_in, (final + LAG) * 32 + 32)
            sp.sem_inc(passed, 1)
            sp.wait_ge(out_dma, (final + LAG + 1) * 16 + 1)
            sp.sem_inc(passed, 1)
            for s, inc in ((src_in[1], 16), (edge_in[1], 64), (q_in[1], 16)):
                sp.wait_ge(s, final // 2 * inc + inc)
                sp.sem_inc(passed, 1)

        @block.gpsimd
        def _(pool):
            for s in (hot_done, veps_done, rstd_done, xr_done):
                pool.sem_inc(s.sem, 1)
            nc.gpsimd.memset(half[:], -0.5).then_inc(half_done, 1)
            pool.wait_ge(half_done, 1)
            pool.wait_ge(setup, SETUP)
            pool.wait_ge(ow_in, 10 * 16)

            def one_hots(s, b, first=False):
                pool.wait_ge(geo.sem, geo.at(s, 2))
                held(pool, hot32_done, hot32_done.at(s - 1, 0) if not first else 1, passed)
                for i in range(T):
                    m = nc.gpsimd.tensor_scalar(hot[b][:, i], iota[:], local[:, i:i + 1], None, ALU.is_equal)
                m.then_inc(hot_done.sem, 1)

            def layers(y):
                held(pool, mv_done, mv_done.at(y, 2), passed)
                nc.gpsimd.tensor_scalar(veps[:], mv[:, :, 1], EPS, None, ALU.add).then_inc(veps_done.sem, 1)
                pool.wait_ge(veps_done.sem, veps_done.at(y, 1))
                nc.gpsimd.tensor_tensor(rstd[:], veps[:], half[:], ALU.pow).then_inc(rstd_done.sem, 1)

            def block_residual(y):
                pool.wait_ge(x_in, y * 32 + 32)
                nc.gpsimd.tensor_tensor(xr[:], xb[:], res[:, 0], ALU.add).then_inc(xr_done.sem, 1)

            def body(s, b, k, x):
                pool.wait_ge(src_in[b], k * 16 + 16)
                for j in range(PAIRS):
                    held(pool, wv_done, wv_done.at(s, j + 1) - AHEAD * PAIRS, passed)
                    for i in (2 * j, 2 * j + 1):
                        pool.indirect_dma_start(kv[b][:, i, :], None, t["kv"][:, :],
                                                bass.IndirectOffsetOnAxis(ap=src[b][:, i:i + 1].bitcast(U32), axis=0)
                                                ).then_inc(kv_in[b][j], 16)
                one_hots(s + 1, 1 - b)
                if x is not None:
                    layers(x)
                    block_residual(x)

            one_hots(0, 0, first=True)
            final = steps(pool, body)
            for y in range(LAG):
                layers(final + y)
                block_residual(final + y)

        @block.tensor
        def _(pe):
            for s in (penS_ps, tr_ps2, ep_ps, qb_ps, seq_ps, back_ps,
                      w2_ps, attT_ps, wo_ps, normT_ps, h_ps):
                pe.sem_inc(s.sem, s.primer)
            pe.wait_ge(we_in, 32)
            pe.wait_ge(ow_in, 10 * 16)
            for f in range(FC):
                for c in range(KC):
                    m = pe.matmul(mm[0][:, 0, f:f + 1], w1[:, c, f * P:(f + 1) * P], lnb[:, c:c + 1],
                                  start=c == 0, stop=c == KC - 1)
            m.then_inc(b1_ps, 1)
            pe.wait_ge(owprep, OWPREP)
            pe.wait_ge(setup, SETUP)
            pe.matmul(agg[:], ones[:], zeros[:], start=True, stop=True).then_inc(agg_done.sem, agg_done.primer)
            pe.matmul(mm[1][:, 0], ones[:], zeros[:, 0:D], start=True, stop=True
                      ).then_inc(wf_ps.sem, wf_ps.primer)

            def turn(s, b, j):
                pe.wait_ge(trcopy.sem, trcopy.at(s, 2 * max(j - 1, 0)))
                pe.wait_ge(ke_done.sem, ke_done.at(s, max(j - 1, 0)))
                for i in range(2):
                    pe.transpose(trh[j % 2][:, i * P:(i + 1) * P], hot[b][:, 2 * j + i], identh[:])
                pe.transpose(trf[j % 2][:], ef[b][:, j * P:(j + 1) * P], ident[:]).then_inc(tr_ps2.sem, 1)

            def spread(s, b, j):
                pe.wait_ge(trcopy.sem, trcopy.at(s, 2 * j + 2))
                pe.matmul(ep[j % 2], efT[j % 2][:], we2[:], start=True, stop=True).then_inc(ep_ps.sem, 1)
                pe.wait_ge(pr_done.sem, pr_done.at(s, max(j - 1, 0)))
                for i in range(2):
                    for c in range(3):
                        m = pe.matmul(qb[j % 2][:, i * D:(i + 1) * D], hotT[j % 2][:, i * P:(i + 1) * P],
                                      qw[b][:, c, :], start=c == 0, stop=c == 2)
                m.then_inc(qb_ps.sem, 1)

            def penalty_rows(s, x):
                pe.wait_ge(penH_done.sem, penH_done.at(s, 2))
                if x is not None:
                    pe.wait_ge(max_done.sem, max_done.at(x, 7))
                for i in range(2):
                    m = pe.transpose(seq[:, 1, i:2 * P:2], penZ[:, i, :], ident[:])
                m.then_inc(penS_ps.sem, 1)

            def max_rows(x):
                pe.wait_ge(penS_done.sem, penS_done.at(x, 1))
                pe.wait_ge(max_done.sem, max_done.at(x, 3))
                sm = segmax[:].rearrange("p (h t) -> p h t", h=H)
                for i, c in enumerate((0, T - 1)):
                    m = pe.transpose(seq[:, 0, i:2 * P:2], sm[:, :, c], ident[:])
                m.then_inc(seq_ps.sem, 1)

            def max_cols(x):
                held(pe, max_done, max_done.at(x, 5), passed)
                for i in range(2):
                    m = pe.transpose(back[:, i * H:(i + 1) * H], across2[:, i:2 * P:2], ident[0:H, 0:H])
                m.then_inc(back_ps.sem, 1)

            def node_sums(x, j):
                if j == 0:
                    pe.wait_ge(merge.sem, merge.at(x, 9))
                    pe.wait_ge(tail_done.sem, tail_done.at(x, 2))
                    pe.wait_ge(hot32_done.sem, hot32_done.at(x, 3))
                pe.wait_ge(wv_done.sem, wv_done.at(x, j + 1))
                for i in (2 * j, 2 * j + 1):
                    m = pe.matmul(agg[:], hot32[:, i], wv[:, i], start=i == 0, stop=i == T - 1)
                if j == PAIRS - 1:
                    m.then_inc(agg_done.sem, 1)

            def block_out(y, units):
                pe.wait_ge(gelu_done.sem, gelu_done.at(y, 1 + units[0] // (FC // 2)))
                pe.wait_ge(res_done.sem, res_done.at(y, 1))
                for f in units:
                    m = pe.matmul(mm[1][:, 0], hT[:, f], w2[:, f], start=f == 0, stop=f == FC - 1)
                if units[-1] == FC - 1:
                    m.then_inc(w2_ps.sem, 1)

            def attention_turn(y):
                pe.wait_ge(out_done.sem, out_done.at(y, 1))
                pe.wait_ge(att_done.sem, att_done.at(y, 1))
                for c in range(KC):
                    m = pe.transpose(mm[1][:, 0, c * P:(c + 1) * P], att[:, c * P:(c + 1) * P], ident[:])
                m.then_inc(attT_ps.sem, 1)

            def attention_out(y):
                pe.wait_ge(attT_done.sem, attT_done.at(y, 1))
                for c in range(KC):
                    m = pe.matmul(mm[1][:, 1], attT[:, c], wo[:, c], start=c == 0, stop=c == KC - 1)
                m.then_inc(wo_ps.sem, 1)

            def norms_turn(y):
                pe.wait_ge(norm_done.sem, norm_done.at(y, 2))
                for n in range(2):
                    for c in range(KC):
                        m = pe.transpose(mm[0][:, n, c * P:(c + 1) * P], norm[:, n, c * P:(c + 1) * P], ident[:])
                m.then_inc(normT_ps.sem, 1)

            def last_layer(y):
                pe.wait_ge(normT_done.sem, normT_done.at(y, 1))
                for c in range(KC):
                    pe.matmul(mm[1][:, 0], normT[:, 1, c], wf[:, c], start=c == 0, stop=False)
                pe.matmul(mm[1][:, 0], ones[:], bf[:], start=False, stop=True).then_inc(wf_ps.sem, 1)

            def hidden(y, units):
                half = FC // 2
                if units[0] == 0:
                    pe.wait_ge(normT_done.sem, normT_done.at(y, 0))
                if units[0] == half:
                    pe.wait_ge(gelu_done.sem, gelu_done.at(y, 1))
                bank = mm[0][:].rearrange("p a n -> p (a n)")
                for f in units:
                    i = f % half
                    for c in range(KC):
                        m = pe.matmul(bank[:, i * P:(i + 1) * P], w1[:, c, f * P:(f + 1) * P], normT[:, 0, c],
                                      start=c == 0, stop=c == KC - 1)
                if units[-1] % half == half - 1:
                    m.then_inc(h_ps.sem, 1)

            def layers(y, place):
                if place == 0:
                    hidden(y, range(0, 2))
                if place == 1:
                    hidden(y, range(2, 4))
                if place == 2:
                    attention_turn(y)
                if place == 3:
                    attention_out(y)
                    hidden(y, range(4, 6))
                if place == 4:
                    hidden(y, range(6, 8))
                if place == 5:
                    block_out(y, range(0, 4))
                if place == 6:
                    block_out(y, range(4, 8))
                if place == 9:
                    norms_turn(y)
                if place == 10:
                    last_layer(y)

            def first_turn(s, b, k):
                pe.wait_ge(edge_in[b], k * 64 + 64)
                pe.wait_ge(hot_done.sem, hot_done.at(s, 1))
                turn(s, b, 0)

            def first_spread(s, b, k):
                pe.wait_ge(q_in[b], k * 16 + 16)
                spread(s, b, 0)

            def body(s, b, k, x):
                for j in range(PAIRS):
                    if j + 1 < PAIRS:
                        turn(s, b, j + 1)
                    if j:
                        spread(s, b, j)
                    if j == 5:
                        penalty_rows(s, x)
                    if x is not None:
                        if j == 1:
                            max_rows(x)
                        if j == 3:
                            max_cols(x)
                        layers(x, j)
                        for i in SUMS.get(j, ()):
                            node_sums(x, i)
                after = k if b == 0 else k + 1
                first_turn(s + 1, 1 - b, after)
                if x is not None:
                    for i in SUMS[PAIRS]:
                        node_sums(x, i)
                        if i == NORMS:
                            layers(x, PAIRS)
                first_spread(s + 1, 1 - b, after)
                if x is not None:
                    layers(x, PAIRS + 1)

            SUMS = {7: (0, 1), 8: (2, 3), 9: (4, 5, 6, 7, 8)}
            NORMS = 5
            first_turn(0, 0, 0)
            first_spread(0, 0, 0)
            final = steps(pe, body)
            for j in range(PAIRS):
                if j == 1:
                    max_rows(final)
                if j == 3:
                    max_cols(final)
                layers(final, j)
            for j in range(PAIRS):
                node_sums(final, j)
            for j in (PAIRS, PAIRS + 1):
                layers(final, j)
            for y in range(1, LAG):
                for j in range(PAIRS + 2):
                    layers(final + y, j)

        @block.scalar
        def _(act):
            for s in (penH_done, penS_done, trcopy, exp_done, factor_done, hot32_done,
                      attT_done, normT_done, gelu_done):
                act.sem_inc(s.sem, 1)
            act.wait_ge(setup, SETUP)
            act.wait_ge(owprep, OWPREP)

            def attention_copy(y):
                act.wait_ge(attT_ps.sem, attT_ps.at(y, 1))
                nc.scalar.activation(attT[:], mm[1][:, 0].rearrange("p (c n) -> p c n", c=KC), ACT.Copy
                                     ).then_inc(attT_done.sem, 1)

            def norms_copy(y):
                act.wait_ge(normT_ps.sem, normT_ps.at(y, 1))
                nc.scalar.activation(normT[:], mm[0][:].rearrange("p a (c n) -> p a c n", c=KC), ACT.Copy
                                     ).then_inc(normT_done.sem, 1)

            def gelu(y, part):
                act.wait_ge(h_ps.sem, h_ps.at(y, part + 1))
                bank = mm[0][:].rearrange("p a n -> p (a n)")
                for i in range(FC // 2):
                    f = part * FC // 2 + i
                    m = nc.scalar.activation(hT[:, f], bank[:, i * P:(i + 1) * P], ACT.Gelu, bias=b1[:, f:f + 1])
                m.then_inc(gelu_done.sem, 1)

            def penalties(s, b):
                ph = penH[b][:, 0:SCAN].rearrange("p (h t) -> p h t", h=H)
                act.wait_ge(geo.sem, geo.at(s, 8))
                nc.scalar.activation(ph[:, :, 1:T], pen[:, 0:T - 1].unsqueeze(1).broadcast_to([P, H, T - 1]),
                                     ACT.Copy).then_inc(penH_done.sem, 1)
                nc.scalar.activation(penZ[:, 0, :], pen1[:].broadcast_to([P, H]), ACT.Copy)
                nc.scalar.activation(penZ[:, 1, :], pen[:, T - 1:T].broadcast_to([P, H]), ACT.Copy
                                     ).then_inc(penH_done.sem, 1)

            def copies(s, j):
                act.wait_ge(tr_ps2.sem, tr_ps2.at(s, j + 1))
                act.wait_ge(qb_ps.sem, qb_ps.at(s, max(j - 1, 0)))
                nc.scalar.activation(efT[j % 2][:], trf[j % 2][:], ACT.Copy).then_inc(trcopy.sem, 1)
                nc.scalar.activation(hotT[j % 2][:], trh[j % 2][:], ACT.Copy).then_inc(trcopy.sem, 1)

            def widen(x, xb, n):
                tiles = slice(n * T // 3, (n + 1) * T // 3)
                act.wait_ge(agg_done.sem, agg_done.at(x, 0))
                nc.scalar.activation(hot32[:, tiles], hot[xb][:, tiles], ACT.Copy).then_inc(hot32_done.sem, 1)

            def exponent(x):
                act.wait_ge(diff_done.sem, diff_done.at(x, 1))
                act.wait_ge(agg_done.sem, agg_done.at(x, 0))
                wh = wv[:, :, 0:AW].rearrange("p t (h d) -> p h t d", h=H)
                nc.scalar.activation(wh[:, :, :, DH], diff[:], ACT.Exp).then_inc(exp_done.sem, 1)

            def factors(x):
                act.wait_ge(merge.sem, merge.at(x, 5))
                nc.scalar.activation(factor[:], shift[:], ACT.Exp).then_inc(factor_done.sem, 1)

            def body(s, b, k, x):
                penalties(s, b)
                for j in range(PAIRS):
                    if j:
                        copies(s, j)
                    if j == 7:
                        act.wait_ge(penS_ps.sem, penS_ps.at(s, 1))
                        nc.scalar.activation(penS[b][:, 1:2 * P + 1], seq[:, 1, :], ACT.Copy
                                             ).then_inc(penS_done.sem, 1)
                    if x is not None:
                        if j == 1:
                            factors(x)
                        if j == 2:
                            gelu(x, 0)
                        if j == 3:
                            attention_copy(x)
                        if j == 5:
                            gelu(x, 1)
                        if j in WIDEN:
                            widen(x, 1 - b, WIDEN.index(j))
                        if j == 6:
                            exponent(x)
                copies(s + 1, 0)
                if x is not None:
                    norms_copy(x)

            WIDEN = (0, 1, 2)
            copies(0, 0)
            final = steps(act, body)
            for y in range(LAG):
                if y < 2:
                    factors(final + y)
                gelu(final + y, 0)
                attention_copy(final + y)
                gelu(final + y, 1)
                if y == 0:
                    for n in range(3):
                        widen(final, 0, n)
                    exponent(final)
                norms_copy(final + y)

        @block.vector
        def _(dve):
            nc.vector.memset(we2[:], 0.0).then_inc(we_zero, 1)
            for s in (inv_done, last_done, att_done, res_done, bn_done, mv_done, norm_done, out_done):
                dve.sem_inc(s.sem, 1)
            for s in (geo, ke_done, pr_done, max_done, diff_done, tail_done, merge):
                dve.sem_inc(s.sem, s.primer)
            dve.sem_inc(red_done.sem, red_done.primer)
            dve.sem_inc(wv_done.sem, wv_done.primer)
            nc.vector.memset(ones[:], 1.0).then_inc(setup, 1)
            nc.vector.memset(zeros[:], 0.0).then_inc(setup, 1)
            for a in (sums, res, xr, normT):
                nc.vector.memset(a[:], 0.0).then_inc(setup, 1)
            nc.vector.memset(top[:], -BIG).then_inc(setup, 1)
            for i in range(2):
                nc.vector.memset(score[i][:], 0.0).then_inc(setup, 1)
                nc.vector.memset(penH[i][:], -BIG).then_inc(setup, 1)
                nc.vector.memset(penS[i][:], -BIG).then_inc(setup, 1)
            nc.vector.tensor_copy(identh[:], ident[:]).then_inc(setup, 1)
            dve.wait_ge(setup, SETUP)
            dve.wait_ge(ow_in, 10 * 16)
            for c in range(KC):
                nc.vector.tensor_scalar(wo[:, c], wo[:, c], oab[:, 0:1], None, ALU.mult).then_inc(owprep, 1)
            for f in range(FC):
                nc.vector.tensor_scalar(w2[:, f], w2[:, f], oab[:, 1:2], None, ALU.mult).then_inc(owprep, 1)
            dve.wait_ge(b1_ps, 1)
            nc.vector.tensor_tensor(b1[:], b1[:], mm[0][:, 0, 0:FC], ALU.add).then_inc(owprep, 1)
            for c in range(KC):
                nc.vector.tensor_scalar(w1[:, c], w1[:, c], lng[:, c:c + 1], None, ALU.mult).then_inc(owprep, 1)

            def positions(s, b, k):
                dve.wait_ge(edge_in[b], k * 64 + 64)
                dve.wait_ge(penH_done.sem, penH_done.at(s, 0))
                dve.wait_ge(hot_done.sem, hot_done.at(s, 0))
                nc.vector.tensor_tensor(same[:], cur[b][:], nxt[b][:], ALU.is_equal).then_inc(geo.sem, 1)
                nc.vector.tensor_scalar(local[:], cur[b][:], keep["wbase"][:, bass.ds(s, 1)], None, ALU.subtract
                                        ).then_inc(geo.sem, 1)
                nc.vector.tensor_tensor(single[:], cur[b][:, 0:1], cur[b][:, T - 1:T], ALU.is_equal
                                        ).then_inc(geo.sem, 1)
                nc.vector.tensor_scalar(ews[b][:], ew[b][:], SCALE, None, ALU.mult).then_inc(geo.sem, 1)
                dve.wait_ge(geo.sem, geo.at(s, 1))
                nc.vector.tensor_tensor(inside[:], same[:], keep["lastmask"][:], ALU.mult).then_inc(geo.sem, 1)
                dve.wait_ge(geo.sem, geo.at(s, 5))
                nc.vector.tensor_scalar(pen[:], inside[:], -1.0, BIG, ALU.add, ALU.mult).then_inc(geo.sem, 1)
                nc.vector.tensor_scalar(pen1[:], single[:], -1.0, BIG, ALU.add, ALU.mult).then_inc(geo.sem, 1)
                dve.wait_ge(geo.sem, geo.at(s, 7))
                dve.sem_inc(geo.sem, 1)

            def last_edges(s, b):
                dve.wait_ge(geo.sem, geo.at(s, 8))
                nc.vector.tensor_scalar(last[b][:], inside[:], -1.0, 1.0, ALU.mult, ALU.add
                                        ).then_inc(last_done.sem, 1)

            def key(s, b, k, j):
                dve.wait_ge(kv_in[b][j], k * 32 + 32)
                dve.wait_ge(ep_ps.sem, ep_ps.at(s, j + 1))
                dve.wait_ge(pr_done.sem, pr_done.at(s, max(j - 1, 0)))
                nc.vector.tensor_tensor(
                    ke[j % 2][:], kv[b][:, 2 * j:2 * j + 2, 0:D].rearrange("p t (h d) -> p t h d", h=H),
                    ep[j % 2].rearrange("p (t d) -> p t d", t=2).unsqueeze(2).broadcast_to([P, 2, H, DH]),
                    ALU.add).then_inc(ke_done.sem, 1)

            def product(s, j):
                dve.wait_ge(ke_done.sem, ke_done.at(s, j + 1))
                dve.wait_ge(qb_ps.sem, qb_ps.at(s, j + 1))
                dve.wait_ge(red_done.sem, red_done.at(s, max(j - 1, 0)))
                nc.vector.tensor_tensor(pr[j % 2][:], ke[j % 2][:],
                                        qb[j % 2][:].rearrange("p (t h d) -> p t h d", t=2, h=H), ALU.mult
                                        ).then_inc(pr_done.sem, 1)

            def reduce(s, b, j):
                dve.wait_ge(pr_done.sem, pr_done.at(s, j + 1))
                nc.vector.tensor_reduce(score[b][:, :, 2 * j:2 * j + 2].rearrange("p h t -> p t h"),
                                        pr[j % 2][:], AX.X, ALU.add).then_inc(red_done.sem, 1)

            def scale_scores(x, xb):
                dve.wait_ge(red_done.sem, red_done.at(x, PAIRS))
                nc.vector.tensor_tensor(score[xb][:, :, 0:T], score[xb][:, :, 0:T],
                                        ews[xb][:].unsqueeze(1).broadcast_to([P, H, T]), ALU.mult
                                        ).then_inc(max_done.sem, 1)

            def scan(x, n, out, pens, values, forward):
                dve.wait_ge(max_done.sem, max_done.at(x, n - 1))
                size = out.shape[1]
                if forward:
                    m = nc.vector.tensor_tensor_scan(out[:], pens[:, 0:size], values, -BIG, ALU.add, ALU.max)
                else:
                    m = nc.vector.tensor_tensor_scan(out[:, ::-1], pens[:, size:0:-1], values[:, ::-1], -BIG,
                                                     ALU.add, ALU.max)
                m.then_inc(max_done.sem, 1)

            def forward_max(x, xb):
                dve.wait_ge(penH_done.sem, penH_done.at(x, 2))
                scan(x, 2, fwd, penH[xb], score[xb][:].rearrange("p h t -> p (h t)"), True)

            def backward_max(x, xb):
                scan(x, 3, segmax, penH[xb], fwd[:], False)

            def across_forward(x, xb):
                dve.wait_ge(seq_ps.sem, seq_ps.at(x, 1))
                scan(x, 4, across, penS[xb], seq[:, 0, :], True)

            def across_backward(x, xb):
                scan(x, 5, across2, penS[xb], across[:], False)

            def join_ends(x):
                sm = segmax[:].rearrange("p (h t) -> p h t", h=H)
                dve.wait_ge(back_ps.sem, back_ps.at(x, 1))
                for i, c in enumerate((0, T - 1)):
                    nc.vector.tensor_tensor(sm[:, :, c], sm[:, :, c], back[:, i * H:(i + 1) * H], ALU.max
                                            ).then_inc(max_done.sem, 1)

            mxh = mx[:].rearrange("p (h t) -> p h t", h=H)

            def differences(x, xb):
                dve.wait_ge(max_done.sem, max_done.at(x, 9))
                nc.vector.tensor_tensor(diff[:], score[xb][:, :, 0:T], mxh[:, :, 0:T], ALU.subtract
                                        ).then_inc(diff_done.sem, 1)
                dve.sem_inc(max_done.sem, 1)

            def tails(x, xb):
                dve.wait_ge(agg_done.sem, agg_done.at(x, 0))
                dve.wait_ge(last_done.sem, last_done.at(x, 1))
                nc.vector.tensor_tensor(wv[:, :, AW:AW + H].rearrange("p t h -> p h t"), mxh[:, :, 0:T],
                                        last[xb][:].unsqueeze(1).broadcast_to([P, H, T]), ALU.mult
                                        ).then_inc(tail_done.sem, 1)
                nc.vector.tensor_copy(wv[:, :, AW + H:RW], last[xb][:].unsqueeze(2)).then_inc(tail_done.sem, 1)

            def weigh(x, xb, j):
                if j == 0:
                    dve.wait_ge(exp_done.sem, exp_done.at(x, 1))
                o = wv[:, 2 * j:2 * j + 2, 0:AW].rearrange("p t (h d) -> p t h d", h=H)
                nc.vector.tensor_tensor(
                    o[:, :, :, 0:DH], kv[xb][:, 2 * j:2 * j + 2, D:2 * D].rearrange("p t (h d) -> p t h d", h=H),
                    o[:, :, :, DH:HW].broadcast_to([P, 2, H, DH]), ALU.mult).then_inc(wv_done.sem, 1)

            def merge_maxima(x):
                dve.wait_ge(agg_done.sem, agg_done.at(x, 0))
                fresh = keep["fresh"][:, bass.ds(x, 1)]
                nc.vector.tensor_scalar(absent[:], agg[:, AW + H:RW], -1.0, BIG, ALU.add, ALU.mult
                                        ).then_inc(merge.sem, 1)
                dve.wait_ge(merge.sem, merge.at(x, 1))
                nc.vector.tensor_scalar(part[:, 0], agg[:, AW:AW + H], absent[:], None, ALU.add
                                        ).then_inc(merge.sem, 1)
                dve.wait_ge(merge.sem, merge.at(x, 2))
                nc.vector.scalar_tensor_tensor(out=part[:, 1], in0=top[:], scalar=fresh, in1=part[:, 0],
                                               op0=ALU.add, op1=ALU.max).then_inc(merge.sem, 1)
                dve.wait_ge(merge.sem, merge.at(x, 3))
                nc.vector.scalar_tensor_tensor(out=shift[:, 0], in0=top[:], scalar=fresh, in1=part[:, 1],
                                               op0=ALU.add, op1=ALU.subtract).then_inc(merge.sem, 1)
                nc.vector.tensor_tensor(shift[:, 1], part[:, 0], part[:, 1], ALU.subtract).then_inc(merge.sem, 1)

            sums3 = sums[:].rearrange("p (h d) -> p h d", h=H)

            def merge_sums(x):
                dve.wait_ge(factor_done.sem, factor_done.at(x, 1))
                nc.vector.tensor_tensor(scaled[:].rearrange("p (h d) -> p h d", h=H),
                                        agg[:, 0:AW].rearrange("p (h d) -> p h d", h=H),
                                        factor[:, 1].unsqueeze(2).broadcast_to([P, H, HW]), ALU.mult
                                        ).then_inc(merge.sem, 1)
                nc.vector.tensor_copy(top[:], part[:, 1]).then_inc(merge.sem, 1)
                nc.vector.tensor_tensor(sums3, sums3, factor[:, 0].unsqueeze(2).broadcast_to([P, H, HW]), ALU.mult
                                        ).then_inc(merge.sem, 1)
                dve.wait_ge(merge.sem, merge.at(x, 8))
                nc.vector.tensor_tensor(sums[:], sums[:], scaled[:], ALU.add).then_inc(merge.sem, 1)

            def attention(x):
                dve.wait_ge(merge.sem, merge.at(x, 9))
                nc.vector.tensor_scalar(inv[:], sums3[:, :, DH], 1e-30, None, ALU.max).then_inc(inv_done.sem, 1)
                dve.wait_ge(inv_done.sem, inv_done.at(x, 1))
                nc.vector.reciprocal(inv[:], inv[:]).then_inc(inv_done.sem, 1)
                dve.wait_ge(inv_done.sem, inv_done.at(x, 2))
                dve.wait_ge(attT_ps.sem, attT_ps.at(x, 0))
                nc.vector.tensor_tensor(att[:].rearrange("p (h d) -> p h d", h=H), sums3[:, :, 0:DH],
                                        inv[:].unsqueeze(2).broadcast_to([P, H, DH]), ALU.mult
                                        ).then_inc(att_done.sem, 1)

            def residual(y, n):
                if n == 1:
                    dve.wait_ge(w2_ps.sem, w2_ps.at(y, 1))
                    dve.wait_ge(xr_done.sem, xr_done.at(y, 0))
                    nc.vector.tensor_tensor(res[:, 1], mm[1][:, 0], xr[:], ALU.add).then_inc(res_done.sem, 1)
                else:
                    dve.wait_ge(wo_ps.sem, wo_ps.at(y, 1))
                    dve.wait_ge(x_in, y * 32 + 32)
                    nc.vector.tensor_tensor(res[:, 0], mm[1][:, 1], x1b[:], ALU.add).then_inc(res_done.sem, 1)

            def statistics(y, n):
                dve.wait_ge(res_done.sem, res_done.at(y, 1 + n))
                nc.vector.bn_stats(bn[:, n], res[:, n]).then_inc(bn_done.sem, 1)

            def variance(y, n):
                held(dve, bn_done, bn_done.at(y, 1 + n), passed)
                nc.vector.bn_aggr(mv[:, n], bn[:, n]).then_inc(mv_done.sem, 1)

            def norms(y):
                dve.wait_ge(rstd_done.sem, rstd_done.at(y, 1))
                for n in range(2):
                    nc.vector.tensor_scalar(norm[:, n], res[:, n], mv[:, n, 0:1], rstd[:, n:n + 1],
                                            ALU.subtract, ALU.mult).then_inc(norm_done.sem, 1)

            def output(y):
                dve.wait_ge(wf_ps.sem, wf_ps.at(y, 0))
                dve.wait_ge(out_free.sem, out_free.at(y, 0))
                nc.vector.tensor_tensor(out[:], mm[1][:, 0], res[:, 1], ALU.add).then_inc(out_done.sem, 1)

            def layers(y, place):
                if place == (0, 2):
                    output(y)
                if place == (4, 1):
                    residual(y, 0)
                if place == (4, 2):
                    statistics(y, 0)
                if place == (5, 0):
                    variance(y, 0)
                if place == (6, 2):
                    residual(y, 1)
                if place == (7, 0):
                    statistics(y, 1)
                if place == (7, 1):
                    variance(y, 1)
                if place == (8, 0):
                    norms(y)

            def softmax_part(x, xb, place):
                if place == (0, 0):
                    scale_scores(x, xb)
                if place == (0, 1):
                    forward_max(x, xb)
                if place == (0, 2):
                    backward_max(x, xb)
                if place == (2, 0):
                    across_forward(x, xb)
                if place == (2, 1):
                    across_backward(x, xb)
                if place == (4, 0):
                    join_ends(x)
                if place == (4, 1):
                    scan(x, 8, fwd2, penH[xb], segmax[:], True)
                if place == (4, 2):
                    scan(x, 9, mx, penH[xb], fwd2[:], False)
                if place == (5, 0):
                    differences(x, xb)
                if place == (5, 1):
                    tails(x, xb)
                if place in WEIGH:
                    weigh(x, xb, WEIGH.index(place))

            def merge_part(x, place):
                if place == (0, 2):
                    merge_maxima(x)
                if place == (1, 0):
                    merge_sums(x)
                if place == (1, 2):
                    attention(x)

            WEIGH = [(6, 0), (6, 1), (6, 2), (7, 0), (7, 1), (7, 2), (8, 0), (8, 1), (8, 2)]

            def between(x, xb, place):
                softmax_part(x, xb, place)
                merge_part(x, place)
                layers(x, place)

            def body(s, b, k, x):
                for j in range(PAIRS + 2):
                    if j < PAIRS:
                        key(s, b, k, j)
                    if x is not None:
                        between(x, 1 - b, (j, 0))
                    if 0 <= j - 1 < PAIRS:
                        product(s, j - 1)
                    if x is not None:
                        between(x, 1 - b, (j, 1))
                    if j >= 2:
                        reduce(s, b, j - 2)
                    if x is not None:
                        between(x, 1 - b, (j, 2))
                    if j == POSITIONS:
                        positions(s + 1, 1 - b, k if b == 0 else k + 1)
                    if j == 7:
                        last_edges(s + 1, 1 - b)

            POSITIONS = 2
            positions(0, 0, 0)
            last_edges(0, 0)
            final = steps(dve, body)
            for y in range(LAG):
                if y == 2:
                    dve.sem_inc(att_done.sem, 1)
                for j in range(PAIRS + 2):
                    for i in range(3):
                        if y == 0:
                            softmax_part(final, 0, (j, i))
                        if y < 2:
                            merge_part(final + y, (j, i))
                        layers(final + y, (j, i))
            output(final + LAG)


def build(nc, t):
    with ExitStack() as ctx:
        sb, _, _ = declare(ctx, nc)
        keep = {
            "ident": sb("ident", [P, P]),
            "iota": sb("iota", [P, P]),
            "below": sb("below", [P, NW + 1]),
            "table": sb("table", [1, 2 * NS + 1], I32),
            "lag": sb("lag", [1, NS], I32),
            "wbase": sb("wbase", [P, NS]),
            "fresh": sb("fresh", [P, NS]),
            "lastmask": sb("lastmask", [P, T]),
        }
        node_stage(nc, t, keep)
        step_stage(nc, keep)
        edge_stage(nc, t, keep)


def kernel(x, src, dst, edge_attr_64, edge_weight, **w):
    import numpy as np
    import concourse.bacc as bacc
    from concourse.bass_utils import run_bass_kernel_spmd

    def rows(a, before, after, fill):
        a = np.asarray(a)
        wide = [(before, after)] + [(0, 0)] * (a.ndim - 1)
        return np.pad(a, wide, constant_values=fill)

    arrays = {
        "x": rows(x, 0, NPAD - N, 0),
        "src": rows(src, 0, CHUNK + 2, 0),
        "dst": rows(dst, 1, CHUNK + 2, FAR),
        "ef": rows(edge_attr_64, 0, CHUNK, 0),
        "ew": rows(edge_weight, 0, CHUNK, 0),
        "WfT": np.ascontiguousarray(np.asarray(w["L0_ffn_weight"]).T),
        "bf": np.asarray(w["L0_ffn_bias"]),
    }
    for name in ("Wq", "bq", "Wk", "bk", "Wv", "bv", "We", "be", "Wo", "bo", "ln1_g", "ln1_b", "ln2_g", "ln2_b",
                 "W1", "b1", "W2", "b2", "alpha", "beta"):
        arrays[name] = np.asarray(w[f"L0_gnn_{name}"])

    nc = bacc.Bacc("TRN2", target_bir_lowering=False, num_devices=1)
    t = {name: nc.dram_tensor(f"in_{name}", a.shape, mybir.dt.from_np(a.dtype), kind="ExternalInput").ap()
         for name, a in arrays.items()}
    t["xb"] = nc.dram_tensor("x_table", (NPAD, D), F32).ap()
    t["x1b"] = nc.dram_tensor("x1_table", (NPAD, D), F32).ap()
    t["kv"] = nc.dram_tensor("kv_table", (NPAD, 2 * D), F32).ap()
    t["q"] = nc.dram_tensor("q_table", (NPAD, 3 * D), BF16).ap()
    t["out"] = nc.dram_tensor("out", (NPAD, D), F32, kind="ExternalOutput").ap()
    build(nc, t)
    r = run_bass_kernel_spmd(nc, [{f"in_{name}": a for name, a in arrays.items()}], core_ids=[0])
    return r.results[0]["out"][:N]
```
